# Optimizing a Trainium2 kernel written in Bass

```python
import numpy as np
import jax
import jax.numpy as jnp

def _softmax(x, axis=-1):
    return jax.nn.softmax(x, axis=axis)

def _gelu(x):
    return jax.nn.gelu(x, approximate=True)

def _silu(x):
    return jax.nn.silu(x)

def _sigmoid(x):
    return jax.nn.sigmoid(x)

def _layernorm(x, axis=-1, eps=1e-05):
    m = jnp.mean(x, axis=axis, keepdims=True)
    v = jnp.var(x, axis=axis, keepdims=True)
    return (x - m) / jnp.sqrt(v + eps)

def _scatter_add(tgt, idx, src, axis=0):
    return tgt.at[idx].add(src)

def _segment_sum(src, seg, n):
    return jax.ops.segment_sum(src, seg, n)
kernel_name = 'mk_cond_seq_d4_seqx_r4_f49546'

def setup_inputs(seed: int=0):
    np.random.seed(seed)
    _w = jnp.asarray

    def _rec_inputs():
        import jax
        import jax.numpy as jnp
        _rk = jax.random.key(seed)
        x = -0.000125 + 0.9999 * jax.random.normal(jax.random.fold_in(_rk, 1), (32, 256, 256), jnp.float32)
        _lenS = 256 - jax.random.randint(jax.random.fold_in(_rk, 7), (32,), 0, max(1, 256 // 4) + 1, jnp.int32)
        _lenS2 = 256 - jax.random.randint(jax.random.fold_in(_rk, 8), (32,), 0, max(1, 256 // 4) + 1, jnp.int32)
        condB_t = jax.random.uniform(jax.random.fold_in(_rk, 11), (32,), jnp.float32, 0.0, 0.983423)
        itok_B_34_63 = jax.random.randint(jax.random.fold_in(_rk, 13), (32,), 34, 64, jnp.int32)
        fside_Bx16xSxS_0 = -1.47943e-05 + 1.00017 * jax.random.normal(jax.random.fold_in(_rk, 14), (32, 16, 256, 256), jnp.float32)
        itok_B_0_7 = jax.random.randint(jax.random.fold_in(_rk, 15), (32,), 0, 8, jnp.int32)
        condB_dt = jax.random.uniform(jax.random.fold_in(_rk, 16), (32,), jnp.float32, 0.0, 0.981965)
        _validS = jnp.arange(256)[None, :] < _lenS[:, None]
        _validS2 = jnp.arange(256)[None, :] < _lenS2[:, None]
        _causal = jnp.tril(jnp.ones((256, 256), dtype=bool))
        mask_Bx1xSxS_bk0 = jnp.logical_not(jnp.broadcast_to(_validS[:, None, None, :], (32, 1, 256, 256)))
        return (x, condB_t, itok_B_34_63, fside_Bx16xSxS_0, itok_B_0_7, condB_dt, mask_Bx1xSxS_bk0)
    x, condB_t, itok_B_34_63, fside_Bx16xSxS_0, itok_B_0_7, condB_dt, mask_Bx1xSxS_bk0 = _rec_inputs()

    def _L0_cond_setup():
        import jax, jax.numpy as jnp
        import numpy as np
        import math
        B, S, D, E = (32, 256, 256, 128)

        def _layer_norm(x, gamma, beta, eps=1e-05):
            mean = jnp.mean(x, axis=(-2, -1), keepdims=True)
            var = jnp.mean(jnp.square(x - mean), axis=(-2, -1), keepdims=True)
            return (x - mean) * jax.lax.rsqrt(var + eps) * gamma + beta

        def _noise_encoding(t, channels):
            half = channels // 2
            freqs = jnp.exp(jnp.arange(half, dtype=jnp.float32) * (-math.log(10000.0) / (half - 1)))
            emb = 5000.0 * t[:, None] * freqs[None, :]
            return jnp.concatenate([jnp.sin(emb), jnp.cos(emb)], axis=1)
        key = jax.random.key(seed)
        ks = jax.random.split(key, 20)

        def lin(k, fan_in, shape):
            return jax.random.normal(k, shape, jnp.float32) / np.sqrt(fan_in)
        inp = {'x': jax.random.normal(ks[0], (B, S, D), jnp.float32), 't': jax.random.uniform(ks[1], (B,), jnp.float32), 'W1': lin(ks[2], E, (E, 4 * E)), 'b1': jnp.zeros((4 * E,), jnp.float32), 'W2': lin(ks[3], 4 * E, (4 * E, 4 * E)), 'b2': jnp.zeros((4 * E,), jnp.float32), 'Wsc': lin(ks[4], 4 * E, (4 * E, D)), 'bsc': jnp.zeros((D,), jnp.float32), 'Wsh': lin(ks[5], 4 * E, (4 * E, D)), 'bsh': jnp.zeros((D,), jnp.float32), 'gamma': jnp.ones((S, D), jnp.float32), 'beta': jnp.zeros((S, D), jnp.float32), 'W_in': lin(ks[6], D, (D, D)), 'b_in': jnp.zeros((D,), jnp.float32), 'W_out': lin(ks[7], D, (D, D)), 'b_out': jnp.zeros((D,), jnp.float32)}
        return inp
    _L0_cond_all = _L0_cond_setup()
    _L0_cond_in = {k: v for k, v in _L0_cond_all.items() if k in ('W1', 'b1', 'W2', 'b2', 'Wsc', 'bsc', 'Wsh', 'bsh', 'gamma', 'beta', 'W_in', 'b_in', 'W_out', 'b_out')}
    del _L0_cond_all

    def _L1_cond_setup():
        import jax, jax.numpy as jnp
        import numpy as np
        import math
        D_MODEL = 256
        N_HEAD = 16
        HEAD_DIM = D_MODEL // N_HEAD
        D_FF = 1024
        NUM_STEPS = 100.0
        RESCALE = 4000.0
        EPS = 1e-05

        def _sin_emb(t):
            half = D_MODEL // 2
            x = t.astype(jnp.float32) / NUM_STEPS * RESCALE
            freqs = jnp.exp(jnp.arange(half, dtype=jnp.float32) * (-math.log(10000.0) / (half - 1)))
            e = x[:, None] * freqs[None, :]
            return jnp.concatenate([jnp.sin(e), jnp.cos(e)], axis=-1)

        def _ln(x):
            m = jnp.mean(x, axis=-1, keepdims=True)
            v = jnp.var(x, axis=-1, keepdims=True)
            return (x - m) / jnp.sqrt(v + EPS)

        def _gelu2(x):
            return x * jax.nn.sigmoid(1.702 * x)
        key = jax.random.key(seed)
        ks = jax.random.split(key, 24)
        B, S, D, F = (4, 128, D_MODEL, D_FF)
        std = 0.02
        inp = {'src': jax.random.normal(ks[0], (B, S, D), dtype=jnp.float32), 'src_mask': jax.random.randint(ks[1], (B, 1, S, S), 0, 2).astype(bool), 'timestep': jax.random.randint(ks[2], (B,), 0, 100, dtype=jnp.int32), 'attention_bias': jax.random.normal(ks[3], (B, N_HEAD, S, S), dtype=jnp.float32), 'W_ada': jax.random.normal(ks[4], (D, 2 * D), dtype=jnp.float32) * std, 'b_ada': jnp.zeros((2 * D,), dtype=jnp.float32), 'Wq': jax.random.normal(ks[5], (D, D), dtype=jnp.float32) * std, 'bq': jnp.zeros((D,), dtype=jnp.float32), 'Wk': jax.random.normal(ks[6], (D, D), dtype=jnp.float32) * std, 'bk': jnp.zeros((D,), dtype=jnp.float32), 'Wv': jax.random.normal(ks[7], (D, D), dtype=jnp.float32) * std, 'bv': jnp.zeros((D,), dtype=jnp.float32), 'Wo': jax.random.normal(ks[8], (D, D), dtype=jnp.float32) * std, 'bo': jnp.zeros((D,), dtype=jnp.float32), 'W1': jax.random.normal(ks[9], (D, F), dtype=jnp.float32) * std, 'b1': jnp.zeros((F,), dtype=jnp.float32), 'W2': jax.random.normal(ks[10], (F, D), dtype=jnp.float32) * std, 'b2': jnp.zeros((D,), dtype=jnp.float32), 'g2': jnp.ones((D,), dtype=jnp.float32), 'beta2': jnp.zeros((D,), dtype=jnp.float32)}
        return inp
    _L1_cond_all = _L1_cond_setup()
    _L1_cond_in = {k: v for k, v in _L1_cond_all.items() if k in ('W_ada', 'b_ada', 'Wq', 'bq', 'Wk', 'bk', 'Wv', 'bv', 'Wo', 'bo', 'W1', 'b1', 'W2', 'b2', 'g2', 'beta2')}
    del _L1_cond_all

    def _L2_cond_setup():
        import jax, jax.numpy as jnp
        import numpy as np
        E, H, I = (8, 256, 1024)
        B, S = (4, 256)
        LN_EPS = 1e-12
        key = jax.random.key(seed)
        ks = jax.random.split(key, 8)
        x = jax.random.normal(ks[0], (B, S, H), dtype=jnp.float32)
        expert_idx = jax.random.randint(ks[1], (B,), 0, E, dtype=jnp.int64)
        Wi = jax.random.normal(ks[2], (E, H, I), dtype=jnp.float32) * 0.02
        bi = jnp.zeros((E, I), dtype=jnp.float32)
        Wo = jax.random.normal(ks[3], (E, I, H), dtype=jnp.float32) * 0.02
        bo = jnp.zeros((E, H), dtype=jnp.float32)
        gamma = jnp.ones((E, H), dtype=jnp.float32)
        beta = jnp.zeros((E, H), dtype=jnp.float32)
        return {'input_tensor': x, 'expert_idx': expert_idx, 'Wi': Wi, 'bi': bi, 'Wo': Wo, 'bo': bo, 'gamma': gamma, 'beta': beta}
    _L2_cond_all = _L2_cond_setup()
    _L2_cond_in = {k: v for k, v in _L2_cond_all.items() if k in ('Wi', 'bi', 'Wo', 'bo', 'gamma', 'beta')}
    del _L2_cond_all

    def _L3_cond_setup():
        import jax, jax.numpy as jnp
        import numpy as np
        B, NX, NY = (16, 256, 256)

        def _grad(f, axis):
            fm = jnp.moveaxis(f, axis, -1)
            g = (jnp.roll(fm, -1, -1) - jnp.roll(fm, 1, -1)) * 0.5
            g0 = (-3.0 * fm[..., 0] + 4.0 * fm[..., 1] - fm[..., 2]) * 0.5
            gN = (3.0 * fm[..., -1] - 4.0 * fm[..., -2] + fm[..., -3]) * 0.5
            g = g.at[..., 0].set(g0).at[..., -1].set(gN)
            return jnp.moveaxis(g, -1, axis)

        def _grad2(f, axis):
            fm = jnp.moveaxis(f, axis, -1)
            g = jnp.roll(fm, -1, -1) - 2.0 * fm + jnp.roll(fm, 1, -1)
            g0 = 2.0 * fm[..., 0] - 5.0 * fm[..., 1] + 4.0 * fm[..., 2] - fm[..., 3]
            gN = 2.0 * fm[..., -1] - 5.0 * fm[..., -2] + 4.0 * fm[..., -3] - fm[..., -4]
            g = g.at[..., 0].set(g0).at[..., -1].set(gN)
            return jnp.moveaxis(g, -1, axis)
        key = jax.random.key(seed)
        k1, k2, k3, k4 = jax.random.split(key, 4)
        f = jax.random.uniform(k1, (B, NX, NY), dtype=jnp.float32)
        A_grid = jax.random.normal(k2, (2, NX, NY), dtype=jnp.float32)
        B_grid = jax.random.uniform(k3, (3, NX, NY), dtype=jnp.float32)
        dt = jax.random.uniform(k4, (B,), dtype=jnp.float32)
        return {'f': f, 'A_grid': A_grid, 'B_grid': B_grid, 'dt': dt}
    _L3_cond_all = _L3_cond_setup()
    _L3_cond_in = {k: v for k, v in _L3_cond_all.items() if k in ('A_grid', 'B_grid')}
    del _L3_cond_all
    return {'x': x, 'condB_t': condB_t, 'itok_B_34_63': itok_B_34_63, 'fside_Bx16xSxS_0': fside_Bx16xSxS_0, 'itok_B_0_7': itok_B_0_7, 'condB_dt': condB_dt, 'mask_Bx1xSxS_bk0': mask_Bx1xSxS_bk0, 'L0_cond_W1': _L0_cond_in['W1'], 'L0_cond_b1': _L0_cond_in['b1'], 'L0_cond_W2': _L0_cond_in['W2'], 'L0_cond_b2': _L0_cond_in['b2'], 'L0_cond_Wsc': _L0_cond_in['Wsc'], 'L0_cond_bsc': _L0_cond_in['bsc'], 'L0_cond_Wsh': _L0_cond_in['Wsh'], 'L0_cond_bsh': _L0_cond_in['bsh'], 'L0_cond_gamma': _L0_cond_in['gamma'], 'L0_cond_beta': _L0_cond_in['beta'], 'L0_cond_W_in': _L0_cond_in['W_in'], 'L0_cond_b_in': _L0_cond_in['b_in'], 'L0_cond_W_out': _L0_cond_in['W_out'], 'L0_cond_b_out': _L0_cond_in['b_out'], 'L1_cond_W_ada': _L1_cond_in['W_ada'], 'L1_cond_b_ada': _L1_cond_in['b_ada'], 'L1_cond_Wq': _L1_cond_in['Wq'], 'L1_cond_bq': _L1_cond_in['bq'], 'L1_cond_Wk': _L1_cond_in['Wk'], 'L1_cond_bk': _L1_cond_in['bk'], 'L1_cond_Wv': _L1_cond_in['Wv'], 'L1_cond_bv': _L1_cond_in['bv'], 'L1_cond_Wo': _L1_cond_in['Wo'], 'L1_cond_bo': _L1_cond_in['bo'], 'L1_cond_W1': _L1_cond_in['W1'], 'L1_cond_b1': _L1_cond_in['b1'], 'L1_cond_W2': _L1_cond_in['W2'], 'L1_cond_b2': _L1_cond_in['b2'], 'L1_cond_g2': _L1_cond_in['g2'], 'L1_cond_beta2': _L1_cond_in['beta2'], 'L2_cond_Wi': _L2_cond_in['Wi'], 'L2_cond_bi': _L2_cond_in['bi'], 'L2_cond_Wo': _L2_cond_in['Wo'], 'L2_cond_bo': _L2_cond_in['bo'], 'L2_cond_gamma': _L2_cond_in['gamma'], 'L2_cond_beta': _L2_cond_in['beta'], 'L3_cond_A_grid': _L3_cond_in['A_grid'], 'L3_cond_B_grid': _L3_cond_in['B_grid']}

def reference(x, condB_t, itok_B_34_63, fside_Bx16xSxS_0, itok_B_0_7, condB_dt, mask_Bx1xSxS_bk0, L0_cond_W1, L0_cond_b1, L0_cond_W2, L0_cond_b2, L0_cond_Wsc, L0_cond_bsc, L0_cond_Wsh, L0_cond_bsh, L0_cond_gamma, L0_cond_beta, L0_cond_W_in, L0_cond_b_in, L0_cond_W_out, L0_cond_b_out, L1_cond_W_ada, L1_cond_b_ada, L1_cond_Wq, L1_cond_bq, L1_cond_Wk, L1_cond_bk, L1_cond_Wv, L1_cond_bv, L1_cond_Wo, L1_cond_bo, L1_cond_W1, L1_cond_b1, L1_cond_W2, L1_cond_b2, L1_cond_g2, L1_cond_beta2, L2_cond_Wi, L2_cond_bi, L2_cond_Wo, L2_cond_bo, L2_cond_gamma, L2_cond_beta, L3_cond_A_grid, L3_cond_B_grid):
    import jax
    import jax.numpy as jnp

    def _L0_cond_ref(x, t, W1, b1, W2, b2, Wsc, bsc, Wsh, bsh, gamma, beta, W_in, b_in, W_out, b_out):
        import jax, jax.numpy as jnp
        import numpy as np
        import math
        B, S, D, E = (32, 256, 256, 128)

        def _layer_norm(x, gamma, beta, eps=1e-05):
            mean = jnp.mean(x, axis=(-2, -1), keepdims=True)
            var = jnp.mean(jnp.square(x - mean), axis=(-2, -1), keepdims=True)
            return (x - mean) * jax.lax.rsqrt(var + eps) * gamma + beta

        def _noise_encoding(t, channels):
            half = channels // 2
            freqs = jnp.exp(jnp.arange(half, dtype=jnp.float32) * (-math.log(10000.0) / (half - 1)))
            emb = 5000.0 * t[:, None] * freqs[None, :]
            return jnp.concatenate([jnp.sin(emb), jnp.cos(emb)], axis=1)
        h = _noise_encoding(t, E)
        h = jax.nn.silu(h @ W1 + b1)
        h = h @ W2 + b2
        scale = (h @ Wsc + bsc)[:, None, :]
        shift = (h @ Wsh + bsh)[:, None, :]
        out = jax.nn.silu(scale * _layer_norm(x, gamma, beta) + shift)
        out = out @ W_in + b_in
        out = jax.nn.silu(scale * _layer_norm(out, gamma, beta) + shift)
        out = out @ W_out + b_out
        return out + x

    def _L1_cond_ref(src, src_mask, timestep, attention_bias, W_ada, b_ada, Wq, bq, Wk, bk, Wv, bv, Wo, bo, W1, b1, W2, b2, g2, beta2):
        import jax, jax.numpy as jnp
        import numpy as np
        import math
        D_MODEL = 256
        N_HEAD = 16
        HEAD_DIM = D_MODEL // N_HEAD
        D_FF = 1024
        NUM_STEPS = 100.0
        RESCALE = 4000.0
        EPS = 1e-05

        def _sin_emb(t):
            half = D_MODEL // 2
            x = t.astype(jnp.float32) / NUM_STEPS * RESCALE
            freqs = jnp.exp(jnp.arange(half, dtype=jnp.float32) * (-math.log(10000.0) / (half - 1)))
            e = x[:, None] * freqs[None, :]
            return jnp.concatenate([jnp.sin(e), jnp.cos(e)], axis=-1)

        def _ln(x):
            m = jnp.mean(x, axis=-1, keepdims=True)
            v = jnp.var(x, axis=-1, keepdims=True)
            return (x - m) / jnp.sqrt(v + EPS)

        def _gelu2(x):
            return x * jax.nn.sigmoid(1.702 * x)
        B, S, D = src.shape
        emb = jax.nn.silu(_sin_emb(timestep)) @ W_ada + b_ada
        scale, shift = jnp.split(emb[:, None, :], 2, axis=-1)
        x = _ln(src) * (1.0 + scale) + shift
        q = (x @ Wq + bq).reshape(B, S, N_HEAD, HEAD_DIM).transpose(0, 2, 1, 3)
        k = (x @ Wk + bk).reshape(B, S, N_HEAD, HEAD_DIM).transpose(0, 2, 1, 3)
        v = (x @ Wv + bv).reshape(B, S, N_HEAD, HEAD_DIM).transpose(0, 2, 1, 3)
        scores = jnp.einsum('bhqd,bhkd->bhqk', q / math.sqrt(HEAD_DIM), k)
        scores = scores + attention_bias
        scores = jnp.where(src_mask, -jnp.inf, scores.astype(jnp.float32))
        probs = jax.nn.softmax(scores, axis=-1).astype(v.dtype)
        ctx = jnp.einsum('bhqk,bhkd->bhqd', probs, v)
        ctx = ctx.transpose(0, 2, 1, 3).reshape(B, S, D)
        x = x + (ctx @ Wo + bo)
        h = _ln(x) * g2 + beta2
        ff = _gelu2(h @ W1 + b1) @ W2 + b2
        return x + ff

    def _L2_cond_ref(input_tensor, expert_idx, Wi, bi, Wo, bo, gamma, beta):
        import jax, jax.numpy as jnp
        import numpy as np
        E, H, I = (8, 256, 1024)
        B, S = (4, 256)
        LN_EPS = 1e-12
        Wi_b = Wi[expert_idx]
        bi_b = bi[expert_idx]
        Wo_b = Wo[expert_idx]
        bo_b = bo[expert_idx]
        g_b = gamma[expert_idx]
        be_b = beta[expert_idx]
        h = jax.nn.gelu(jnp.einsum('bsh,bhi->bsi', input_tensor, Wi_b) + bi_b[:, None, :], approximate=False)
        o = jnp.einsum('bsi,bih->bsh', h, Wo_b) + bo_b[:, None, :]
        r = o + input_tensor
        mu = jnp.mean(r, axis=-1, keepdims=True)
        var = jnp.mean(jnp.square(r - mu), axis=-1, keepdims=True)
        y = (r - mu) * jax.lax.rsqrt(var + LN_EPS)
        return y * g_b[:, None, :] + be_b[:, None, :]

    def _L3_cond_ref(f, A_grid, B_grid, dt):
        import jax, jax.numpy as jnp
        import numpy as np
        B, NX, NY = (16, 256, 256)

        def _grad(f, axis):
            fm = jnp.moveaxis(f, axis, -1)
            g = (jnp.roll(fm, -1, -1) - jnp.roll(fm, 1, -1)) * 0.5
            g0 = (-3.0 * fm[..., 0] + 4.0 * fm[..., 1] - fm[..., 2]) * 0.5
            gN = (3.0 * fm[..., -1] - 4.0 * fm[..., -2] + fm[..., -3]) * 0.5
            g = g.at[..., 0].set(g0).at[..., -1].set(gN)
            return jnp.moveaxis(g, -1, axis)

        def _grad2(f, axis):
            fm = jnp.moveaxis(f, axis, -1)
            g = jnp.roll(fm, -1, -1) - 2.0 * fm + jnp.roll(fm, 1, -1)
            g0 = 2.0 * fm[..., 0] - 5.0 * fm[..., 1] + 4.0 * fm[..., 2] - fm[..., 3]
            gN = 2.0 * fm[..., -1] - 5.0 * fm[..., -2] + 4.0 * fm[..., -3] - fm[..., -4]
            g = g.at[..., 0].set(g0).at[..., -1].set(gN)
            return jnp.moveaxis(g, -1, axis)
        Af = A_grid[None] * f[:, None]
        Bf = B_grid[None] * f[:, None]
        gradv_Af = _grad(Af[:, 0], 1) + _grad(Af[:, 1], 2)
        gradvv_Bf = _grad2(Bf[:, 0], 1) + _grad2(Bf[:, 1], 2) + _grad(_grad(Bf[:, 2], 2), 1) + _grad(_grad(Bf[:, 2], 1), 2)
        df = -gradv_Af + gradvv_Bf * 0.5
        f_new = f + df * dt[:, None, None]
        return jnp.maximum(f_new, 0.0)
    x = _L0_cond_ref(x, condB_t, L0_cond_W1, L0_cond_b1, L0_cond_W2, L0_cond_b2, L0_cond_Wsc, L0_cond_bsc, L0_cond_Wsh, L0_cond_bsh, L0_cond_gamma, L0_cond_beta, L0_cond_W_in, L0_cond_b_in, L0_cond_W_out, L0_cond_b_out)
    x = _L1_cond_ref(x, mask_Bx1xSxS_bk0, itok_B_34_63, fside_Bx16xSxS_0, L1_cond_W_ada, L1_cond_b_ada, L1_cond_Wq, L1_cond_bq, L1_cond_Wk, L1_cond_bk, L1_cond_Wv, L1_cond_bv, L1_cond_Wo, L1_cond_bo, L1_cond_W1, L1_cond_b1, L1_cond_W2, L1_cond_b2, L1_cond_g2, L1_cond_beta2)
    x = _L2_cond_ref(x, itok_B_0_7, L2_cond_Wi, L2_cond_bi, L2_cond_Wo, L2_cond_bo, L2_cond_gamma, L2_cond_beta)
    x = _L3_cond_ref(x, L3_cond_A_grid, L3_cond_B_grid, condB_dt)
    return x

_drawn_inputs = setup_inputs


def setup_inputs(seed=0):
    import zlib

    import numpy as np

    out = dict(_drawn_inputs(seed))
    spreads = {'L0_cond_b1': (0.0, 0.1),
     'L0_cond_b2': (0.0, 0.1),
     'L0_cond_bsc': (0.0, 0.1),
     'L0_cond_bsh': (0.0, 0.1),
     'L0_cond_gamma': (1.0, 0.2),
     'L0_cond_beta': (0.0, 0.296),
     'L0_cond_b_in': (0.0, 0.1),
     'L0_cond_b_out': (0.0, 0.1),
     'L1_cond_b_ada': (0.0, 0.1),
     'L1_cond_bq': (0.0, 0.8),
     'L1_cond_bk': (0.0, 0.8),
     'L1_cond_bv': (0.0, 0.1),
     'L1_cond_bo': (0.0, 0.1),
     'L1_cond_b1': (0.0, 0.1),
     'L1_cond_b2': (0.0, 0.1),
     'L1_cond_g2': (1.0, 0.6),
     'L1_cond_beta2': (0.0, 0.652),
     'L2_cond_bi': (0.0, 0.1),
     'L2_cond_bo': (0.0, 0.1),
     'L2_cond_gamma': (1.0, 0.2),
     'L2_cond_beta': (0.0, 0.1)}
    factors = {'fside_Bx16xSxS_0': 7.157, 'L1_cond_Wq': 8.0, 'L1_cond_Wk': 8.0}
    for name, (base, spread) in spreads.items():
        noise = np.random.default_rng([zlib.crc32(name.encode()), seed]).standard_normal(out[name].shape)
        drawn = base * np.exp(spread * noise) if base else spread * noise
        out[name] = jnp.asarray(drawn.astype(out[name].dtype))
    for name, factor in factors.items():
        out[name] = (out[name] * factor).astype(out[name].dtype)
    return out
```

```python
import math
from contextlib import ExitStack

import concourse.bass as bass
import numpy as np
from concourse import mybir

BATCHES, SEQ, DIM, HEADS, FF, EXPERTS = 32, 256, 256, 16, 1024, 8
NOISE = 128
P = 128
HD = DIM // HEADS
CH = DIM // P
FC = FF // P
HEADS_PER_CHUNK = P // HD
HEADS_PER_GROUP = 4
GROUPS = HEADS // HEADS_PER_GROUP
RING = 3
TWO_PI = 2.0 * math.pi
ROUND = 12582912.0
COND = 4 * CH


def stencil_matrices():
    first = np.zeros((SEQ, SEQ), np.float32)
    second = np.zeros((SEQ, SEQ), np.float32)
    for i in range(1, SEQ - 1):
        first[i, i - 1], first[i, i + 1] = -0.5, 0.5
        second[i, i - 1], second[i, i], second[i, i + 1] = 1.0, -2.0, 1.0
    first[0, :3] = (-1.5, 2.0, -0.5)
    first[-1, -3:] = (0.5, -2.0, 1.5)
    second[0, :4] = (2.0, -5.0, 4.0, -1.0)
    second[-1, -4:] = (-1.0, 4.0, -5.0, 2.0)
    return first, second


def build_program(nc, d, out):
    f32, i32, u8 = mybir.dt.float32, mybir.dt.int32, mybir.dt.uint8
    ALU, ACT, AX = mybir.AluOpType, mybir.ActivationFunctionType, mybir.AxisListType
    PE_, DVE_ = nc.tensor, nc.vector

    ctx = ExitStack()
    with ctx:
        def sb(name, shape, dt=f32):
            return ctx.enter_context(nc.sbuf_tensor(name, [P] + shape, dt))

        def bank(name):
            return ctx.enter_context(nc.psum_tensor(name, [P, CH, DIM], f32))

        def sem(name):
            return ctx.enter_context(nc.semaphore(name))

        w_in, w_out = sb("w_in", [CH, DIM]), sb("w_out", [CH, DIM])
        w_q, w_k, w_v, w_o = (sb(n, [CH, DIM]) for n in ("w_q", "w_k", "w_v", "w_o"))
        w_ff1, w_ff2 = sb("w_ff1", [CH, FF]), sb("w_ff2", [FC, DIM])
        w_ex1, w_ex2 = sb("w_ex1", [CH, FF]), sb("w_ex2", [FC, DIM])
        gammaT, betaT = sb("gammaT", [CH, SEQ]), sb("betaT", [CH, SEQ])
        coef = sb("coef", [7, CH, DIM])
        edge_coef = sb("edge_coef", [2, CH, 2, 4])
        firstT, secondT = sb("firstT", [CH, SEQ]), sb("secondT", [CH, SEQ])
        ident, mean_w = sb("ident", [P]), sb("mean_w", [P])
        rows = sb("rows", [4, DIM])
        cols = sb("cols", [44])
        consts = sb("consts", [16])
        q_cols = sb("q_cols", [2, 1 + CH])
        ex_rows, ex_cols = sb("ex_rows", [3, DIM]), sb("ex_cols", [FC])
        cond_all, cond = sb("cond_all", [BATCHES, COND]), sb("cond", [COND])
        dt_all, dt = sb("dt_all", [BATCHES]), sb("dt", [1])
        expert = ctx.enter_context(nc.sbuf_tensor("expert", [1, BATCHES], i32))
        B_OUT, B_V, B_O, B_FF2 = range(4)
        C_BIN, C_BK, C_G2, C_BETA2, C_BQ, C_FF1 = 0, 2, 4, 6, 8, 10
        C_B1, C_B2, C_BSC, C_BSH, C_ADA = 18, 22, 26, 28, 30
        C_FREQ0, C_FREQ1, C_EVEN, C_ODD, C_PHASE = 34, 35, 36, 37, 38
        NEG_HALF = 0

        xT, x, mask_u8 = sb("xT", [CH, SEQ]), sb("x", [CH, DIM]), sb("mask_u8", [CH, SEQ], u8)
        bias = sb("bias", [GROUPS, HEADS_PER_GROUP, CH, SEQ])
        stat6, stat2, stat4 = sb("stat6", [CH, 6]), sb("stat2", [CH, 2]), sb("stat4", [4])
        varA, rstdA = sb("varA", [CH]), sb("rstdA", [CH])
        half_w, gate = sb("half_w", [CH, SEQ]), sb("gate", [CH, SEQ])
        h1 = sb("h1", [CH, SEQ])
        x_bias, mask_far = sb("x_bias", [CH, DIM]), sb("mask_far", [CH, SEQ])
        x0 = sb("x0", [CH, DIM])
        x1T = sb("x1T", [CH, SEQ])
        q_even, q_odd, kT = sb("q_even", [CH, SEQ]), sb("q_odd", [CH, SEQ]), sb("kT", [CH, SEQ])
        v = sb("v", [CH, DIM])
        probs, probsT = sb("probs", [RING, CH, SEQ]), sb("probsT", [RING, CH, SEQ])
        neg_max, denom = sb("neg_max", [CH, HEADS]), sb("denom", [CH, HEADS])
        inv = sb("inv", [CH, HEADS])
        attn = sb("attn", [CH, DIM])
        attnT = sb("attnT", [CH, SEQ])
        statB6, statB2 = sb("statB6", [CH, 6]), sb("statB2", [CH, 2])
        varB, rstdB = sb("varB", [CH]), sb("rstdB", [CH])
        x2, x2_bias, xn2, hT = sb("x2", [CH, DIM]), sb("x2_bias", [CH, DIM]), sb("xn2", [CH, DIM]), sb("hT", [CH, SEQ])
        hidden = sb("hidden", [FC, SEQ])
        x3, x3_bias, x3T = sb("x3", [CH, DIM]), sb("x3_bias", [CH, DIM]), sb("x3T", [CH, SEQ])
        y, f = sb("y", [CH, DIM]), sb("f", [CH, DIM])
        prod = sb("prod", [7, CH, DIM])
        diff = sb("diff", [2, CH, DIM])
        edge = sb("edge", [2, CH, 2, 4])
        f_r, res = sb("f_r", [CH, DIM]), sb("res", [CH, DIM])

        S = [bank("S0"), bank("S1")]
        T = [bank("T0"), bank("T1")]
        C = bank("C")
        G = [bank("G0"), bank("G1"), bank("G2")]

        stage = bias[:, :, :, :].rearrange("p a b c n -> p (a b c n)")
        at = [0]

        def scratch(n):
            at[0] += n
            return stage[:, at[0] - n:at[0]]

        s_w1 = scratch(512)
        s_w2 = scratch(2048).rearrange("p (c n) -> p c n", c=4)
        s_wsc = scratch(1024).rearrange("p (c n) -> p c n", c=4)
        s_wsh = scratch(1024).rearrange("p (c n) -> p c n", c=4)
        s_ada = scratch(1024).rearrange("p (c n) -> p c n", c=2)
        grids = scratch(5 * CH * DIM).rearrange("p (a c n) -> p a c n", a=5, c=CH)
        ang = half_w[:, :, :].rearrange("p c (a n) -> p (c a) n", n=BATCHES)
        emb = gate[:, :, :].rearrange("p c (a n) -> p (c a) n", n=BATCHES)
        hid = h1[:, :, :].rearrange("p c (a n) -> p (c a) n", n=BATCHES)
        t_f = x0[:, 0, 0:3 * BATCHES].rearrange("p (a n) -> p a n", n=BATCHES)
        t_i = ctx.enter_context(nc.sbuf_tensor("t_i", [P, BATCHES], i32))

        weights_loaded, cond_loaded, expert_loaded = sem("weights_loaded"), sem("cond_loaded"), sem("expert_loaded")
        ident_zeroed, tables_made, edges_cleared = sem("ident_zeroed"), sem("tables_made"), sem("edges_cleared")
        angles_ready, sines_ready, emb_ready = sem("angles_ready"), sem("sines_ready"), sem("emb_ready")
        mlp_mm, mlp_act = sem("mlp_mm"), sem("mlp_act")
        silu_half, silu_tanh = sem("silu_half"), sem("silu_tanh")
        ex1_free, ex2_free, ex_small_free = sem("ex1_free"), sem("ex2_free"), sem("ex_small_free")

        weight_loads = [
            (w_in, "L0_cond_W_in"), (w_out, "L0_cond_W_out"), (w_q, "L1_cond_Wq"), (w_k, "L1_cond_Wk"),
            (w_v, "L1_cond_Wv"), (w_o, "L1_cond_Wo"), (w_ff1, "L1_cond_W1"), (w_ff2, "L1_cond_W2"),
            (gammaT, "gammaT"), (betaT, "betaT"), (firstT, "firstT"), (secondT, "secondT"),
        ]
        stage_loads = [(s_w2, "L0_cond_W2"), (s_wsc, "L0_cond_Wsc"), (s_wsh, "L0_cond_Wsh"), (s_ada, "L1_cond_W_ada")]

        with nc.Block() as block:
            @block.sync
            def _(sp):
                sp.dma_start(cols[:, :], d["cols"]).then_inc(cond_loaded, 16)
                sp.dma_start(t_f[:, 0, :], d["condB_t"].rearrange("(a n) -> a n", a=1).to_broadcast([P, BATCHES])).then_inc(cond_loaded, 16)
                sp.dma_start(t_i[:, :], d["itok_B_34_63"].rearrange("(a n) -> a n", a=1).to_broadcast([P, BATCHES])).then_inc(cond_loaded, 16)
                sp.dma_start(dt_all[:, :], d["condB_dt"].rearrange("(a n) -> a n", a=1).to_broadcast([P, BATCHES])).then_inc(cond_loaded, 16)
                sp.dma_start(s_w1, d["L0_cond_W1"]).then_inc(cond_loaded, 16)
                for dst, name in stage_loads:
                    sp.dma_start(dst, d[name].rearrange("(c p) n -> p c n", p=P)).then_inc(cond_loaded, 16)
                for a in range(2):
                    sp.dma_start(grids[:, a, :, :], d["L3_cond_A_grid"][a, :, :].rearrange("(c p) n -> p c n", p=P)).then_inc(cond_loaded, 16)
                for a in range(3):
                    sp.dma_start(grids[:, 2 + a, :, :], d["L3_cond_B_grid"][a, :, :].rearrange("(c p) n -> p c n", p=P)).then_inc(cond_loaded, 16)
                for dst, name in weight_loads:
                    sp.dma_start(dst[:, :, :], d[name].rearrange("(c p) n -> p c n", p=P)).then_inc(weights_loaded, 16)
                for a, name in enumerate(("L0_cond_b_out", "L1_cond_bv", "L1_cond_bo", "L1_cond_b2")):
                    sp.dma_start(rows[:, a, :], d[name].rearrange("(a n) -> a n", a=1).to_broadcast([P, DIM])).then_inc(weights_loaded, 16)
                sp.dma_start(expert[:, :], d["itok_B_0_7"].rearrange("(a n) -> a n", a=1)).then_inc(expert_loaded, 16)
                sp.wait_ge(expert_loaded, 16)
                sp.wait_ge(weights_loaded, 16 * (len(weight_loads) + 4))

            @block.gpsimd
            def _(pool):
                pool.memset(ident[:, :], 0.0).then_inc(ident_zeroed, 1)
                pool.memset(mean_w[:, :], 1.0 / P).then_inc(tables_made, 1)
                pool.memset(consts[:, 0:4], -0.5).then_inc(ex1_free, 1)
                pool.memset(consts[:, 4:8], -0.5).then_inc(ex2_free, 1)
                pool.memset(consts[:, 8:16], -0.5).then_inc(ex_small_free, 1)
                pool.memset(edge_coef[:, :, :, :, :], 0.0).then_inc(edges_cleared, 1)
                pool.wait_ge(ident_zeroed, 1)
                pool.affine_select(out=ident[:, :], in_=ident[:, :], compare_op=ALU.not_equal, fill=1.0,
                                   base=0, pattern=[[-1, P]], channel_multiplier=1).then_inc(tables_made, 1)

            @block.vector
            def _(dve):
                dve.wait_ge(cond_loaded, 16 * 14)
                dve.tensor_copy(t_f[:, 1, :], t_i[:, :])
                dve.tensor_scalar(ang[:, 0, :], t_f[:, 0, :], 5000.0, cols[:, C_FREQ0:C_FREQ0 + 1], ALU.mult, ALU.mult)
                dve.drain()
                dve.tensor_scalar(t_f[:, 2, :], t_f[:, 1, :], 0.01, 4000.0, ALU.mult, ALU.mult)
                dve.drain()
                for a in (1, 2):
                    dve.tensor_scalar(ang[:, a, :], t_f[:, 2, :], cols[:, C_FREQ1:C_FREQ1 + 1], None, ALU.mult)
                dve.drain()
                for a in range(3):
                    dve.tensor_scalar(ang[:, 3 + a, :], ang[:, a, :], 1.0 / TWO_PI, cols[:, C_PHASE + a:C_PHASE + a + 1], ALU.mult, ALU.add)
                dve.drain()
                dve.tensor_scalar(ang[:, 6:9, :], ang[:, 3:6, :], ROUND, None, ALU.add)
                dve.drain()
                dve.tensor_scalar(ang[:, 3:6, :], ang[:, 6:9, :], -ROUND, None, ALU.add)
                hi = 6.28125
                mid = float(np.float32(np.round((TWO_PI - hi) * 2 ** 21) / 2 ** 21))
                lo = TWO_PI - hi - mid
                for part in (hi, mid, lo):
                    dve.drain()
                    dve.scalar_tensor_tensor(out=ang[:, 0:3, :], in0=ang[:, 3:6, :], scalar=-part, in1=ang[:, 0:3, :], op0=ALU.mult, op1=ALU.add)
                dve.drain()
                for a in range(3):
                    dve.tensor_scalar(ang[:, 9 + a, :], ang[:, a, :], cols[:, C_PHASE + 3 + a:C_PHASE + 4 + a], None, ALU.add)
                dve.drain()
                dve.tensor_scalar(ang[:, 12:15, :], ang[:, 9:12, :], 3.1415925, -3.1415925, ALU.min, ALU.max).then_inc(angles_ready, 1)
                dve.wait_ge(sines_ready, 1)
                dve.tensor_scalar(emb[:, 3:5, :], emb[:, 1:3, :], 0.5, None, ALU.mult).then_inc(silu_half, 1)
                dve.wait_ge(silu_tanh, 1)
                dve.scalar_tensor_tensor(out=emb[:, 1:3, :], in0=emb[:, 5:7, :], scalar=1.0, in1=emb[:, 3:5, :], op0=ALU.add, op1=ALU.mult).then_inc(emb_ready, 1)
                dve.wait_ge(mlp_mm, 1)
                for c in range(4):
                    dve.tensor_scalar(hid[:, c, :], G[0][:, 0, c * BATCHES:(c + 1) * BATCHES], cols[:, C_B1 + c:C_B1 + c + 1], 0.5, ALU.add, ALU.mult)
                dve.drain().then_inc(silu_half, 1)
                dve.wait_ge(silu_tanh, 2)
                dve.scalar_tensor_tensor(out=hid[:, 8:12, :], in0=hid[:, 4:8, :], scalar=1.0, in1=hid[:, 0:4, :], op0=ALU.add, op1=ALU.mult).then_inc(mlp_act, 1)
                dve.wait_ge(mlp_mm, 2)
                for c in range(4):
                    dve.tensor_scalar(hid[:, 12 + c, :], G[1][:, 0, c * BATCHES:(c + 1) * BATCHES], cols[:, C_B2 + c:C_B2 + c + 1], None, ALU.add)
                dve.drain().then_inc(mlp_act, 1)
                dve.wait_ge(mlp_mm, 3)
                for c in range(4):
                    dve.tensor_scalar(cond_all[:, :, c], G[2][:, 0, c * BATCHES:(c + 1) * BATCHES], cols[:, C_BSC + c:C_BSC + c + 1], 0.5, ALU.add, ALU.mult)
                for c in range(4):
                    dve.tensor_scalar(cond_all[:, :, 4 + c], G[2][:, 1, c * BATCHES:(c + 1) * BATCHES], cols[:, C_ADA + c:C_ADA + c + 1],
                                      1.0 if c < 2 else 0.0, ALU.add, ALU.add)
                for a, col in enumerate((C_EVEN, C_ODD)):
                    dve.tensor_copy(q_cols[:, a, 0:1], cols[:, col:col + 1])
                    dve.tensor_scalar(q_cols[:, a, 1:1 + CH], cols[:, C_BQ:C_BQ + CH], cols[:, col:col + 1], None, ALU.mult)
                A0, A1, B0, B1, B2 = (grids[:, a, :, :] for a in range(5))
                dve.tensor_scalar(coef[:, 0, :, :], B2, 0.5, None, ALU.mult)
                dve.tensor_scalar(coef[:, 2, :, :], B2, -0.5, None, ALU.mult)
                dve.tensor_copy(coef[:, 4, :, :], A0)
                dve.tensor_copy(coef[:, 5, :, :], B1)
                dve.tensor_scalar(coef[:, 6, :, :], B0, 0.5, None, ALU.mult)
                dve.tensor_scalar(prod[:, 0, :, :], A1, 0.5, None, ALU.mult)
                dve.tensor_scalar(prod[:, 1, :, :], B1, 0.5, None, ALU.mult)
                dve.drain()
                dve.tensor_tensor(out=coef[:, 1, :, :], in0=prod[:, 1, :, :], in1=prod[:, 0, :, :], op=ALU.subtract)
                dve.tensor_tensor(out=coef[:, 3, :, :], in0=prod[:, 1, :, :], in1=prod[:, 0, :, :], op=ALU.add)
                N = DIM
                ec = edge_coef
                dve.wait_ge(edges_cleared, 1)
                for side, j, k in ((0, 0, -1.5), (0, 1, 2.0), (0, 2, -0.5), (1, 1, 0.5), (1, 2, -2.0), (1, 3, 1.5)):
                    col = j + (N - 4) * side
                    dve.tensor_scalar(ec[:, 0, :, side, j], B2[:, :, col], k, None, ALU.mult)
                for side, j, kb, ka in ((0, 0, 2.0, 1.5), (0, 1, -2.5, -2.0), (0, 2, 2.0, 0.5), (0, 3, -0.5, 0.0),
                                        (1, 0, -0.5, 0.0), (1, 1, 2.0, -0.5), (1, 2, -2.5, 2.0), (1, 3, 2.0, -1.5)):
                    col = j + (N - 4) * side
                    dve.tensor_scalar(edge[:, 0, :, side, j], A1[:, :, col], ka, None, ALU.mult)
                    dve.tensor_scalar(edge[:, 1, :, side, j], B1[:, :, col], kb, None, ALU.mult)
                dve.drain()
                dve.tensor_tensor(out=ec[:, 1, :, :, :], in0=edge[:, 0, :, :, :], in1=edge[:, 1, :, :, :], op=ALU.add)

            @block.scalar
            def _(act):
                act.wait_ge(angles_ready, 1)
                act.activation(emb[:, 0:3, :], ang[:, 12:15, :], ACT.Sin).then_inc(sines_ready, 1)
                act.wait_ge(silu_half, 1)
                act.activation(emb[:, 5:7, :], emb[:, 3:5, :], ACT.Tanh).then_inc(silu_tanh, 1)
                act.wait_ge(silu_half, 2)
                act.activation(hid[:, 4:8, :], hid[:, 0:4, :], ACT.Tanh).then_inc(silu_tanh, 1)

            @block.tensor
            def _(pe):
                pe.wait_ge(cond_loaded, 16 * 14)
                pe.wait_ge(emb_ready, 1)
                for c in range(4):
                    last = pe.matmul(G[0][:, 0, c * BATCHES:(c + 1) * BATCHES], s_w1[:, c * P:(c + 1) * P], emb[:, 0, :], start=True, stop=True)
                last.then_inc(mlp_mm, 1)
                for c in range(4):
                    for k in range(2):
                        pe.matmul(G[2][:, 1, c * BATCHES:(c + 1) * BATCHES], s_ada[:, k, c * P:(c + 1) * P], emb[:, 1 + k, :], start=k == 0, stop=k == 1)
                pe.wait_ge(mlp_act, 1)
                for c in range(4):
                    for k in range(4):
                        last = pe.matmul(G[1][:, 0, c * BATCHES:(c + 1) * BATCHES], s_w2[:, k, c * P:(c + 1) * P], hid[:, 8 + k, :], start=k == 0, stop=k == 3)
                last.then_inc(mlp_mm, 1)
                pe.wait_ge(mlp_act, 2)
                for w, base in ((s_wsc, 0), (s_wsh, 2)):
                    for c in range(2):
                        for k in range(4):
                            last = pe.matmul(G[2][:, 0, (base + c) * BATCHES:(base + c + 1) * BATCHES], w[:, k, c * P:(c + 1) * P], hid[:, 12 + k, :], start=k == 0, stop=k == 3)
                last.then_inc(mlp_mm, 1)

        names = {}

        def S_(name):
            if name not in names:
                names[name] = sem(name)
            return names[name]

        xT_loaded, x_loaded, mask_loaded = S_("xT_loaded"), S_("x_loaded"), S_("mask_loaded")
        bias_loaded = [S_(f"bias_loaded{g}") for g in range(GROUPS)]
        ex1_loaded, ex2_loaded, ex_rows_loaded, ex_cols_loaded = (S_(n) for n in ("ex1_loaded", "ex2_loaded", "ex_rows_loaded", "ex_cols_loaded"))
        xT_free, x_free, mask_free = S_("xT_free"), S_("x_free"), S_("mask_free")
        bias_free = [S_(f"bias_free{g}") for g in range(GROUPS)]
        stored = S_("stored")
        (momentsA1_ready, momentsA2_ready, act1_ready, act2_ready, xn_ready, xn2_ready, x3_ready, q_ready, v_ready,
         probsT_ready, attn_ready, edges_to_pe) = (S_(n) for n in (
             "momentsA1_ready", "momentsA2_ready", "act1_ready", "act2_ready", "xn_ready", "xn2_ready", "x3_ready", "q_ready", "v_ready",
             "probsT_ready", "attn_ready", "edges_to_pe"))
        attnT_ready, hT_ready, ff1_ready, x1T_ready, x3T_ready, k_ready, ex_hidden_ready, probs_ready = (S_(n) for n in (
            "attnT_ready", "hT_ready", "ff1_ready", "x1T_ready", "x3T_ready", "k_ready", "ex_hidden_ready", "probs_ready"))
        (stats1_done, stats2_done, proj_done, mm2_done, ff2_done, q_done, v_done, scores_done, probsT_done, attn_done,
         ex2_done, stencil_done) = (S_(n) for n in (
             "stats1_done", "stats2_done", "proj_done", "mm2_done", "ff2_done", "q_done", "v_done", "scores_done", "probsT_done",
             "attn_done", "ex2_done", "stencil_done"))
        attnT_done, mm1_done, hT_done, ff1_done, x1T_done, x3T_done, k_done, ex1_done = (S_(n) for n in (
            "attnT_done", "mm1_done", "hT_done", "ff1_done", "x1T_done", "x3T_done", "k_done", "ex1_done"))
        half_ready, tanh_ready, h1_ready, logits_ready, res_ready = (S_(n) for n in (
            "half_ready", "tanh_ready", "h1_ready", "logits_ready", "res_ready"))
        varA_ready, rstdA_ready, varB_ready, rstdB_ready, x_bias_ready, x2_bias_ready = (S_(n) for n in (
            "varA_ready", "rstdA_ready", "varB_ready", "rstdB_ready", "x_bias_ready", "x2_bias_ready"))
        bias_masked, x3_for_bias, x3_bias_ready, y_ready, f_ready, edges_ready, terms_ready = (S_(n) for n in (
            "bias_masked", "x3_for_bias", "x3_bias_ready", "y_ready", "f_ready", "edges_ready", "terms_ready"))
        inner_ready = S_("inner_ready")

        def settle(eng, counts):
            eng.drain()
            for s, n in counts:
                eng.sem_inc(s, -n)

        def load_A(sp, b, first):
            if not first:
                sp.wait_ge(xT_free, 1)
            sp.dma_start(xT[:, :, :], d["xT"][bass.ds(b, 1), :, :].rearrange("a (c p) n -> p (a c) n", p=P)).then_inc(xT_loaded, 16)
            if not first:
                sp.wait_ge(x_free, 1)
            sp.dma_start(x[:, :, :], d["x"][bass.ds(b, 1), :, :].rearrange("a (c p) n -> p (a c) n", p=P)).then_inc(x_loaded, 16)
            if not first:
                sp.wait_ge(mask_free, 1)
            sp.dma_start(mask_u8[:, :, :], d["mask"][bass.ds(b, 1), :, :].rearrange("a (c p) n -> p (a c) n", p=P)).then_inc(mask_loaded, 16)

        def load_bias(sp, b, g, first):
            if not first:
                sp.wait_ge(bias_free[g], 1)
            src = d["fside"][bass.ds(b, 1), g, :, :].rearrange("a p (h c n) -> p (a h) c n", h=HEADS_PER_GROUP, c=CH)
            sp.dma_start(bias[:, g, :, :, :], src).then_inc(bias_loaded[g], 16)

        def load_expert(sp, b, part):
            sp.wait_ge(expert_loaded, 16)
            e = sp.value_load(expert[0:1, bass.ds(b, 1)], min_val=0, max_val=EXPERTS - 1)
            one = bass.ds(e, 1)
            if part == 0:
                sp.wait_ge(ex1_free, 1)
                sp.dma_start(w_ex1[:, :, :], d["L2_cond_Wi"][one, :, :].rearrange("a (c p) n -> p (a c) n", p=P)).then_inc(ex1_loaded, 16)
            elif part == 1:
                sp.wait_ge(ex2_free, 1)
                sp.dma_start(w_ex2[:, :, :], d["L2_cond_Wo"][one, :, :].rearrange("a (c p) n -> p (a c) n", p=P)).then_inc(ex2_loaded, 16)
            else:
                sp.wait_ge(ex_small_free, 1)
                sp.dma_start(ex_cols[:, :], d["ex_bi"][one, :, :].rearrange("a p n -> p (a n)")).then_inc(ex_cols_loaded, 16)
                sp.dma_start(ex_rows[:, :, :].rearrange("p a n -> p (a n)"),
                             d["ex_rows"][one, :].to_broadcast([P, 3 * DIM])).then_inc(ex_rows_loaded, 16)

        def sync_body(sp, a, b):
            first = isinstance(a, int) and a == 0
            if a is not None:
                load_A(sp, a, first)
            if b is not None:
                load_expert(sp, b, 0)
            if a is not None:
                load_bias(sp, a, 0, first)
                load_bias(sp, a, 1, first)
            if b is not None:
                load_expert(sp, b, 2)
            if a is not None:
                load_bias(sp, a, 2, first)
            if b is not None:
                load_expert(sp, b, 1)
            if a is not None:
                load_bias(sp, a, 3, first)
            counts = []
            if a is not None and not first:
                counts += [(s, 1) for s in [xT_free, x_free, mask_free] + bias_free]
            if b is not None:
                counts += [(ex1_free, 1), (ex2_free, 1), (ex_small_free, 1)]
            if counts:
                settle(sp, counts)

        def transposes(pe, dst, src):
            for c in range(CH):
                for r in range(CH):
                    last = pe.transpose(dst[:, c, r * P:(r + 1) * P], src[:, r, c * P:(c + 1) * P], ident[:, :])
            return last

        def feature_major(pe, dst, w, srcT):
            for c in range(CH):
                for k in range(CH):
                    last = pe.matmul(dst[:, c, :], w[:, k, c * P:(c + 1) * P], srcT[:, k, :], start=k == 0, stop=k == CH - 1)
            return last

        def row_major(pe, dst, srcT, w, r, chunks):
            for k in range(chunks):
                last = pe.matmul(dst[:, r, :], srcT[:, k, r * P:(r + 1) * P], w[:, k, :], start=k == 0, stop=k == chunks - 1)
            return last

        def tensor_body(pe, A, B):
            def hidden_group(j, w, srcT, done):
                dst = G[j % 3]
                for u in range(CH):
                    c = CH * j + u
                    for k in range(CH):
                        last = pe.matmul(dst[:, u, :], w[:, k, c * P:(c + 1) * P], srcT[:, k, :], start=k == 0, stop=k == CH - 1)
                last.then_inc(done, 1)

            if B:
                pe.wait_ge(attn_ready, 1)
                transposes(pe, G[0], attn).then_inc(attnT_done, 1)
            if A:
                pe.wait_ge(momentsA1_ready, 1)
                pe.matmul(C[:, 0, 0:2], mean_w[:, :], stat4[:, 0:2], start=True, stop=True).then_inc(stats1_done, 1)
            if B:
                pe.wait_ge(attnT_ready, 1)
                for r in range(CH):
                    pe.matmul(G[1][:, r, :], attnT[:, 0, r * P:(r + 1) * P], w_o[:, 0, :], start=True, stop=False)
                    for c in range(CH):
                        pe.matmul(G[1][:, r, c * P:(c + 1) * P], x1T[:, c, r * P:(r + 1) * P], ident[:, :], start=False, stop=False)
                    last = pe.matmul(G[1][:, r, :], attnT[:, 1, r * P:(r + 1) * P], w_o[:, 1, :], start=False, stop=True)
                last.then_inc(proj_done, 1)
                pe.wait_ge(xn2_ready, 1)
                transposes(pe, G[2], xn2).then_inc(hT_done, 1)
            if A:
                pe.wait_ge(act1_ready, 1)
                feature_major(pe, S[0], w_in, gate).then_inc(mm1_done, 1)
            if B:
                pe.wait_ge(hT_ready, 1)
                hidden_group(0, w_ff1, hT, ff1_done)
                hidden_group(1, w_ff1, hT, ff1_done)
            if A:
                pe.wait_ge(momentsA2_ready, 1)
                pe.matmul(C[:, 0, 0:2], mean_w[:, :], stat4[:, 2:4], start=True, stop=True).then_inc(stats2_done, 1)
            if B:
                hidden_group(2, w_ff1, hT, ff1_done)
                pe.wait_ge(ff1_ready, 1)
                hidden_group(3, w_ff1, hT, ff1_done)
                pe.wait_ge(ff1_ready, 4)
                row_major(pe, G[1], hidden, w_ff2, 0, FC)
            if A:
                pe.wait_ge(act2_ready, 1)
                for r in range(CH):
                    last = row_major(pe, S[1], gate, w_out, r, CH)
                last.then_inc(mm2_done, 1)
            if B:
                row_major(pe, G[1], hidden, w_ff2, 1, FC).then_inc(ff2_done, 1)
            if A:
                pe.wait_ge(xn_ready, 1)
                transposes(pe, T[0], x0).then_inc(x1T_done, 1)
            if B:
                pe.wait_ge(x3_ready, 1)
                transposes(pe, G[2], x3).then_inc(x3T_done, 1)
            if A:
                pe.wait_ge(x1T_ready, 1)
                feature_major(pe, S[0], w_q, x1T).then_inc(q_done, 1)
                feature_major(pe, S[1], w_k, x1T).then_inc(k_done, 1)
                for r in range(CH):
                    last = row_major(pe, T[1], x1T, w_v, r, CH)
                last.then_inc(v_done, 1)

            def scores(h):
                c, part = h // HEADS_PER_CHUNK, 32 * ((h % HEADS_PER_CHUNK) // 2)
                q = (q_even, q_odd)[h % 2]
                for r in range(CH):
                    last = pe.matmul(S[h % 2][:, r, :], q[part:part + 32, c, r * P:(r + 1) * P], kT[part:part + 32, c, :],
                                     start=True, stop=True)
                last.then_inc(scores_done, 1)

            def values(h):
                pe.wait_ge(probsT_ready, h + 1)
                for r in range(CH):
                    for k in range(CH):
                        last = pe.matmul(C[:, r, h * HD:(h + 1) * HD], probsT[:, h % RING, k, r * P:(r + 1) * P],
                                         v[:, k, h * HD:(h + 1) * HD], start=k == 0, stop=k == CH - 1)
                return last

            if A:
                pe.wait_ge(q_ready, 1)
                pe.wait_ge(k_ready, 1)
                scores(0)
                scores(1)
            if B:
                pe.wait_ge(x3T_ready, 1)
                pe.wait_ge(ex1_loaded, 16)
                for j in range(3):
                    hidden_group(j, w_ex1, x3T, ex1_done)
                pe.wait_ge(ex_hidden_ready, 1)
                hidden_group(3, w_ex1, x3T, ex1_done)
            for h in range(HEADS):
                if A:
                    if h == 0:
                        pe.wait_ge(v_ready, 1)
                    pe.wait_ge(probs_ready, h + 1)
                    transposes(pe, T[h % 2], probs[:, h % RING, :, :]).then_inc(probsT_done, 1)
                    if h + 2 < HEADS:
                        scores(h + 2)
                    if h >= 1:
                        values(h - 1)
                if B and h == 2:
                    pe.wait_ge(ex2_loaded, 16)
                    pe.wait_ge(ex_hidden_ready, 4)
                if B and h in (2, 4):
                    last = row_major(pe, G[1], hidden, w_ex2, (h - 2) // 2, FC)
                    if h == 4:
                        last.then_inc(ex2_done, 1)
            if A:
                values(HEADS - 1).then_inc(attn_done, 1)
            if B:
                pe.wait_ge(inner_ready, 1)
                for r in range(CH):
                    for k in range(CH):
                        pe.matmul(G[2][:, r, :], firstT[:, k, r * P:(r + 1) * P], diff[:, 0, k, :], start=k == 0, stop=False)
                        last = pe.matmul(G[2][:, r, :], secondT[:, k, r * P:(r + 1) * P], prod[:, 6, k, :], start=False, stop=k == CH - 1)
                last.then_inc(stencil_done, 1)
            counts = []
            if A:
                counts += [(momentsA1_ready, 1), (act1_ready, 1), (momentsA2_ready, 1), (act2_ready, 1), (xn_ready, 1), (x1T_ready, 1),
                           (q_ready, 1), (k_ready, 1), (v_ready, 1), (probs_ready, HEADS), (probsT_ready, HEADS)]
            if B:
                counts += [(attn_ready, 1), (attnT_ready, 1), (xn2_ready, 1), (hT_ready, 1), (ff1_ready, 4), (x3_ready, 1), (x3T_ready, 1),
                           (ex1_loaded, 16), (ex2_loaded, 16), (ex_hidden_ready, 4), (inner_ready, 1)]
            settle(pe, counts)

        def scalar_body(act, A, B, store_b, first_store):
            def affine(dst, src, scale, shift):
                for c in range(CH):
                    last = act.activation(dst[:, c, :], src[:, c, :], ACT.Identity,
                                          bias=shift[:, c:c + 1], scale=scale[:, c:c + 1] if scale is not None else 1.0)
                return last

            if B:
                act.wait_ge(attnT_done, 1)
                act.activation(attnT[:, :, :], G[0][:, :, :], ACT.Copy).then_inc(attnT_ready, 1)
                act.wait_ge(hT_done, 1)
                affine(hT, G[2], cols[:, C_G2:C_G2 + CH], cols[:, C_BETA2:C_BETA2 + CH]).then_inc(hT_ready, 1)
            if A:
                act.wait_ge(half_ready, 1)
                act.activation(gate[:, :, :], half_w[:, :, :], ACT.Tanh).then_inc(tanh_ready, 1)
                act.wait_ge(mm1_done, 1)
                affine(h1, S[0], None, cols[:, C_BIN:C_BIN + CH]).then_inc(h1_ready, 1)
            if B:
                for j in range(4):
                    act.wait_ge(ff1_done, j + 1)
                    for u in range(CH):
                        c = CH * j + u
                        last = act.activation(hidden[:, c, :], G[j % 3][:, u, :], ACT.Gelu_apprx_sigmoid, bias=cols[:, C_FF1 + c:C_FF1 + c + 1])
                    last.then_inc(ff1_ready, 1)
            if A:
                act.wait_ge(half_ready, 2)
                act.activation(gate[:, :, :], half_w[:, :, :], ACT.Tanh).then_inc(tanh_ready, 1)
                act.wait_ge(x1T_done, 1)
                affine(x1T, T[0], cond[:, 4:4 + CH], cond[:, 6:6 + CH]).then_inc(x1T_ready, 1)
            if B:
                act.wait_ge(x3T_done, 1)
                act.activation(x3T[:, :, :], G[2][:, :, :], ACT.Copy).then_inc(x3T_ready, 1)
            if A:
                act.wait_ge(k_done, 1)
                affine(kT, S[1], None, cols[:, C_BK:C_BK + CH]).then_inc(k_ready, 1)
            if B:
                act.wait_ge(ex_cols_loaded, 16)
                for j in range(4):
                    act.wait_ge(ex1_done, j + 1)
                    for u in range(CH):
                        c = CH * j + u
                        last = act.activation(hidden[:, c, :], G[j % 3][:, u, :], ACT.Gelu, bias=ex_cols[:, c:c + 1])
                        if j == 3 and u == 0:
                            last.then_inc(ex1_free, 1)
                    last.then_inc(ex_hidden_ready, 1)
            if A:
                for h in range(HEADS):
                    for r in range(CH):
                        act.wait_ge(logits_ready, CH * h + r + 1)
                        p = probs[:, h % RING, r, :]
                        last = act.activation(p, p, ACT.Exp, scale=-1.0, bias=neg_max[:, r, h:h + 1], accum_out=denom[:, r, h:h + 1])
                        if r == 0 and h and h % HEADS_PER_GROUP == 0:
                            last.then_inc(bias_free[h // HEADS_PER_GROUP - 1], 1)
                    last.then_inc(probs_ready, 1)
            if B:
                act.wait_ge(res_ready, 1)
                if not first_store:
                    act.wait_ge(stored, 16)
                act.activation(res[:, :, :], f_r[:, :, :], ACT.Relu)
                act.drain()
                act.dma_start(out[bass.ds(store_b, 1), :, :].rearrange("a (c p) n -> p (a c) n", p=P), res[:, :, :]).then_inc(stored, 16)
            counts = []
            if A:
                counts += [(half_ready, 2), (mm1_done, 1), (x1T_done, 1), (k_done, 1), (logits_ready, CH * HEADS)]
            if B:
                counts += [(attnT_done, 1), (hT_done, 1), (ff1_done, 4), (x3T_done, 1), (ex_cols_loaded, 16), (ex1_done, 4), (res_ready, 1)]
                if not first_store:
                    counts += [(stored, 16)]
            settle(act, counts)

        def vector_body(dve, A, B):
            def layer_moments(src, s6, s2, var, eps):
                for r in range(CH):
                    dve.bn_stats(out=s6[:, r, :], in_=src[:, r, :])
                dve.drain()
                for r in range(CH):
                    dve.bn_aggr(out=s2[:, r, :], in_=s6[:, r, :])
                dve.drain()
                return dve.tensor_scalar(var[:, :], s2[:, :, 1], eps, None, ALU.add)

            def normalise(dst, src, s2, rstd):
                for r in range(CH):
                    last = dve.tensor_scalar(dst[:, r, :], src[:, r, :], s2[:, r, 0:1], rstd[:, r:r + 1], ALU.subtract, ALU.mult)
                return last

            def partition_moments(src, k):
                dve.bn_stats(out=stat6[:, 0, :], in_=src[:, :, :].rearrange("p c n -> p (c n)"))
                dve.drain()
                dve.bn_aggr(out=stat2[:, 0, :], in_=stat6[:, 0, :])
                dve.drain()
                dve.tensor_copy(stat4[:, 2 * k:2 * k + 1], stat2[:, 0, 0:1])
                dve.scalar_tensor_tensor(out=stat4[:, 2 * k + 1:2 * k + 2], in0=stat2[:, 0, 0:1], scalar=stat2[:, 0, 0:1], in1=stat2[:, 0, 1:2],
                                         op0=ALU.mult, op1=ALU.add)
                return dve.drain()

            def global_variance():
                dve.tensor_copy(stat2[:, 1, :], C[:, 0, 0:2])
                dve.drain()
                dve.scalar_tensor_tensor(out=varA[:, 1:2], in0=stat2[:, 1, 0:1], scalar=stat2[:, 1, 0:1], in1=stat2[:, 1, 1:2],
                                         op0=ALU.mult, op1=ALU.subtract)
                dve.drain()
                return dve.tensor_scalar(varA[:, 0:1], varA[:, 1:2], -1.0, 1e-5, ALU.mult, ALU.add)

            def silu_argument(src, free):
                ins = dve.scalar_tensor_tensor(out=h1[:, :, :], in0=src[:, :, :], scalar=stat2[:, 1, 0:1], in1=gammaT[:, :, :],
                                               op0=ALU.subtract, op1=ALU.mult)
                if free is not None:
                    ins.then_inc(free, 1)
                dve.drain()
                dve.scalar_tensor_tensor(out=h1[:, :, :], in0=h1[:, :, :], scalar=rstdA[:, 0:1], in1=betaT[:, :, :], op0=ALU.mult, op1=ALU.add)
                dve.drain()
                for c in range(CH):
                    last = dve.tensor_scalar(half_w[:, c, :], h1[:, c, :], cond[:, c:c + 1], cond[:, 2 + c:3 + c], ALU.mult, ALU.add)
                return last

            def silu_product():
                return dve.scalar_tensor_tensor(out=gate[:, :, :], in0=gate[:, :, :], scalar=1.0, in1=half_w[:, :, :], op0=ALU.add, op1=ALU.mult)

            if A is not None:
                dve.tensor_copy(cond[:, :], cond_all[:, bass.ds(A, 1), :].rearrange("p a n -> p (a n)"))
                dve.wait_ge(xT_loaded, 16)
                partition_moments(xT, 0).then_inc(momentsA1_ready, 1)
                dve.wait_ge(stats1_done, 1)
                global_variance().then_inc(varA_ready, 1)
            if B is not None:
                dve.tensor_copy(dt[:, :], dt_all[:, bass.ds(B, 1)])
                dve.wait_ge(proj_done, 1)
                dve.tensor_tensor(out=x2[:, :, :], in0=G[1][:, :, :], in1=rows[:, B_O:B_O + 1, :].to_broadcast([P, CH, DIM]), op=ALU.add)
                dve.drain()
                layer_moments(x2, statB6, statB2, varB, 1e-5).then_inc(varB_ready, 1)
            if A is not None:
                dve.wait_ge(rstdA_ready, 1)
                silu_argument(xT, xT_free).then_inc(half_ready, 1)
            if B is not None:
                dve.wait_ge(rstdB_ready, 1)
                normalise(xn2, x2, statB2, rstdB).then_inc(xn2_ready, 1)
            if A is not None:
                dve.wait_ge(tanh_ready, 1)
                silu_product().then_inc(act1_ready, 1)
                dve.wait_ge(h1_ready, 1)
                partition_moments(h1, 1).then_inc(momentsA2_ready, 1)
                dve.wait_ge(stats2_done, 1)
                global_variance().then_inc(varA_ready, 1)
                dve.wait_ge(rstdA_ready, 2)
                silu_argument(h1, None).then_inc(half_ready, 1)
                dve.wait_ge(tanh_ready, 2)
                silu_product().then_inc(act2_ready, 1)
                dve.wait_ge(mm2_done, 1)
                dve.wait_ge(x_bias_ready, 1)
                dve.tensor_tensor(out=x0[:, :, :], in0=S[1][:, :, :], in1=x_bias[:, :, :], op=ALU.add)
                dve.drain()
                layer_moments(x0, stat6, stat2, varA, 1e-5).then_inc(varA_ready, 1)
                dve.wait_ge(rstdA_ready, 3)
                normalise(x0, x0, stat2, rstdA).then_inc(xn_ready, 1)
            if B is not None:
                dve.wait_ge(ff2_done, 1)
                dve.wait_ge(x2_bias_ready, 1)
                dve.tensor_tensor(out=x3[:, :, :], in0=G[1][:, :, :], in1=x2_bias[:, :, :], op=ALU.add).then_inc(x3_ready, 1)
                dve.drain().then_inc(x3_for_bias, 1)
            if A is not None:
                dve.wait_ge(q_done, 1)
                for a, q in enumerate((q_even, q_odd)):
                    for c in range(CH):
                        last = dve.tensor_scalar(q[:, c, :], S[0][:, c, :], q_cols[:, a, 0:1], q_cols[:, a, 1 + c:2 + c], ALU.mult, ALU.add)
                last.then_inc(q_ready, 1)
                dve.wait_ge(v_done, 1)
                dve.tensor_tensor(out=v[:, :, :], in0=T[1][:, :, :], in1=rows[:, B_V:B_V + 1, :].to_broadcast([P, CH, DIM]), op=ALU.add)\
                    .then_inc(v_ready, 1)

            def logits(h):
                dve.wait_ge(scores_done, h + 1)
                dve.wait_ge(bias_masked, h + 1)
                for r in range(CH):
                    dve.tensor_tensor_reduce(out=probs[:, h % RING, r, :], in0=S[h % 2][:, r, :],
                                             in1=bias[:, h // HEADS_PER_GROUP, h % HEADS_PER_GROUP, r, :], scale=1.0, scalar=3.0e38,
                                             op0=ALU.add, op1=ALU.min, accum_out=neg_max[:, r, h:h + 1]).then_inc(logits_ready, 1)

            def move_probsT(h):
                dve.wait_ge(probsT_done, h + 1)
                dve.tensor_copy(probsT[:, h % RING, :, :], T[h % 2][:, :, :]).then_inc(probsT_ready, 1)

            def expert_tail():
                dve.wait_ge(ex2_done, 1)
                dve.wait_ge(x3_bias_ready, 1)
                dve.tensor_tensor(out=y[:, :, :], in0=G[1][:, :, :], in1=x3_bias[:, :, :], op=ALU.add).then_inc(ex2_free, 1)
                dve.drain()
                layer_moments(y, statB6, statB2, varB, 1e-12).then_inc(varB_ready, 1)

            def expert_norm():
                dve.wait_ge(rstdB_ready, 2)
                normalise(y, y, statB2, rstdB).then_inc(y_ready, 1)

            def edge_columns():
                dve.wait_ge(f_ready, 1)
                f_edge = f[:, :, :]
                for a in range(2):
                    for side in range(2):
                        lo = (DIM - 4) * side
                        dve.tensor_tensor(out=edge[:, a, :, side, :], in0=f_edge[:, :, lo:lo + 4], in1=edge_coef[:, a, :, side, :], op=ALU.mult)
                dve.drain()
                dst = diff[:, :, :, :].rearrange("p a c n -> p (a c) n")[:, :, 0:DIM:DIM - 1]
                dve.tensor_reduce(out=dst, in_=edge[:, :, :, :, :].rearrange("p a c s j -> p (a c) s j"), axis=AX.X, op=ALU.add).then_inc(edges_ready, 1)

            if A is not None:
                logits(0)
                logits(1)
            for h in range(HEADS):
                if A is not None:
                    if h + 2 < HEADS and h >= 1:
                        logits(h + 1)
                    elif h >= 1 and h + 1 < HEADS:
                        logits(h + 1)
                    move_probsT(h)
                if B is not None and h == 7:
                    expert_tail()
                if B is not None and h == 9:
                    expert_norm()
                if B is not None and h == 12:
                    edge_columns()
            if A is not None:
                dve.wait_ge(attn_done, 1)
                dve.reciprocal(inv[:, :, :], denom[:, :, :]).then_inc(bias_free[GROUPS - 1], 1)
                dve.drain()
                dve.tensor_tensor(out=attn[:, :, :].rearrange("p c (h e) -> p (c h) e", e=HD), in0=C[:, :, :].rearrange("p c (h e) -> p (c h) e", e=HD),
                                  in1=inv[:, :, :].rearrange("p c (h e) -> p (c h) e", e=1).to_broadcast([P, CH * HEADS, HD]), op=ALU.mult)\
                    .then_inc(attn_ready, 1)
            if B is not None:
                dve.wait_ge(terms_ready, 1)
                dve.scalar_tensor_tensor(out=y[:, :, :], in0=diff[:, 1, :, :], scalar=dt[:, 0:1], in1=f[:, :, :], op0=ALU.mult, op1=ALU.add)
                dve.drain()
                dve.wait_ge(stencil_done, 1)
                dve.scalar_tensor_tensor(out=f_r[:, :, :], in0=G[2][:, :, :], scalar=dt[:, 0:1], in1=y[:, :, :], op0=ALU.mult, op1=ALU.add)\
                    .then_inc(res_ready, 1)
            counts = []
            if A is not None:
                counts += [(xT_loaded, 16), (stats1_done, 1), (rstdA_ready, 3), (tanh_ready, 2), (h1_ready, 1), (stats2_done, 1), (mm2_done, 1),
                           (x_bias_ready, 1), (q_done, 1), (v_done, 1), (scores_done, HEADS), (bias_masked, HEADS), (probsT_done, HEADS), (attn_done, 1)]
            if B is not None:
                counts += [(proj_done, 1), (rstdB_ready, 2), (ff2_done, 1), (x2_bias_ready, 1), (ex2_done, 1), (x3_bias_ready, 1), (f_ready, 1),
                           (terms_ready, 1), (stencil_done, 1)]
            settle(dve, counts)

        def pool_body(pool, A, B):
            def rsqrt(var, rstd, n):
                return pool.tensor_tensor(out=rstd[:, 0:n], in0=var[:, 0:n], in1=consts[:, NEG_HALF:NEG_HALF + n], op=ALU.pow)

            def mask_bias(heads):
                for h in heads:
                    if h % HEADS_PER_GROUP == 0:
                        pool.wait_ge(bias_loaded[h // HEADS_PER_GROUP], 16)
                    t = bias[:, h // HEADS_PER_GROUP, h % HEADS_PER_GROUP, :, :]
                    pool.tensor_tensor(out=t, in0=mask_far[:, :, :], in1=t, op=ALU.subtract).then_inc(bias_masked, 1)

            if A:
                pool.wait_ge(mask_loaded, 16)
                pool.tensor_scalar(mask_far[:, :, :], mask_u8[:, :, :], 1.0e38, 1.0, ALU.mult, ALU.mult).then_inc(mask_free, 1)
                pool.wait_ge(x_loaded, 16)
                pool.tensor_tensor(out=x_bias[:, :, :], in0=x[:, :, :], in1=rows[:, B_OUT:B_OUT + 1, :].to_broadcast([P, CH, DIM]), op=ALU.add)\
                    .then_inc(x_bias_ready, 1)
                pool.drain().then_inc(x_free, 1)
                pool.wait_ge(varA_ready, 1)
                rsqrt(varA, rstdA, 1).then_inc(rstdA_ready, 1)
            if B:
                pool.wait_ge(varB_ready, 1)
                rsqrt(varB, rstdB, CH).then_inc(rstdB_ready, 1)
                pool.tensor_tensor(out=x2_bias[:, :, :], in0=x2[:, :, :], in1=rows[:, B_FF2:B_FF2 + 1, :].to_broadcast([P, CH, DIM]), op=ALU.add)\
                    .then_inc(x2_bias_ready, 1)
            if A:
                mask_bias(range(0, 2))
                pool.wait_ge(varA_ready, 2)
                rsqrt(varA, rstdA, 1).then_inc(rstdA_ready, 1)
                mask_bias(range(2, 4))
                pool.wait_ge(varA_ready, 3)
                rsqrt(varA, rstdA, CH).then_inc(rstdA_ready, 1)
            if B:
                pool.wait_ge(x3_for_bias, 1)
                pool.wait_ge(ex_rows_loaded, 16)
                pool.tensor_tensor(out=x3_bias[:, :, :], in0=x3[:, :, :], in1=ex_rows[:, 0:1, :].to_broadcast([P, CH, DIM]), op=ALU.add)\
                    .then_inc(x3_bias_ready, 1)
            if A:
                mask_bias(range(4, 12))
            if B:
                pool.wait_ge(varB_ready, 2)
                rsqrt(varB, rstdB, CH).then_inc(rstdB_ready, 1)
            if A:
                mask_bias(range(12, 16))
            if B:
                pool.wait_ge(y_ready, 1)
                pool.tensor_tensor(out=f[:, :, :], in0=y[:, :, :], in1=ex_rows[:, 1:2, :].to_broadcast([P, CH, DIM]), op=ALU.mult)
                pool.drain()
                pool.tensor_tensor(out=f[:, :, :], in0=f[:, :, :], in1=ex_rows[:, 2:3, :].to_broadcast([P, CH, DIM]), op=ALU.add).then_inc(f_ready, 1)
                pool.drain().then_inc(ex_small_free, 1)
                for a in range(7):
                    pool.tensor_tensor(out=prod[:, a, :, :], in0=coef[:, a, :, :], in1=f[:, :, :], op=ALU.mult)
                pool.drain()
                for a in range(2):
                    pool.tensor_tensor(out=diff[:, a, :, 1:DIM - 1], in0=prod[:, a, :, 2:DIM], in1=prod[:, 2 + a, :, 0:DIM - 2], op=ALU.add)
                pool.drain()
                pool.wait_ge(edges_ready, 1)
                pool.tensor_tensor(out=diff[:, 0, :, :], in0=diff[:, 0, :, :], in1=prod[:, 4, :, :], op=ALU.subtract).then_inc(inner_ready, 1)
                pool.tensor_tensor(out=diff[:, 1, :, :], in0=diff[:, 1, :, :], in1=prod[:, 5, :, :], op=ALU.subtract).then_inc(terms_ready, 1)
            counts = []
            if A:
                counts += [(mask_loaded, 16), (x_loaded, 16), (varA_ready, 3)] + [(s, 16) for s in bias_loaded]
            if B:
                counts += [(varB_ready, 2), (x3_for_bias, 1), (ex_rows_loaded, 16), (y_ready, 1), (edges_ready, 1)]
            settle(pool, counts)

        with nc.Block() as block:
            @block.sync
            def _(sp):
                sync_body(sp, 0, None)
                with sp.Fori(1, BATCHES) as i:
                    sync_body(sp, i, i - 1)
                sync_body(sp, None, BATCHES - 1)

            @block.tensor
            def _(pe):
                tensor_body(pe, True, False)
                with pe.Fori(1, BATCHES) as i:
                    tensor_body(pe, True, True)
                tensor_body(pe, False, True)

            @block.scalar
            def _(act):
                scalar_body(act, True, False, None, False)
                scalar_body(act, True, True, 0, True)
                with act.Fori(2, BATCHES) as i:
                    scalar_body(act, True, True, i - 1, False)
                scalar_body(act, False, True, BATCHES - 1, False)
                act.wait_ge(stored, 16)

            @block.vector
            def _(dve):
                vector_body(dve, 0, None)
                with dve.Fori(1, BATCHES) as i:
                    vector_body(dve, i, i - 1)
                vector_body(dve, None, BATCHES - 1)

            @block.gpsimd
            def _(pool):
                pool_body(pool, True, False)
                with pool.Fori(1, BATCHES) as i:
                    pool_body(pool, True, True)
                pool_body(pool, False, True)


def columns(v):
    return np.asarray(v).reshape(-1, P).T


def kernel(**inputs):
    import concourse.bacc as _bacc
    from concourse import mybir as _mybir
    from concourse.bass_utils import run_bass_kernel_spmd as _run

    g = {k: np.asarray(a) for k, a in inputs.items()}
    f0 = np.exp(np.arange(NOISE // 2, dtype=np.float32) * np.float32(-math.log(10000.0) / (NOISE // 2 - 1)))
    f1 = np.exp(np.arange(DIM // 2, dtype=np.float32) * np.float32(-math.log(10000.0) / (DIM // 2 - 1)))
    p = np.arange(P)
    phase0 = np.where(p < NOISE // 2, 0.0, 0.25).astype(np.float32)
    even = np.where((p // HD) % 2 == 0, -1.0 / math.sqrt(HD), 0.0).astype(np.float32)
    odd = np.where((p // HD) % 2 == 1, -1.0 / math.sqrt(HD), 0.0).astype(np.float32)
    zero, quarter = np.zeros(P, np.float32), np.full(P, 0.25, np.float32)
    turn = np.float32(TWO_PI)
    tables = np.stack([np.concatenate([f0, f0]), f1, even, odd, phase0, zero, quarter, phase0 * turn, zero, quarter * turn], axis=1)
    cols = np.concatenate([columns(g[n]) for n in (
        "L0_cond_b_in", "L1_cond_bk", "L1_cond_g2", "L1_cond_beta2", "L1_cond_bq", "L1_cond_b1", "L0_cond_b1", "L0_cond_b2",
        "L0_cond_bsc", "L0_cond_bsh", "L1_cond_b_ada")] + [tables], axis=1)
    first, second = stencil_matrices()
    arrays = {
        "x": g["x"], "xT": g["x"].transpose(0, 2, 1),
        "mask": g["mask_Bx1xSxS_bk0"].reshape(BATCHES, SEQ, SEQ),
        "fside": g["fside_Bx16xSxS_0"].reshape(BATCHES, GROUPS, HEADS_PER_GROUP, CH, P, SEQ).transpose(0, 1, 4, 2, 3, 5)
        .reshape(BATCHES, GROUPS, P, HEADS_PER_GROUP * CH * SEQ),
        "cols": cols, "gammaT": g["L0_cond_gamma"].T, "betaT": g["L0_cond_beta"].T, "firstT": first.T, "secondT": second.T,
        "ex_bi": g["L2_cond_bi"].reshape(EXPERTS, FC, P).transpose(0, 2, 1),
        "ex_rows": np.concatenate([g["L2_cond_bo"], g["L2_cond_gamma"], g["L2_cond_beta"]], axis=1),
    }
    for n in ("condB_t", "condB_dt", "itok_B_34_63", "itok_B_0_7", "L0_cond_W1", "L0_cond_W2", "L0_cond_Wsc", "L0_cond_Wsh", "L0_cond_W_in",
              "L0_cond_W_out", "L0_cond_b_out", "L1_cond_W_ada", "L1_cond_Wq", "L1_cond_Wk", "L1_cond_Wv", "L1_cond_Wo", "L1_cond_bv",
              "L1_cond_bo", "L1_cond_W1", "L1_cond_W2", "L1_cond_b2", "L2_cond_Wi", "L2_cond_Wo", "L3_cond_A_grid", "L3_cond_B_grid"):
        arrays[n] = g[n]
    nc = _bacc.Bacc("TRN2", target_bir_lowering=False, num_devices=1)
    sent, d = {}, {}
    for n, a in arrays.items():
        a = np.ascontiguousarray(a)
        sent[f"in_{n}"] = a
        d[n] = nc.dram_tensor(f"in_{n}", a.shape, _mybir.dt.from_np(a.dtype), kind="ExternalInput").ap()
    out = nc.dram_tensor("out", (BATCHES, SEQ, DIM), _mybir.dt.float32, kind="ExternalOutput").ap()
    build_program(nc, d, out)
    r = _run(nc, [sent], core_ids=[0])
    return r.results[0]["out"]
```

```python
import math
from contextlib import ExitStack

import concourse.bass as bass
import numpy as np
from concourse import mybir

BATCHES, SEQ, DIM, HEADS, FF, EXPERTS = 32, 256, 256, 16, 1024, 8
NOISE = 128
P = 128
HD = DIM // HEADS
CH = DIM // P
FC = FF // P
HEADS_PER_CHUNK = P // HD
HEADS_PER_GROUP = 4
GROUPS = HEADS // HEADS_PER_GROUP
RING = 3
TWO_PI = 2.0 * math.pi
ROUND = 12582912.0
COND = 4 * CH


def stencil_matrices():
    first = np.zeros((SEQ, SEQ), np.float32)
    second = np.zeros((SEQ, SEQ), np.float32)
    for i in range(1, SEQ - 1):
        first[i, i - 1], first[i, i + 1] = -0.5, 0.5
        second[i, i - 1], second[i, i], second[i, i + 1] = 1.0, -2.0, 1.0
    first[0, :3] = (-1.5, 2.0, -0.5)
    first[-1, -3:] = (0.5, -2.0, 1.5)
    second[0, :4] = (2.0, -5.0, 4.0, -1.0)
    second[-1, -4:] = (-1.0, 4.0, -5.0, 2.0)
    return first, second


def build_program(nc, d, out):
    f32, i32, u8 = mybir.dt.float32, mybir.dt.int32, mybir.dt.uint8
    ALU, ACT, AX = mybir.AluOpType, mybir.ActivationFunctionType, mybir.AxisListType
    PE_, DVE_ = nc.tensor, nc.vector

    ctx = ExitStack()
    with ctx:
        def sb(name, shape, dt=f32):
            return ctx.enter_context(nc.sbuf_tensor(name, [P] + shape, dt))

        def bank(name):
            return ctx.enter_context(nc.psum_tensor(name, [P, CH, DIM], f32))

        def sem(name):
            return ctx.enter_context(nc.semaphore(name))

        w_in, w_out = sb("w_in", [CH, DIM]), sb("w_out", [CH, DIM])
        w_q, w_k, w_v, w_o = (sb(n, [CH, DIM]) for n in ("w_q", "w_k", "w_v", "w_o"))
        w_ff1, w_ff2 = sb("w_ff1", [CH, FF]), sb("w_ff2", [FC, DIM])
        w_ex1, w_ex2 = sb("w_ex1", [CH, FF]), sb("w_ex2", [FC, DIM])
        gammaT, betaT = sb("gammaT", [CH, SEQ]), sb("betaT", [CH, SEQ])
        coef = sb("coef", [7, CH, DIM])
        edge_coef = sb("edge_coef", [2, CH, 2, 4])
        firstT, secondT = sb("firstT", [CH, SEQ]), sb("secondT", [CH, SEQ])
        ident, mean_w = sb("ident", [P]), sb("mean_w", [P])
        rows = sb("rows", [4, DIM])
        cols = sb("cols", [44])
        consts = sb("consts", [16])
        q_cols = sb("q_cols", [2, 1 + CH])
        ex_rows, ex_cols = sb("ex_rows", [3, DIM]), sb("ex_cols", [FC])
        cond_all, cond = sb("cond_all", [BATCHES, COND]), sb("cond", [COND])
        dt_all, dt = sb("dt_all", [BATCHES]), sb("dt", [1])
        expert = ctx.enter_context(nc.sbuf_tensor("expert", [1, BATCHES], i32))
        B_OUT, B_V, B_O, B_FF2 = range(4)
        C_BIN, C_BK, C_G2, C_BETA2, C_BQ, C_FF1 = 0, 2, 4, 6, 8, 10
        C_B1, C_B2, C_BSC, C_BSH, C_ADA = 18, 22, 26, 28, 30
        C_FREQ0, C_FREQ1, C_EVEN, C_ODD, C_PHASE = 34, 35, 36, 37, 38
        NEG_HALF = 0

        xT, x, mask_u8 = sb("xT", [CH, SEQ]), sb("x", [CH, DIM]), sb("mask_u8", [CH, SEQ], u8)
        bias = sb("bias", [GROUPS, HEADS_PER_GROUP, CH, SEQ])
        stat6, stat2, stat4 = sb("stat6", [CH, 6]), sb("stat2", [CH, 2]), sb("stat4", [4])
        varA, rstdA = sb("varA", [CH]), sb("rstdA", [CH])
        half_w, gate = sb("half_w", [CH, SEQ]), sb("gate", [CH, SEQ])
        h1 = sb("h1", [CH, SEQ])
        x_bias, mask_far = sb("x_bias", [CH, DIM]), sb("mask_far", [CH, SEQ])
        x0 = sb("x0", [CH, DIM])
        x1T, x1T_kept_sb = sb("x1T", [CH, SEQ]), sb("x1T_kept_sb", [CH, SEQ])
        q_even, q_odd, kT = sb("q_even", [CH, SEQ]), sb("q_odd", [CH, SEQ]), sb("kT", [CH, SEQ])
        v = sb("v", [CH, DIM])
        probs, probsT = sb("probs", [RING, CH, SEQ]), sb("probsT", [RING, CH, SEQ])
        neg_max, denom = sb("neg_max", [2, CH, HEADS]), sb("denom", [CH, HEADS])
        inv = sb("inv", [CH, HEADS])
        attn = sb("attn", [CH, DIM])
        attnT = sb("attnT", [CH, SEQ])
        statB6, statB2 = sb("statB6", [CH, 6]), sb("statB2", [CH, 2])
        varB, rstdB = sb("varB", [CH]), sb("rstdB", [CH])
        x2, x2_bias, xn2, hT = sb("x2", [CH, DIM]), sb("x2_bias", [CH, DIM]), sb("xn2", [CH, DIM]), sb("hT", [CH, SEQ])
        hidden = sb("hidden", [FC, SEQ])
        x3, x3_bias, x3T = sb("x3", [CH, DIM]), sb("x3_bias", [CH, DIM]), sb("x3T", [CH, SEQ])
        y, f = sb("y", [CH, DIM]), sb("f", [CH, DIM])
        prod = sb("prod", [7, CH, DIM])
        diff = sb("diff", [2, CH, DIM])
        edge = sb("edge", [2, CH, 2, 4])
        f_r, res = sb("f_r", [CH, DIM]), sb("res", [CH, DIM])

        S = [bank("S0"), bank("S1")]
        T = [bank("T0"), bank("T1")]
        C = bank("C")
        G = [bank("G0"), bank("G1")]
        F = bank("F")

        stage = bias[:, :, :, :].rearrange("p a b c n -> p (a b c n)")
        at = [0]

        def scratch(n):
            at[0] += n
            return stage[:, at[0] - n:at[0]]

        s_w1 = scratch(512)
        s_w2 = scratch(2048).rearrange("p (c n) -> p c n", c=4)
        s_wsc = scratch(1024).rearrange("p (c n) -> p c n", c=4)
        s_wsh = scratch(1024).rearrange("p (c n) -> p c n", c=4)
        s_ada = scratch(1024).rearrange("p (c n) -> p c n", c=2)
        grids = scratch(5 * CH * DIM).rearrange("p (a c n) -> p a c n", a=5, c=CH)
        ang = half_w[:, :, :].rearrange("p c (a n) -> p (c a) n", n=BATCHES)
        emb = gate[:, :, :].rearrange("p c (a n) -> p (c a) n", n=BATCHES)
        hid = h1[:, :, :].rearrange("p c (a n) -> p (c a) n", n=BATCHES)
        t_f = x0[:, 0, 0:3 * BATCHES].rearrange("p (a n) -> p a n", n=BATCHES)
        t_i = ctx.enter_context(nc.sbuf_tensor("t_i", [P, BATCHES], i32))

        weights_loaded, cond_loaded, expert_loaded = sem("weights_loaded"), sem("cond_loaded"), sem("expert_loaded")
        ident_zeroed, tables_made, edges_cleared = sem("ident_zeroed"), sem("tables_made"), sem("edges_cleared")
        angles_ready, sines_ready, emb_ready = sem("angles_ready"), sem("sines_ready"), sem("emb_ready")
        mlp_mm, mlp_act = sem("mlp_mm"), sem("mlp_act")
        silu_half, silu_tanh = sem("silu_half"), sem("silu_tanh")
        ex1_free, ex2_free, ex_small_free = sem("ex1_free"), sem("ex2_free"), sem("ex_small_free")

        weight_loads = [
            (w_in, "L0_cond_W_in"), (w_out, "L0_cond_W_out"), (w_q, "L1_cond_Wq"), (w_k, "L1_cond_Wk"),
            (w_v, "L1_cond_Wv"), (w_o, "L1_cond_Wo"), (w_ff1, "L1_cond_W1"), (w_ff2, "L1_cond_W2"),
            (gammaT, "gammaT"), (betaT, "betaT"), (firstT, "firstT"), (secondT, "secondT"),
        ]
        stage_loads = [(s_w2, "L0_cond_W2"), (s_wsc, "L0_cond_Wsc"), (s_wsh, "L0_cond_Wsh"), (s_ada, "L1_cond_W_ada")]

        with nc.Block() as block:
            @block.sync
            def _(sp):
                sp.dma_start(cols[:, :], d["cols"]).then_inc(cond_loaded, 16)
                sp.dma_start(t_f[:, 0, :], d["condB_t"].rearrange("(a n) -> a n", a=1).to_broadcast([P, BATCHES])).then_inc(cond_loaded, 16)
                sp.dma_start(t_i[:, :], d["itok_B_34_63"].rearrange("(a n) -> a n", a=1).to_broadcast([P, BATCHES])).then_inc(cond_loaded, 16)
                sp.dma_start(dt_all[:, :], d["condB_dt"].rearrange("(a n) -> a n", a=1).to_broadcast([P, BATCHES])).then_inc(cond_loaded, 16)
                sp.dma_start(s_w1, d["L0_cond_W1"]).then_inc(cond_loaded, 16)
                for dst, name in stage_loads:
                    sp.dma_start(dst, d[name].rearrange("(c p) n -> p c n", p=P)).then_inc(cond_loaded, 16)
                for a in range(2):
                    sp.dma_start(grids[:, a, :, :], d["L3_cond_A_grid"][a, :, :].rearrange("(c p) n -> p c n", p=P)).then_inc(cond_loaded, 16)
                for a in range(3):
                    sp.dma_start(grids[:, 2 + a, :, :], d["L3_cond_B_grid"][a, :, :].rearrange("(c p) n -> p c n", p=P)).then_inc(cond_loaded, 16)
                for dst, name in weight_loads:
                    sp.dma_start(dst[:, :, :], d[name].rearrange("(c p) n -> p c n", p=P)).then_inc(weights_loaded, 16)
                for a, name in enumerate(("L0_cond_b_out", "L1_cond_bv", "L1_cond_bo", "L1_cond_b2")):
                    sp.dma_start(rows[:, a, :], d[name].rearrange("(a n) -> a n", a=1).to_broadcast([P, DIM])).then_inc(weights_loaded, 16)
                sp.dma_start(expert[:, :], d["itok_B_0_7"].rearrange("(a n) -> a n", a=1)).then_inc(expert_loaded, 16)
                sp.wait_ge(expert_loaded, 16)
                sp.wait_ge(weights_loaded, 16 * (len(weight_loads) + 4))

            @block.gpsimd
            def _(pool):
                pool.memset(ident[:, :], 0.0).then_inc(ident_zeroed, 1)
                pool.memset(mean_w[:, :], 1.0 / P).then_inc(tables_made, 1)
                pool.memset(consts[:, 0:4], -0.5).then_inc(ex1_free, 1)
                pool.memset(consts[:, 4:8], -0.5).then_inc(ex2_free, 1)
                pool.memset(consts[:, 8:16], -0.5).then_inc(ex_small_free, 1)
                pool.memset(edge_coef[:, :, :, :, :], 0.0).then_inc(edges_cleared, 1)
                pool.wait_ge(ident_zeroed, 1)
                pool.affine_select(out=ident[:, :], in_=ident[:, :], compare_op=ALU.not_equal, fill=1.0,
                                   base=0, pattern=[[-1, P]], channel_multiplier=1).then_inc(tables_made, 1)

            @block.vector
            def _(dve):
                dve.wait_ge(cond_loaded, 16 * 14)
                dve.tensor_copy(t_f[:, 1, :], t_i[:, :])
                dve.tensor_scalar(ang[:, 0, :], t_f[:, 0, :], 5000.0, cols[:, C_FREQ0:C_FREQ0 + 1], ALU.mult, ALU.mult)
                dve.drain()
                dve.tensor_scalar(t_f[:, 2, :], t_f[:, 1, :], 0.01, 4000.0, ALU.mult, ALU.mult)
                dve.drain()
                for a in (1, 2):
                    dve.tensor_scalar(ang[:, a, :], t_f[:, 2, :], cols[:, C_FREQ1:C_FREQ1 + 1], None, ALU.mult)
                dve.drain()
                for a in range(3):
                    dve.tensor_scalar(ang[:, 3 + a, :], ang[:, a, :], 1.0 / TWO_PI, cols[:, C_PHASE + a:C_PHASE + a + 1], ALU.mult, ALU.add)
                dve.drain()
                dve.tensor_scalar(ang[:, 6:9, :], ang[:, 3:6, :], ROUND, None, ALU.add)
                dve.drain()
                dve.tensor_scalar(ang[:, 3:6, :], ang[:, 6:9, :], -ROUND, None, ALU.add)
                hi = 6.28125
                mid = float(np.float32(np.round((TWO_PI - hi) * 2 ** 21) / 2 ** 21))
                lo = TWO_PI - hi - mid
                for part in (hi, mid, lo):
                    dve.drain()
                    dve.scalar_tensor_tensor(out=ang[:, 0:3, :], in0=ang[:, 3:6, :], scalar=-part, in1=ang[:, 0:3, :], op0=ALU.mult, op1=ALU.add)
                dve.drain()
                for a in range(3):
                    dve.tensor_scalar(ang[:, 9 + a, :], ang[:, a, :], cols[:, C_PHASE + 3 + a:C_PHASE + 4 + a], None, ALU.add)
                dve.drain()
                dve.tensor_scalar(ang[:, 12:15, :], ang[:, 9:12, :], 3.1415925, -3.1415925, ALU.min, ALU.max).then_inc(angles_ready, 1)
                dve.wait_ge(sines_ready, 1)
                dve.tensor_scalar(emb[:, 3:5, :], emb[:, 1:3, :], 0.5, None, ALU.mult).then_inc(silu_half, 1)
                dve.wait_ge(silu_tanh, 1)
                dve.scalar_tensor_tensor(out=emb[:, 1:3, :], in0=emb[:, 5:7, :], scalar=1.0, in1=emb[:, 3:5, :], op0=ALU.add, op1=ALU.mult).then_inc(emb_ready, 1)
                dve.wait_ge(mlp_mm, 1)
                for c in range(4):
                    dve.tensor_scalar(hid[:, c, :], G[0][:, 0, c * BATCHES:(c + 1) * BATCHES], cols[:, C_B1 + c:C_B1 + c + 1], 0.5, ALU.add, ALU.mult)
                dve.drain().then_inc(silu_half, 1)
                dve.wait_ge(silu_tanh, 2)
                dve.scalar_tensor_tensor(out=hid[:, 8:12, :], in0=hid[:, 4:8, :], scalar=1.0, in1=hid[:, 0:4, :], op0=ALU.add, op1=ALU.mult).then_inc(mlp_act, 1)
                dve.wait_ge(mlp_mm, 2)
                for c in range(4):
                    dve.tensor_scalar(hid[:, 12 + c, :], G[1][:, 0, c * BATCHES:(c + 1) * BATCHES], cols[:, C_B2 + c:C_B2 + c + 1], None, ALU.add)
                dve.drain().then_inc(mlp_act, 1)
                dve.wait_ge(mlp_mm, 3)
                for c in range(4):
                    dve.tensor_scalar(cond_all[:, :, c], F[:, 0, c * BATCHES:(c + 1) * BATCHES], cols[:, C_BSC + c:C_BSC + c + 1], 0.5, ALU.add, ALU.mult)
                for c in range(4):
                    dve.tensor_scalar(cond_all[:, :, 4 + c], F[:, 1, c * BATCHES:(c + 1) * BATCHES], cols[:, C_ADA + c:C_ADA + c + 1],
                                      1.0 if c < 2 else 0.0, ALU.add, ALU.add)
                for a, col in enumerate((C_EVEN, C_ODD)):
                    dve.tensor_copy(q_cols[:, a, 0:1], cols[:, col:col + 1])
                    dve.tensor_scalar(q_cols[:, a, 1:1 + CH], cols[:, C_BQ:C_BQ + CH], cols[:, col:col + 1], None, ALU.mult)
                A0, A1, B0, B1, B2 = (grids[:, a, :, :] for a in range(5))
                dve.tensor_scalar(coef[:, 0, :, :], B2, 0.5, None, ALU.mult)
                dve.tensor_scalar(coef[:, 2, :, :], B2, -0.5, None, ALU.mult)
                dve.tensor_copy(coef[:, 4, :, :], A0)
                dve.tensor_copy(coef[:, 5, :, :], B1)
                dve.tensor_scalar(coef[:, 6, :, :], B0, 0.5, None, ALU.mult)
                dve.tensor_scalar(prod[:, 0, :, :], A1, 0.5, None, ALU.mult)
                dve.tensor_scalar(prod[:, 1, :, :], B1, 0.5, None, ALU.mult)
                dve.drain()
                dve.tensor_tensor(out=coef[:, 1, :, :], in0=prod[:, 1, :, :], in1=prod[:, 0, :, :], op=ALU.subtract)
                dve.tensor_tensor(out=coef[:, 3, :, :], in0=prod[:, 1, :, :], in1=prod[:, 0, :, :], op=ALU.add)
                N = DIM
                ec = edge_coef
                dve.wait_ge(edges_cleared, 1)
                for side, j, k in ((0, 0, -1.5), (0, 1, 2.0), (0, 2, -0.5), (1, 1, 0.5), (1, 2, -2.0), (1, 3, 1.5)):
                    col = j + (N - 4) * side
                    dve.tensor_scalar(ec[:, 0, :, side, j], B2[:, :, col], k, None, ALU.mult)
                for side, j, kb, ka in ((0, 0, 2.0, 1.5), (0, 1, -2.5, -2.0), (0, 2, 2.0, 0.5), (0, 3, -0.5, 0.0),
                                        (1, 0, -0.5, 0.0), (1, 1, 2.0, -0.5), (1, 2, -2.5, 2.0), (1, 3, 2.0, -1.5)):
                    col = j + (N - 4) * side
                    dve.tensor_scalar(edge[:, 0, :, side, j], A1[:, :, col], ka, None, ALU.mult)
                    dve.tensor_scalar(edge[:, 1, :, side, j], B1[:, :, col], kb, None, ALU.mult)
                dve.drain()
                dve.tensor_tensor(out=ec[:, 1, :, :, :], in0=edge[:, 0, :, :, :], in1=edge[:, 1, :, :, :], op=ALU.add)

            @block.scalar
            def _(act):
                act.wait_ge(angles_ready, 1)
                act.activation(emb[:, 0:3, :], ang[:, 12:15, :], ACT.Sin).then_inc(sines_ready, 1)
                act.wait_ge(silu_half, 1)
                act.activation(emb[:, 5:7, :], emb[:, 3:5, :], ACT.Tanh).then_inc(silu_tanh, 1)
                act.wait_ge(silu_half, 2)
                act.activation(hid[:, 4:8, :], hid[:, 0:4, :], ACT.Tanh).then_inc(silu_tanh, 1)

            @block.tensor
            def _(pe):
                pe.wait_ge(cond_loaded, 16 * 14)
                pe.wait_ge(emb_ready, 1)
                for c in range(4):
                    last = pe.matmul(G[0][:, 0, c * BATCHES:(c + 1) * BATCHES], s_w1[:, c * P:(c + 1) * P], emb[:, 0, :], start=True, stop=True)
                last.then_inc(mlp_mm, 1)
                for c in range(4):
                    for k in range(2):
                        pe.matmul(F[:, 1, c * BATCHES:(c + 1) * BATCHES], s_ada[:, k, c * P:(c + 1) * P], emb[:, 1 + k, :], start=k == 0, stop=k == 1)
                pe.wait_ge(mlp_act, 1)
                for c in range(4):
                    for k in range(4):
                        last = pe.matmul(G[1][:, 0, c * BATCHES:(c + 1) * BATCHES], s_w2[:, k, c * P:(c + 1) * P], hid[:, 8 + k, :], start=k == 0, stop=k == 3)
                last.then_inc(mlp_mm, 1)
                pe.wait_ge(mlp_act, 2)
                for w, base in ((s_wsc, 0), (s_wsh, 2)):
                    for c in range(2):
                        for k in range(4):
                            last = pe.matmul(F[:, 0, (base + c) * BATCHES:(base + c + 1) * BATCHES], w[:, k, c * P:(c + 1) * P], hid[:, 12 + k, :], start=k == 0, stop=k == 3)
                last.then_inc(mlp_mm, 1)


        xT_loaded, x_loaded, mask_loaded = sem("xT_loaded"), sem("x_loaded"), sem("mask_loaded")
        bias_loaded = [sem(f"bias_loaded{g}") for g in range(GROUPS)]
        ex1_loaded, ex2_loaded, ex_rows_loaded, ex_cols_loaded = (sem(n) for n in ("ex1_loaded", "ex2_loaded", "ex_rows_loaded", "ex_cols_loaded"))
        xT_free, x_free, mask_free = sem("xT_free"), sem("x_free"), sem("mask_free")
        bias_free = [sem(f"bias_free{g}") for g in range(GROUPS)]
        stored = sem("stored")
        momentsA1_ready, momentsA2_ready, act1_ready, act2_ready, xn_ready, xn2_ready, x3_ready = (sem(n) for n in (
            "momentsA1_ready", "momentsA2_ready", "act1_ready", "act2_ready", "xn_ready", "xn2_ready", "x3_ready"))
        q_ready, v_ready, probsT_ready, attn_ready, field_read = (sem(n) for n in ("q_ready", "v_ready", "probsT_ready", "attn_ready", "field_read"))
        attnT_ready, hT_ready, ff1_ready, x1T_ready, x3T_ready, k_ready, ex_hidden_ready, probs_ready = (sem(n) for n in (
            "attnT_ready", "hT_ready", "ff1_ready", "x1T_ready", "x3T_ready", "k_ready", "ex_hidden_ready", "probs_ready"))
        stats1_done, stats2_done, proj_done, mm2_done, ff2_done, q_done, v_done = (sem(n) for n in (
            "stats1_done", "stats2_done", "proj_done", "mm2_done", "ff2_done", "q_done", "v_done"))
        scores_done, probsT_done, attn_done, ex2_done, stencil_done = (sem(n) for n in (
            "scores_done", "probsT_done", "attn_done", "ex2_done", "stencil_done"))
        attnT_done, mm1_done, hT_done, ff1_done, x1T_done, x3T_done, k_done, ex1_done = (sem(n) for n in (
            "attnT_done", "mm1_done", "hT_done", "ff1_done", "x1T_done", "x3T_done", "k_done", "ex1_done"))
        half_ready, tanh_ready, h1_ready, logits_ready, res_ready = (sem(n) for n in (
            "half_ready", "tanh_ready", "h1_ready", "logits_ready", "res_ready"))
        varA_ready, rstdA_ready, varB_ready, rstdB_ready, x_bias_ready, x2_bias_ready = (sem(n) for n in (
            "varA_ready", "rstdA_ready", "varB_ready", "rstdB_ready", "x_bias_ready", "x2_bias_ready"))
        bias_masked, x3_for_bias, x3_bias_ready, y_ready, f_ready, edges_ready, terms_ready = (sem(n) for n in (
            "bias_masked", "x3_for_bias", "x3_bias_ready", "y_ready", "f_ready", "edges_ready", "terms_ready"))
        inner_ready, x1T_kept = sem("inner_ready"), sem("x1T_kept")

        AHEAD = 2
        LATER = HEADS - AHEAD

        def settle(eng, counts):
            eng.drain()
            for s, n in counts:
                eng.sem_inc(s, -n)

        def sync_body(sp, front, attention, tail):
            used = []

            def reuse(s):
                sp.wait_ge(s, 1)
                used.append(s)

            def chunked(src, b):
                return d[src][bass.ds(b, 1), :, :].rearrange("a (c p) n -> p (a c) n", p=P)

            def load_bias(b, g):
                if not (isinstance(b, int) and b == 0):
                    reuse(bias_free[g])
                src = d["fside"][bass.ds(b, 1), g, :, :].rearrange("a p (h c n) -> p (a h) c n", h=HEADS_PER_GROUP, c=CH)
                sp.dma_start(bias[:, g, :, :, :], src).then_inc(bias_loaded[g], 16)

            later = not (isinstance(front, int) and front == 0)
            if front is not None:
                if later:
                    reuse(xT_free)
                sp.dma_start(xT[:, :, :], chunked("xT", front)).then_inc(xT_loaded, 16)
                if later:
                    reuse(x_free)
                sp.dma_start(x[:, :, :], chunked("x", front)).then_inc(x_loaded, 16)
            if attention is not None:
                load_bias(attention, GROUPS - 1)
            if tail is not None:
                sp.wait_ge(expert_loaded, 16)
                e = sp.value_load(expert[0:1, bass.ds(tail, 1)], min_val=0, max_val=EXPERTS - 1)
                one = bass.ds(e, 1)
                reuse(ex1_free)
                sp.dma_start(w_ex1[:, :, :], d["L2_cond_Wi"][one, :, :].rearrange("a (c p) n -> p (a c) n", p=P)).then_inc(ex1_loaded, 16)
                reuse(ex_small_free)
                sp.dma_start(ex_cols[:, :], d["ex_bi"][one, :, :].rearrange("a p n -> p (a n)")).then_inc(ex_cols_loaded, 16)
                sp.dma_start(ex_rows[:, :, :].rearrange("p a n -> p (a n)"),
                             d["ex_rows"][one, :].to_broadcast([P, 3 * DIM])).then_inc(ex_rows_loaded, 16)
                reuse(ex2_free)
                sp.dma_start(w_ex2[:, :, :], d["L2_cond_Wo"][one, :, :].rearrange("a (c p) n -> p (a c) n", p=P)).then_inc(ex2_loaded, 16)
            if front is not None:
                if later:
                    reuse(mask_free)
                sp.dma_start(mask_u8[:, :, :], chunked("mask", front)).then_inc(mask_loaded, 16)
                for g in range(GROUPS - 1):
                    load_bias(front, g)
            if used:
                settle(sp, [(s, 1) for s in used])

        def transposes(pe, dst, src):
            for c in range(CH):
                for r in range(CH):
                    last = pe.transpose(dst[:, c, r * P:(r + 1) * P], src[:, r, c * P:(c + 1) * P], ident[:, :])
            return last

        def feature_major(pe, dst, w, srcT):
            for c in range(CH):
                for k in range(CH):
                    last = pe.matmul(dst[:, c, :], w[:, k, c * P:(c + 1) * P], srcT[:, k, :], start=k == 0, stop=k == CH - 1)
            return last

        def row_major(pe, dst, srcT, w, r, chunks):
            for k in range(chunks):
                last = pe.matmul(dst[:, r, :], srcT[:, k, r * P:(r + 1) * P], w[:, k, :], start=k == 0, stop=k == chunks - 1)
            return last

        def tensor_body(pe, front, attention, tail):
            def hidden_layer(w, srcT, done, read):
                for j in range(4):
                    if j >= 2:
                        pe.wait_ge(read, j - 1)
                    for u in range(CH):
                        c = CH * j + u
                        for k in range(CH):
                            last = pe.matmul(G[(j + 1) % 2][:, u, :], w[:, k, c * P:(c + 1) * P], srcT[:, k, :], start=k == 0, stop=k == CH - 1)
                    last.then_inc(done, 1)

            def scores(h):
                c, part = h // HEADS_PER_CHUNK, 32 * ((h % HEADS_PER_CHUNK) // 2)
                q = (q_even, q_odd)[h % 2]
                for r in range(CH):
                    last = pe.matmul(S[h % 2][:, r, :], q[part:part + 32, c, r * P:(r + 1) * P], kT[part:part + 32, c, :],
                                     start=True, stop=True)
                last.then_inc(scores_done, 1)

            def values(h):
                pe.wait_ge(probsT_ready, h + 1)
                for r in range(CH):
                    for k in range(CH):
                        last = pe.matmul(C[:, r, h * HD:(h + 1) * HD], probsT[:, h % RING, k, r * P:(r + 1) * P],
                                         v[:, k, h * HD:(h + 1) * HD], start=k == 0, stop=k == CH - 1)
                return last

            for h in range(HEADS):
                if attention:
                    pe.wait_ge(probs_ready, h + 1)
                    transposes(pe, T[h % 2], probs[:, h % RING, :, :]).then_inc(probsT_done, 1)
                    if h + AHEAD < HEADS:
                        scores(h + AHEAD)
                    if h >= 1:
                        values(h - 1)
                if h == 0 and front:
                    pe.wait_ge(momentsA1_ready, 1)
                    pe.matmul(F[:, 0, 0:2], mean_w[:, :], stat4[:, 0:2], start=True, stop=True).then_inc(stats1_done, 1)
                if h == 0 and tail:
                    pe.wait_ge(attn_ready, 1)
                    if not front:
                        pe.wait_ge(field_read, 1)
                    transposes(pe, G[0], attn).then_inc(attnT_done, 1)
                if h == 1 and tail:
                    pe.wait_ge(attnT_ready, 1)
                    for r in range(CH):
                        pe.matmul(G[1][:, r, :], attnT[:, 0, r * P:(r + 1) * P], w_o[:, 0, :], start=True, stop=False)
                        for c in range(CH):
                            pe.matmul(G[1][:, r, c * P:(c + 1) * P], x1T_kept_sb[:, c, r * P:(r + 1) * P], ident[:, :], start=False, stop=False)
                        last = pe.matmul(G[1][:, r, :], attnT[:, 1, r * P:(r + 1) * P], w_o[:, 1, :], start=False, stop=True)
                    last.then_inc(proj_done, 1)
                if h == 4 and tail:
                    pe.wait_ge(xn2_ready, 1)
                    transposes(pe, G[0], xn2).then_inc(hT_done, 1)
                if h == 4 and front:
                    pe.wait_ge(act1_ready, 1)
                    feature_major(pe, F, w_in, gate).then_inc(mm1_done, 1)
                if h == 5 and tail:
                    pe.wait_ge(hT_ready, 1)
                    hidden_layer(w_ff1, hT, ff1_done, ff1_ready)
                if h == 5 and front:
                    pe.wait_ge(momentsA2_ready, 1)
                    pe.matmul(F[:, 0, 0:2], mean_w[:, :], stat4[:, 2:4], start=True, stop=True).then_inc(stats2_done, 1)
                if h == 5 and tail:
                    pe.wait_ge(ff1_ready, 4)
                    row_major(pe, G[1], hidden, w_ff2, 0, FC)
                if h == 6 and tail:
                    row_major(pe, G[1], hidden, w_ff2, 1, FC).then_inc(ff2_done, 1)
                if h == 6 and front:
                    pe.wait_ge(act2_ready, 1)
                    for r in range(CH):
                        last = row_major(pe, F, gate, w_out, r, CH)
                    last.then_inc(mm2_done, 1)
                if h == 8 and tail:
                    pe.wait_ge(x3_ready, 1)
                    transposes(pe, G[0], x3).then_inc(x3T_done, 1)
                if h == 8 and front:
                    pe.wait_ge(xn_ready, 1)
                    transposes(pe, F, x0).then_inc(x1T_done, 1)
                if h == 9 and tail:
                    pe.wait_ge(x3T_ready, 1)
                    pe.wait_ge(ex1_loaded, 16)
                    hidden_layer(w_ex1, x3T, ex1_done, ex_hidden_ready)
                    pe.wait_ge(ex2_loaded, 16)
                    pe.wait_ge(ex_hidden_ready, 4)
                    row_major(pe, G[1], hidden, w_ex2, 0, FC)
                if h == 10 and tail:
                    row_major(pe, G[1], hidden, w_ex2, 1, FC).then_inc(ex2_done, 1)
            if front:
                pe.wait_ge(x1T_ready, 1)
                feature_major(pe, S[0], w_q, x1T).then_inc(q_done, 1)
                feature_major(pe, S[1], w_k, x1T).then_inc(k_done, 1)
            if attention:
                values(HEADS - 1).then_inc(attn_done, 1)
            if front:
                for r in range(CH):
                    last = row_major(pe, T[1], x1T, w_v, r, CH)
                last.then_inc(v_done, 1)
                pe.wait_ge(q_ready, 1)
                pe.wait_ge(k_ready, 1)
                for h in range(AHEAD):
                    scores(h)
            if tail:
                pe.wait_ge(inner_ready, 1)
                for r in range(CH):
                    for k in range(CH):
                        pe.matmul(G[0][:, r, :], firstT[:, k, r * P:(r + 1) * P], diff[:, 0, k, :], start=k == 0, stop=False)
                        last = pe.matmul(G[0][:, r, :], secondT[:, k, r * P:(r + 1) * P], prod[:, 6, k, :], start=False, stop=k == CH - 1)
                last.then_inc(stencil_done, 1)
            if front:
                pe.wait_ge(v_ready, 1)
            counts = []
            if front:
                counts += [(s, 1) for s in (momentsA1_ready, act1_ready, momentsA2_ready, act2_ready, xn_ready, x1T_ready, q_ready, k_ready, v_ready)]
            if attention:
                counts += [(probs_ready, HEADS), (probsT_ready, HEADS)]
            if not front:
                counts += [(field_read, 1)]
            if tail:
                counts += [(attn_ready, 1), (attnT_ready, 1), (xn2_ready, 1), (hT_ready, 1), (ff1_ready, 4), (x3_ready, 1), (x3T_ready, 1),
                           (ex1_loaded, 16), (ex2_loaded, 16), (ex_hidden_ready, 4), (inner_ready, 1)]
            settle(pe, counts)

        def scalar_body(act, front, attention, tail, first_store=False):
            def affine(dst, src, scale, shift):
                for c in range(CH):
                    last = act.activation(dst[:, c, :], src[:, c, :], ACT.Identity,
                                          bias=shift[:, c:c + 1], scale=scale[:, c:c + 1] if scale is not None else 1.0)
                return last

            def softmax(h, k):
                for r in range(CH):
                    act.wait_ge(logits_ready, CH * k + r + 1)
                    p = probs[:, h % RING, r, :]
                    last = act.activation(p, p, ACT.Exp, scale=-1.0, bias=neg_max[:, h % 2, r, h:h + 1], accum_out=denom[:, r, h:h + 1])
                    if r == 0 and h and h % HEADS_PER_GROUP == 0:
                        last.then_inc(bias_free[h // HEADS_PER_GROUP - 1], 1)
                last.then_inc(probs_ready, 1)

            for h in range(HEADS):
                if attention and h + AHEAD < HEADS:
                    softmax(h + AHEAD, h)
                if h == 0 and tail is not None:
                    act.wait_ge(attnT_done, 1)
                    act.activation(attnT[:, :, :], G[0][:, :, :], ACT.Copy).then_inc(attnT_ready, 1)
                if h == 2 and front:
                    act.wait_ge(half_ready, 1)
                    act.activation(gate[:, :, :], half_w[:, :, :], ACT.Tanh).then_inc(tanh_ready, 1)
                if h == 4 and tail is not None:
                    act.wait_ge(hT_done, 1)
                    affine(hT, G[0], cols[:, C_G2:C_G2 + CH], cols[:, C_BETA2:C_BETA2 + CH]).then_inc(hT_ready, 1)
                if h == 4 and front:
                    act.wait_ge(mm1_done, 1)
                    affine(h1, F, None, cols[:, C_BIN:C_BIN + CH]).then_inc(h1_ready, 1)
                if h == 5 and tail is not None:
                    for j in range(4):
                        act.wait_ge(ff1_done, j + 1)
                        for u in range(CH):
                            c = CH * j + u
                            last = act.activation(hidden[:, c, :], G[(j + 1) % 2][:, u, :], ACT.Gelu_apprx_sigmoid, bias=cols[:, C_FF1 + c:C_FF1 + c + 1])
                        last.then_inc(ff1_ready, 1)
                if h == 5 and front:
                    act.wait_ge(half_ready, 2)
                    act.activation(gate[:, :, :], half_w[:, :, :], ACT.Tanh).then_inc(tanh_ready, 1)
                if h == 8 and tail is not None:
                    act.wait_ge(x3T_done, 1)
                    act.activation(x3T[:, :, :], G[0][:, :, :], ACT.Copy).then_inc(x3T_ready, 1)
                if h == 8 and front:
                    act.wait_ge(x1T_done, 1)
                    if attention:
                        act.wait_ge(x1T_kept, 1)
                    affine(x1T, F, cond[:, 4:4 + CH], cond[:, 6:6 + CH]).then_inc(x1T_ready, 1)
                if h == 9 and tail is not None:
                    act.wait_ge(ex_cols_loaded, 16)
                    for j in range(4):
                        act.wait_ge(ex1_done, j + 1)
                        for u in range(CH):
                            c = CH * j + u
                            last = act.activation(hidden[:, c, :], G[(j + 1) % 2][:, u, :], ACT.Gelu, bias=ex_cols[:, c:c + 1])
                            if j == 3 and u == 0:
                                last.then_inc(ex1_free, 1)
                        last.then_inc(ex_hidden_ready, 1)
            if front:
                act.wait_ge(k_done, 1)
                affine(kT, S[1], None, cols[:, C_BK:C_BK + CH]).then_inc(k_ready, 1)
                for h in range(AHEAD):
                    softmax(h, (LATER if attention else 0) + h)
            if tail is not None:
                act.wait_ge(res_ready, 1)
                if not first_store:
                    act.wait_ge(stored, 16)
                act.activation(res[:, :, :], f_r[:, :, :], ACT.Relu)
                act.drain()
                act.dma_start(out[bass.ds(tail, 1), :, :].rearrange("a (c p) n -> p (a c) n", p=P), res[:, :, :]).then_inc(stored, 16)
            counts = [(logits_ready, CH * ((LATER if attention else 0) + (AHEAD if front else 0)))] if front or attention else []
            if front:
                counts += [(half_ready, 2), (mm1_done, 1), (x1T_done, 1), (k_done, 1)] + ([(x1T_kept, 1)] if attention else [])
            elif attention:
                act.wait_ge(x1T_kept, 1)
                counts += [(x1T_kept, 1)]
            if tail is not None:
                counts += [(attnT_done, 1), (hT_done, 1), (ff1_done, 4), (x3T_done, 1), (ex_cols_loaded, 16), (ex1_done, 4), (res_ready, 1)]
                if not first_store:
                    counts += [(stored, 16)]
            settle(act, counts)

        def vector_body(dve, front, attention, tail):
            def layer_moments(src, s6, s2, var, eps):
                for r in range(CH):
                    dve.bn_stats(out=s6[:, r, :], in_=src[:, r, :])
                dve.drain()
                for r in range(CH):
                    dve.bn_aggr(out=s2[:, r, :], in_=s6[:, r, :])
                dve.drain()
                return dve.tensor_scalar(var[:, :], s2[:, :, 1], eps, None, ALU.add)

            def normalise(dst, src, s2, rstd):
                for r in range(CH):
                    last = dve.tensor_scalar(dst[:, r, :], src[:, r, :], s2[:, r, 0:1], rstd[:, r:r + 1], ALU.subtract, ALU.mult)
                return last

            def partition_moments(src, k):
                dve.bn_stats(out=stat6[:, 0, :], in_=src[:, :, :].rearrange("p c n -> p (c n)"))
                dve.drain()
                dve.bn_aggr(out=stat2[:, 0, :], in_=stat6[:, 0, :])
                dve.drain()
                dve.tensor_copy(stat4[:, 2 * k:2 * k + 1], stat2[:, 0, 0:1])
                dve.scalar_tensor_tensor(out=stat4[:, 2 * k + 1:2 * k + 2], in0=stat2[:, 0, 0:1], scalar=stat2[:, 0, 0:1], in1=stat2[:, 0, 1:2],
                                         op0=ALU.mult, op1=ALU.add)
                return dve.drain()

            def global_variance():
                dve.tensor_copy(stat2[:, 1, :], F[:, 0, 0:2])
                dve.drain()
                dve.scalar_tensor_tensor(out=varA[:, 1:2], in0=stat2[:, 1, 0:1], scalar=stat2[:, 1, 0:1], in1=stat2[:, 1, 1:2],
                                         op0=ALU.mult, op1=ALU.subtract)
                dve.drain()
                return dve.tensor_scalar(varA[:, 0:1], varA[:, 1:2], -1.0, 1e-5, ALU.mult, ALU.add)

            def silu_argument(src, free):
                ins = dve.scalar_tensor_tensor(out=h1[:, :, :], in0=src[:, :, :], scalar=stat2[:, 1, 0:1], in1=gammaT[:, :, :],
                                               op0=ALU.subtract, op1=ALU.mult)
                if free is not None:
                    ins.then_inc(free, 1)
                dve.drain()
                dve.scalar_tensor_tensor(out=h1[:, :, :], in0=h1[:, :, :], scalar=rstdA[:, 0:1], in1=betaT[:, :, :], op0=ALU.mult, op1=ALU.add)
                dve.drain()
                for c in range(CH):
                    last = dve.tensor_scalar(half_w[:, c, :], h1[:, c, :], cond[:, c:c + 1], cond[:, 2 + c:3 + c], ALU.mult, ALU.add)
                return last

            def silu_product():
                return dve.scalar_tensor_tensor(out=gate[:, :, :], in0=gate[:, :, :], scalar=1.0, in1=half_w[:, :, :], op0=ALU.add, op1=ALU.mult)

            def logits(h, k):
                dve.wait_ge(scores_done, k + 1)
                dve.wait_ge(bias_masked, k + 1)
                for r in range(CH):
                    dve.tensor_tensor_reduce(out=probs[:, h % RING, r, :], in0=S[h % 2][:, r, :],
                                             in1=bias[:, h // HEADS_PER_GROUP, h % HEADS_PER_GROUP, r, :], scale=1.0, scalar=3.0e38,
                                             op0=ALU.add, op1=ALU.min, accum_out=neg_max[:, h % 2, r, h:h + 1]).then_inc(logits_ready, 1)

            for h in range(HEADS):
                if attention:
                    dve.wait_ge(probsT_done, h + 1)
                    dve.tensor_copy(probsT[:, h % RING, :, :], T[h % 2][:, :, :]).then_inc(probsT_ready, 1)
                    if h + AHEAD < HEADS:
                        logits(h + AHEAD, h)
                if h == 0 and front is not None:
                    dve.wait_ge(stats1_done, 1)
                    global_variance().then_inc(varA_ready, 1)
                if h == 1 and front is not None:
                    dve.wait_ge(rstdA_ready, 1)
                    silu_argument(xT, xT_free).then_inc(half_ready, 1)
                if h == 1 and tail is not None:
                    dve.wait_ge(proj_done, 1)
                    dve.tensor_tensor(out=x2[:, :, :], in0=G[1][:, :, :], in1=rows[:, B_O:B_O + 1, :].to_broadcast([P, CH, DIM]), op=ALU.add)
                    dve.drain()
                    layer_moments(x2, statB6, statB2, varB, 1e-5).then_inc(varB_ready, 1)
                if h == 2 and tail is not None:
                    dve.wait_ge(rstdB_ready, 1)
                    normalise(xn2, x2, statB2, rstdB).then_inc(xn2_ready, 1)
                if h == 3 and front is not None:
                    dve.wait_ge(tanh_ready, 1)
                    silu_product().then_inc(act1_ready, 1)
                if h == 4 and front is not None:
                    dve.wait_ge(h1_ready, 1)
                    partition_moments(h1, 1).then_inc(momentsA2_ready, 1)
                if h == 5 and front is not None:
                    dve.wait_ge(stats2_done, 1)
                    global_variance().then_inc(varA_ready, 1)
                    dve.wait_ge(rstdA_ready, 2)
                    silu_argument(h1, None).then_inc(half_ready, 1)
                    dve.wait_ge(tanh_ready, 2)
                    silu_product().then_inc(act2_ready, 1)
                if h == 6 and tail is not None:
                    dve.wait_ge(ff2_done, 1)
                    dve.wait_ge(x2_bias_ready, 1)
                    dve.tensor_tensor(out=x3[:, :, :], in0=G[1][:, :, :], in1=x2_bias[:, :, :], op=ALU.add).then_inc(x3_ready, 1)
                    dve.drain().then_inc(x3_for_bias, 1)
                if h == 6 and front is not None:
                    dve.wait_ge(mm2_done, 1)
                    dve.wait_ge(x_bias_ready, 1)
                    dve.tensor_tensor(out=x0[:, :, :], in0=F[:, :, :], in1=x_bias[:, :, :], op=ALU.add)
                    dve.drain()
                    layer_moments(x0, stat6, stat2, varA, 1e-5).then_inc(varA_ready, 1)
                if h == 7 and front is not None:
                    dve.wait_ge(rstdA_ready, 3)
                    normalise(x0, x0, stat2, rstdA).then_inc(xn_ready, 1)
                if h == 10 and tail is not None:
                    dve.wait_ge(ex2_done, 1)
                    dve.wait_ge(x3_bias_ready, 1)
                    dve.tensor_tensor(out=y[:, :, :], in0=G[1][:, :, :], in1=x3_bias[:, :, :], op=ALU.add).then_inc(ex2_free, 1)
                    dve.drain()
                    layer_moments(y, statB6, statB2, varB, 1e-12).then_inc(varB_ready, 1)
                if h == 11 and tail is not None:
                    dve.wait_ge(rstdB_ready, 2)
                    normalise(y, y, statB2, rstdB).then_inc(y_ready, 1)
                if h == 13 and tail is not None:
                    dve.wait_ge(f_ready, 1)
                    for a in range(2):
                        for side in range(2):
                            lo = (DIM - 4) * side
                            dve.tensor_tensor(out=edge[:, a, :, side, :], in0=f[:, :, lo:lo + 4], in1=edge_coef[:, a, :, side, :], op=ALU.mult)
                    dve.drain()
                    dst = diff[:, :, :, :].rearrange("p a c n -> p (a c) n")[:, :, 0:DIM:DIM - 1]
                    dve.tensor_reduce(out=dst, in_=edge[:, :, :, :, :].rearrange("p a c s j -> p (a c) s j"), axis=AX.X, op=ALU.add).then_inc(edges_ready, 1)
            if front is not None:
                dve.wait_ge(q_done, 1)
                for a, q in enumerate((q_even, q_odd)):
                    for c in range(CH):
                        last = dve.tensor_scalar(q[:, c, :], S[0][:, c, :], q_cols[:, a, 0:1], q_cols[:, a, 1 + c:2 + c], ALU.mult, ALU.add)
                last.then_inc(q_ready, 1)
            if attention:
                dve.wait_ge(attn_done, 1)
                dve.reciprocal(inv[:, :, :], denom[:, :, :]).then_inc(bias_free[GROUPS - 1], 1)
                dve.drain()
                dve.tensor_tensor(out=attn[:, :, :].rearrange("p c (h e) -> p (c h) e", e=HD), in0=C[:, :, :].rearrange("p c (h e) -> p (c h) e", e=HD),
                                  in1=inv[:, :, :].rearrange("p c (h e) -> p (c h) e", e=1).to_broadcast([P, CH * HEADS, HD]), op=ALU.mult)\
                    .then_inc(attn_ready, 1)
            if front is not None:
                dve.wait_ge(v_done, 1)
                dve.tensor_tensor(out=v[:, :, :], in0=T[1][:, :, :], in1=rows[:, B_V:B_V + 1, :].to_broadcast([P, CH, DIM]), op=ALU.add)\
                    .then_inc(v_ready, 1)
                for h in range(AHEAD):
                    logits(h, (LATER if attention else 0) + h)
            if tail is not None:
                dve.tensor_copy(dt[:, :], dt_all[:, bass.ds(tail, 1)])
                dve.drain()
                dve.wait_ge(terms_ready, 1)
                dve.scalar_tensor_tensor(out=y[:, :, :], in0=diff[:, 1, :, :], scalar=dt[:, 0:1], in1=f[:, :, :], op0=ALU.mult, op1=ALU.add)
                dve.drain()
                dve.wait_ge(stencil_done, 1)
                dve.scalar_tensor_tensor(out=f_r[:, :, :], in0=G[0][:, :, :], scalar=dt[:, 0:1], in1=y[:, :, :], op0=ALU.mult, op1=ALU.add)\
                    .then_inc(res_ready, 1)
            counts = [(s, (LATER if attention else 0) + (AHEAD if front is not None else 0)) for s in (scores_done, bias_masked)] \
                if attention or front is not None else []
            if front is not None:
                counts += [(xT_loaded, 16), (stats1_done, 1), (rstdA_ready, 3), (tanh_ready, 2), (h1_ready, 1), (stats2_done, 1), (mm2_done, 1),
                           (x_bias_ready, 1), (q_done, 1), (v_done, 1)]
            if attention:
                counts += [(probsT_done, HEADS), (attn_done, 1)]
            if tail is not None:
                counts += [(proj_done, 1), (rstdB_ready, 2), (ff2_done, 1), (x2_bias_ready, 1), (ex2_done, 1), (x3_bias_ready, 1), (f_ready, 1),
                           (terms_ready, 1), (stencil_done, 1)]
            settle(dve, counts)

        def vector_iteration(dve, front, attention, tail):
            if front is not None:
                dve.tensor_copy(cond[:, :], cond_all[:, bass.ds(front, 1), :].rearrange("p a n -> p (a n)"))
                dve.wait_ge(xT_loaded, 16)
                dve.bn_stats(out=stat6[:, 0, :], in_=xT[:, :, :].rearrange("p c n -> p (c n)"))
                dve.drain()
                dve.bn_aggr(out=stat2[:, 0, :], in_=stat6[:, 0, :])
                dve.drain()
                dve.tensor_copy(stat4[:, 0:1], stat2[:, 0, 0:1])
                dve.scalar_tensor_tensor(out=stat4[:, 1:2], in0=stat2[:, 0, 0:1], scalar=stat2[:, 0, 0:1], in1=stat2[:, 0, 1:2],
                                         op0=ALU.mult, op1=ALU.add)
                dve.drain().then_inc(momentsA1_ready, 1)
            else:
                dve.drain().then_inc(field_read, 1)
            vector_body(dve, front, attention, tail)

        def pool_body(pool, front, attention, tail):
            def rsqrt(var, rstd, n):
                return pool.tensor_tensor(out=rstd[:, 0:n], in0=var[:, 0:n], in1=consts[:, NEG_HALF:NEG_HALF + n], op=ALU.pow)

            def mask_bias(heads):
                for h in heads:
                    if h % HEADS_PER_GROUP == 0:
                        pool.wait_ge(bias_loaded[h // HEADS_PER_GROUP], 16)
                    t = bias[:, h // HEADS_PER_GROUP, h % HEADS_PER_GROUP, :, :]
                    pool.tensor_tensor(out=t, in0=mask_far[:, :, :], in1=t, op=ALU.subtract).then_inc(bias_masked, 1)

            def add_row(dst, src, row):
                return pool.tensor_tensor(out=dst[:, :, :], in0=src[:, :, :], in1=row.to_broadcast([P, CH, DIM]), op=ALU.add)

            if attention:
                mask_bias(range(4, 5))
            if front:
                pool.wait_ge(varA_ready, 1)
                rsqrt(varA, rstdA, 1).then_inc(rstdA_ready, 1)
            if attention:
                mask_bias(range(5, 6))
            if tail:
                pool.wait_ge(varB_ready, 1)
                rsqrt(varB, rstdB, CH).then_inc(rstdB_ready, 1)
            if attention:
                pool.tensor_copy(x1T_kept_sb[:, :, :], x1T[:, :, :]).then_inc(x1T_kept, 1)
            if tail:
                add_row(x2_bias, x2, rows[:, B_FF2:B_FF2 + 1, :]).then_inc(x2_bias_ready, 1)
            if attention:
                mask_bias(range(6, 9))
            if front:
                pool.wait_ge(x_loaded, 16)
                add_row(x_bias, x, rows[:, B_OUT:B_OUT + 1, :]).then_inc(x_bias_ready, 1)
                pool.drain().then_inc(x_free, 1)
                pool.wait_ge(varA_ready, 2)
                rsqrt(varA, rstdA, 1).then_inc(rstdA_ready, 1)
            if attention:
                mask_bias(range(9, 11))
            if tail:
                pool.wait_ge(x3_for_bias, 1)
                pool.wait_ge(ex_rows_loaded, 16)
                add_row(x3_bias, x3, ex_rows[:, 0:1, :]).then_inc(x3_bias_ready, 1)
            if front:
                pool.wait_ge(varA_ready, 3)
                rsqrt(varA, rstdA, CH).then_inc(rstdA_ready, 1)
            if attention:
                mask_bias(range(11, HEADS))
            if front:
                pool.wait_ge(mask_loaded, 16)
                pool.drain()
                pool.tensor_scalar(mask_far[:, :, :], mask_u8[:, :, :], 1.0e38, 1.0, ALU.mult, ALU.mult).then_inc(mask_free, 1)
                pool.drain()
                mask_bias(range(1))
            if tail:
                pool.wait_ge(varB_ready, 2)
                rsqrt(varB, rstdB, CH).then_inc(rstdB_ready, 1)
            if front:
                mask_bias(range(1, 4))
            if tail:
                pool.wait_ge(y_ready, 1)
                pool.tensor_tensor(out=f[:, :, :], in0=y[:, :, :], in1=ex_rows[:, 1:2, :].to_broadcast([P, CH, DIM]), op=ALU.mult)
                pool.drain()
                add_row(f, f, ex_rows[:, 2:3, :]).then_inc(f_ready, 1)
                pool.drain().then_inc(ex_small_free, 1)
                for a in (0, 2, 4, 6):
                    pool.tensor_tensor(out=prod[:, a, :, :], in0=coef[:, a, :, :], in1=f[:, :, :], op=ALU.mult)
                pool.drain()
                pool.tensor_tensor(out=diff[:, 0, :, 1:DIM - 1], in0=prod[:, 0, :, 2:DIM], in1=prod[:, 2, :, 0:DIM - 2], op=ALU.add)
                pool.drain()
                pool.wait_ge(edges_ready, 1)
                pool.tensor_tensor(out=diff[:, 0, :, :], in0=diff[:, 0, :, :], in1=prod[:, 4, :, :], op=ALU.subtract).then_inc(inner_ready, 1)
                for a in (1, 3, 5):
                    pool.tensor_tensor(out=prod[:, a, :, :], in0=coef[:, a, :, :], in1=f[:, :, :], op=ALU.mult)
                pool.drain()
                pool.tensor_tensor(out=diff[:, 1, :, 1:DIM - 1], in0=prod[:, 1, :, 2:DIM], in1=prod[:, 3, :, 0:DIM - 2], op=ALU.add)
                pool.drain()
                pool.tensor_tensor(out=diff[:, 1, :, :], in0=diff[:, 1, :, :], in1=prod[:, 5, :, :], op=ALU.subtract).then_inc(terms_ready, 1)
            counts = []
            if front:
                counts += [(mask_loaded, 16), (x_loaded, 16), (varA_ready, 3), (bias_loaded[0], 16)]
            if attention:
                counts += [(s, 16) for s in bias_loaded[1:]]
            if tail:
                counts += [(varB_ready, 2), (x3_for_bias, 1), (ex_rows_loaded, 16), (y_ready, 1), (edges_ready, 1)]
            settle(pool, counts)

        def program(eng, body, **first):
            body(eng, 0, None, None)
            body(eng, 1, 0, None)
            body(eng, 2, 1, 0, **first)
            with eng.Fori(2, BATCHES - 1) as i:
                body(eng, i + 1, i, i - 1)
            body(eng, None, BATCHES - 1, BATCHES - 2)
            body(eng, None, None, BATCHES - 1)

        def flags(body):
            return lambda eng, front, attention, tail: body(eng, front is not None, attention is not None, tail is not None)

        with nc.Block() as block:
            @block.sync
            def _(sp):
                program(sp, sync_body)

            @block.tensor
            def _(pe):
                program(pe, flags(tensor_body))

            @block.scalar
            def _(act):
                program(act, lambda eng, f_, a_, t_, first_store=False: scalar_body(eng, f_ is not None, a_ is not None, t_, first_store),
                        first_store=True)
                act.wait_ge(stored, 16)

            @block.vector
            def _(dve):
                program(dve, lambda eng, f_, a_, t_: vector_iteration(eng, f_, a_ is not None, t_))

            @block.gpsimd
            def _(pool):
                program(pool, flags(pool_body))


def columns(v):
    return np.asarray(v).reshape(-1, P).T


def kernel(**inputs):
    import concourse.bacc as _bacc
    from concourse import mybir as _mybir
    from concourse.bass_utils import run_bass_kernel_spmd as _run

    g = {k: np.asarray(a) for k, a in inputs.items()}
    f0 = np.exp(np.arange(NOISE // 2, dtype=np.float32) * np.float32(-math.log(10000.0) / (NOISE // 2 - 1)))
    f1 = np.exp(np.arange(DIM // 2, dtype=np.float32) * np.float32(-math.log(10000.0) / (DIM // 2 - 1)))
    p = np.arange(P)
    phase0 = np.where(p < NOISE // 2, 0.0, 0.25).astype(np.float32)
    even = np.where((p // HD) % 2 == 0, -1.0 / math.sqrt(HD), 0.0).astype(np.float32)
    odd = np.where((p // HD) % 2 == 1, -1.0 / math.sqrt(HD), 0.0).astype(np.float32)
    zero, quarter = np.zeros(P, np.float32), np.full(P, 0.25, np.float32)
    turn = np.float32(TWO_PI)
    tables = np.stack([np.concatenate([f0, f0]), f1, even, odd, phase0, zero, quarter, phase0 * turn, zero, quarter * turn], axis=1)
    cols = np.concatenate([columns(g[n]) for n in (
        "L0_cond_b_in", "L1_cond_bk", "L1_cond_g2", "L1_cond_beta2", "L1_cond_bq", "L1_cond_b1", "L0_cond_b1", "L0_cond_b2",
        "L0_cond_bsc", "L0_cond_bsh", "L1_cond_b_ada")] + [tables], axis=1)
    first, second = stencil_matrices()
    arrays = {
        "x": g["x"], "xT": g["x"].transpose(0, 2, 1),
        "mask": g["mask_Bx1xSxS_bk0"].reshape(BATCHES, SEQ, SEQ),
        "fside": g["fside_Bx16xSxS_0"].reshape(BATCHES, GROUPS, HEADS_PER_GROUP, CH, P, SEQ).transpose(0, 1, 4, 2, 3, 5)
        .reshape(BATCHES, GROUPS, P, HEADS_PER_GROUP * CH * SEQ),
        "cols": cols, "gammaT": g["L0_cond_gamma"].T, "betaT": g["L0_cond_beta"].T, "firstT": first.T, "secondT": second.T,
        "ex_bi": g["L2_cond_bi"].reshape(EXPERTS, FC, P).transpose(0, 2, 1),
        "ex_rows": np.concatenate([g["L2_cond_bo"], g["L2_cond_gamma"], g["L2_cond_beta"]], axis=1),
    }
    for n in ("condB_t", "condB_dt", "itok_B_34_63", "itok_B_0_7", "L0_cond_W1", "L0_cond_W2", "L0_cond_Wsc", "L0_cond_Wsh", "L0_cond_W_in",
              "L0_cond_W_out", "L0_cond_b_out", "L1_cond_W_ada", "L1_cond_Wq", "L1_cond_Wk", "L1_cond_Wv", "L1_cond_Wo", "L1_cond_bv",
              "L1_cond_bo", "L1_cond_W1", "L1_cond_W2", "L1_cond_b2", "L2_cond_Wi", "L2_cond_Wo", "L3_cond_A_grid", "L3_cond_B_grid"):
        arrays[n] = g[n]
    nc = _bacc.Bacc("TRN2", target_bir_lowering=False, num_devices=1)
    sent, d = {}, {}
    for n, a in arrays.items():
        a = np.ascontiguousarray(a)
        sent[f"in_{n}"] = a
        d[n] = nc.dram_tensor(f"in_{n}", a.shape, _mybir.dt.from_np(a.dtype), kind="ExternalInput").ap()
    out = nc.dram_tensor("out", (BATCHES, SEQ, DIM), _mybir.dt.float32, kind="ExternalOutput").ap()
    build_program(nc, d, out)
    r = _run(nc, [sent], core_ids=[0])
    return r.results[0]["out"]
```

```python
import math
from contextlib import ExitStack

import concourse.bass as bass
import numpy as np
from concourse import mybir

BATCHES, SEQ, DIM, HEADS, FF, EXPERTS = 32, 256, 256, 16, 1024, 8
NOISE = 128
P = 128
HD = DIM // HEADS
CH = DIM // P
FC = FF // P
HEADS_PER_GROUP = 4
GROUPS = HEADS // HEADS_PER_GROUP
RING = 3
BIAS_BUFFERS = 2
COEFS = K_MIXED, K_RIGHT, K_LEFT, K_ROW, K_MIDDLE, K_SECOND = range(6)
PARTS = 2
PROBS_T = 6
TWO_PI = 2.0 * math.pi
ROUND = 12582912.0
COND = 4 * CH


def stencil_matrices():
    first = np.zeros((SEQ, SEQ), np.float32)
    second = np.zeros((SEQ, SEQ), np.float32)
    for i in range(1, SEQ - 1):
        first[i, i - 1], first[i, i + 1] = -0.5, 0.5
        second[i, i - 1], second[i, i], second[i, i + 1] = 1.0, -2.0, 1.0
    first[0, :3] = (-1.5, 2.0, -0.5)
    first[-1, -3:] = (0.5, -2.0, 1.5)
    second[0, :4] = (2.0, -5.0, 4.0, -1.0)
    second[-1, -4:] = (-1.0, 4.0, -5.0, 2.0)
    return first, second


def build_program(nc, d, out):
    f32, f32r, i32, u8 = mybir.dt.float32, mybir.dt.float32r, mybir.dt.int32, mybir.dt.uint8
    ALU, ACT, AX = mybir.AluOpType, mybir.ActivationFunctionType, mybir.AxisListType

    ctx = ExitStack()
    with ctx:
        def sb(name, shape, dt=f32):
            return ctx.enter_context(nc.sbuf_tensor(name, [P] + shape, dt))

        def bank(name):
            return ctx.enter_context(nc.psum_tensor(name, [P, CH, DIM], f32))

        def sem(name):
            return ctx.enter_context(nc.semaphore(name))

        w_in, w_out = sb("w_in", [CH, DIM]), sb("w_out", [CH, DIM])
        w_q, w_k, w_v = (sb(n, [CH, DIM]) for n in ("w_q", "w_k", "w_v"))
        w_o = sb("w_o", [GROUPS, DIM])
        select = sb("select", [4, 4, P], f32r)
        w_ff1, w_ff2 = sb("w_ff1", [CH, FF]), sb("w_ff2", [FC, DIM])
        w_ex1, w_ex2 = sb("w_ex1", [CH, FF]), sb("w_ex2", [FC, DIM])
        gammaT, betaT = sb("gammaT", [CH, SEQ]), sb("betaT", [CH, SEQ])
        coef = sb("coef", [len(COEFS), CH, DIM])
        edge_coef = sb("edge_coef", [2, CH, 2, 4])
        firstT, secondT = sb("firstT", [CH, SEQ]), sb("secondT", [CH, SEQ])
        ident, mean_w = sb("ident", [P]), sb("mean_w", [P])
        rows = sb("rows", [4, DIM])
        cols = sb("cols", [42])
        consts = sb("consts", [16])
        q_cols = sb("q_cols", [CH])
        ex_rows, ex_cols = sb("ex_rows", [3, DIM]), sb("ex_cols", [FC])
        cond_all, cond = sb("cond_all", [BATCHES, COND]), sb("cond", [COND])
        dt_all, dt = sb("dt_all", [BATCHES]), sb("dt", [1])
        expert = ctx.enter_context(nc.sbuf_tensor("expert", [1, BATCHES], i32))
        B_OUT, B_V, B_O, B_FF2 = range(4)
        C_BIN, C_BK, C_G2, C_BETA2, C_BQ, C_FF1 = 0, 2, 4, 6, 8, 10
        C_B1, C_B2, C_BSC, C_BSH, C_ADA = 18, 22, 26, 28, 30
        C_FREQ0, C_FREQ1, C_PHASE = 34, 35, 36
        NEG_HALF = 0

        xT, mask_u8 = sb("xT", [CH, SEQ]), sb("mask_u8", [CH, SEQ], u8)
        bias = sb("bias", [BIAS_BUFFERS, HEADS_PER_GROUP, CH, SEQ])
        stat6, stat2, stat4 = sb("stat6", [CH, 6]), sb("stat2", [CH, 2]), sb("stat4", [4])
        varA, rstdA = sb("varA", [CH]), sb("rstdA", [CH])
        half_w, gate = sb("half_w", [CH, SEQ]), sb("gate", [CH, SEQ])
        h1 = sb("h1", [CH, SEQ])
        mask_far = sb("mask_far", [CH, SEQ])
        x0 = sb("x0", [CH, DIM])
        x, x_bias = x0, x0
        x1T, x1T_copy = sb("x1T", [CH, SEQ]), half_w
        q_stack, k_stack = sb("q_stack", [HEADS // 2, SEQ], f32r), sb("k_stack", [HEADS // 2, SEQ], f32r)
        v_next, v = h1, sb("v", [CH, DIM + HD])
        probs, probsT = sb("probs", [RING, CH, SEQ]), sb("probsT", [PROBS_T, CH, SEQ])
        neg_max, denom, inv = sb("neg_max", [2, CH, HEADS]), sb("denom", [CH, HEADS]), sb("inv", [CH, HEADS])
        attnT = sb("attnT", [GROUPS, SEQ])
        statB6, statB2 = sb("statB6", [CH, 6]), sb("statB2", [CH, 2])
        varB, rstdB = sb("varB", [CH]), sb("rstdB", [CH])
        x2_bias, xn2, hT = sb("x2_bias", [CH, DIM]), sb("xn2", [CH, DIM]), sb("hT", [CH, SEQ])
        hidden = sb("hidden", [FC, SEQ])
        x2, x3, x3_bias, x3T = gate, xn2, x2_bias, hT
        y = sb("y", [CH, DIM])
        f, field = y, h1
        q_parts, k_parts = sb("q_parts", [PARTS, CH, SEQ], f32r), sb("k_parts", [PARTS, CH, SEQ], f32r)
        prod = sb("prod", [3, CH, DIM])
        diff = sb("diff", [2, CH, DIM])
        edge = sb("edge", [2, CH, 2, 4])
        res = sb("res", [CH, DIM])

        S = [bank("S0"), bank("S1")]
        T = [bank("T0"), bank("T1")]
        C = bank("C")
        G = [bank("G0"), bank("G1")]
        F = bank("F")
        HIDDEN_BANKS = G[1], G[0], F

        stage = bias[:, :, :, :, :].rearrange("p a b c n -> p (a b c n)")
        s_w1, s_ada = stage[:, 0:512], stage[:, 512:1536].rearrange("p (c n) -> p c n", c=2)
        grids = stage[:, 1536:4096].rearrange("p (a c n) -> p a c n", a=5, c=CH)
        s_w2 = w_ex1[:, :, :].rearrange("p a n -> p (a n)").rearrange("p (c n) -> p c n", c=4)
        s_wsc, s_wsh = (w_ex2[:, i:i + 4, :] for i in (0, 4))
        s_select = hidden[:, :, :].rearrange("p c n -> p (c n)")
        ang = half_w[:, :, :].rearrange("p c (a n) -> p (c a) n", n=BATCHES)
        emb = gate[:, :, :].rearrange("p c (a n) -> p (c a) n", n=BATCHES)
        hid = h1[:, :, :].rearrange("p c (a n) -> p (c a) n", n=BATCHES)
        t_f = x0[:, 0, 0:3 * BATCHES].rearrange("p (a n) -> p a n", n=BATCHES)
        t_i = ctx.enter_context(nc.sbuf_tensor("t_i", [P, BATCHES], i32))

        weights_loaded, cond_loaded, expert_loaded = sem("weights_loaded"), sem("cond_loaded"), sem("expert_loaded")
        select_loaded, w_q_loaded, v_end_cleared = sem("select_loaded"), sem("w_q_loaded"), sem("v_end_cleared")
        ident_zeroed, tables_made, edges_cleared = sem("ident_zeroed"), sem("tables_made"), sem("edges_cleared")
        angles_ready, sines_ready, emb_ready = sem("angles_ready"), sem("sines_ready"), sem("emb_ready")
        mlp_mm, mlp_act = sem("mlp_mm"), sem("mlp_act")
        silu_half, silu_tanh = sem("silu_half"), sem("silu_tanh")
        ex1_free, ex2_free, ex_small_free = sem("ex1_free"), sem("ex2_free"), sem("ex_small_free")

        weight_loads = [
            (w_in, "L0_cond_W_in"), (w_out, "L0_cond_W_out"), (w_k, "L1_cond_Wk"),
            (w_v, "L1_cond_Wv"), (w_o, "Wo_spaced"), (w_ff1, "L1_cond_W1"), (w_ff2, "L1_cond_W2"),
            (gammaT, "gammaT"), (betaT, "betaT"), (firstT, "firstT"), (secondT, "secondT"),
        ]
        stage_loads = [(s_w2, "L0_cond_W2"), (s_wsc, "L0_cond_Wsc"), (s_wsh, "L0_cond_Wsh"), (s_ada, "L1_cond_W_ada")]

        with nc.Block() as block:
            @block.sync
            def _(sp):
                sp.dma_start(cols[:, :], d["cols"]).then_inc(cond_loaded, 16)
                sp.dma_start(t_f[:, 0, :], d["condB_t"].rearrange("(a n) -> a n", a=1).to_broadcast([P, BATCHES])).then_inc(cond_loaded, 16)
                sp.dma_start(t_i[:, :], d["itok_B_34_63"].rearrange("(a n) -> a n", a=1).to_broadcast([P, BATCHES])).then_inc(cond_loaded, 16)
                sp.dma_start(dt_all[:, :], d["condB_dt"].rearrange("(a n) -> a n", a=1).to_broadcast([P, BATCHES])).then_inc(cond_loaded, 16)
                sp.dma_start(s_w1, d["L0_cond_W1"]).then_inc(cond_loaded, 16)
                sp.dma_start(s_select, d["select"]).then_inc(select_loaded, 16)
                for dst, name in stage_loads:
                    sp.dma_start(dst, d[name].rearrange("(c p) n -> p c n", p=P)).then_inc(cond_loaded, 16)
                for a in range(2):
                    sp.dma_start(grids[:, a, :, :], d["L3_cond_A_grid"][a, :, :].rearrange("(c p) n -> p c n", p=P)).then_inc(cond_loaded, 16)
                for a in range(3):
                    sp.dma_start(grids[:, 2 + a, :, :], d["L3_cond_B_grid"][a, :, :].rearrange("(c p) n -> p c n", p=P)).then_inc(cond_loaded, 16)
                sp.dma_start(w_q[:, :, :], d["L1_cond_Wq"].rearrange("(c p) n -> p c n", p=P)).then_inc(w_q_loaded, 16)
                for dst, name in weight_loads:
                    sp.dma_start(dst[:, :, :], d[name].rearrange("(c p) n -> p c n", p=P)).then_inc(weights_loaded, 16)
                for a, name in enumerate(("L0_cond_b_out", "L1_cond_bv", "L1_cond_bo", "L1_cond_b2")):
                    sp.dma_start(rows[:, a, :], d[name].rearrange("(a n) -> a n", a=1).to_broadcast([P, DIM])).then_inc(weights_loaded, 16)
                sp.dma_start(expert[:, :], d["itok_B_0_7"].rearrange("(a n) -> a n", a=1)).then_inc(expert_loaded, 16)
                sp.wait_ge(expert_loaded, 16)
                sp.wait_ge(weights_loaded, 16 * (len(weight_loads) + 4))

            @block.gpsimd
            def _(pool):
                pool.memset(ident[:, :], 0.0).then_inc(ident_zeroed, 1)
                pool.memset(mean_w[:, :], 1.0 / P).then_inc(tables_made, 1)
                pool.memset(consts[:, 0:4], -0.5).then_inc(ex1_free, 1)
                pool.memset(consts[:, 4:8], -0.5).then_inc(ex2_free, 1)
                pool.memset(consts[:, 8:16], -0.5).then_inc(ex_small_free, 1)
                pool.memset(edge_coef[:, :, :, :, :], 0.0).then_inc(edges_cleared, 1)
                pool.memset(v[:, :, DIM:DIM + HD], 0.0).then_inc(v_end_cleared, 1)
                pool.wait_ge(ident_zeroed, 1)
                pool.affine_select(out=ident[:, :], in_=ident[:, :], compare_op=ALU.not_equal, fill=1.0,
                                   base=0, pattern=[[-1, P]], channel_multiplier=1).then_inc(tables_made, 1)

            @block.vector
            def _(dve):
                dve.wait_ge(cond_loaded, 16 * 14)
                dve.tensor_copy(t_f[:, 1, :], t_i[:, :])
                dve.tensor_scalar(ang[:, 0, :], t_f[:, 0, :], 5000.0, cols[:, C_FREQ0:C_FREQ0 + 1], ALU.mult, ALU.mult)
                dve.drain()
                dve.tensor_scalar(t_f[:, 2, :], t_f[:, 1, :], 0.01, 4000.0, ALU.mult, ALU.mult)
                dve.drain()
                for a in (1, 2):
                    dve.tensor_scalar(ang[:, a, :], t_f[:, 2, :], cols[:, C_FREQ1:C_FREQ1 + 1], None, ALU.mult)
                dve.drain()
                for a in range(3):
                    dve.tensor_scalar(ang[:, 3 + a, :], ang[:, a, :], 1.0 / TWO_PI, cols[:, C_PHASE + a:C_PHASE + a + 1], ALU.mult, ALU.add)
                dve.drain()
                dve.tensor_scalar(ang[:, 6:9, :], ang[:, 3:6, :], ROUND, None, ALU.add)
                dve.drain()
                dve.tensor_scalar(ang[:, 3:6, :], ang[:, 6:9, :], -ROUND, None, ALU.add)
                hi = 6.28125
                mid = float(np.float32(np.round((TWO_PI - hi) * 2 ** 21) / 2 ** 21))
                lo = TWO_PI - hi - mid
                for part in (hi, mid, lo):
                    dve.drain()
                    dve.scalar_tensor_tensor(out=ang[:, 0:3, :], in0=ang[:, 3:6, :], scalar=-part, in1=ang[:, 0:3, :], op0=ALU.mult, op1=ALU.add)
                dve.drain()
                for a in range(3):
                    dve.tensor_scalar(ang[:, 9 + a, :], ang[:, a, :], cols[:, C_PHASE + 3 + a:C_PHASE + 4 + a], None, ALU.add)
                dve.drain()
                dve.tensor_scalar(ang[:, 12:15, :], ang[:, 9:12, :], 3.1415925, -3.1415925, ALU.min, ALU.max).then_inc(angles_ready, 1)
                dve.wait_ge(sines_ready, 1)
                dve.tensor_scalar(emb[:, 3:5, :], emb[:, 1:3, :], 0.5, None, ALU.mult).then_inc(silu_half, 1)
                dve.wait_ge(silu_tanh, 1)
                dve.scalar_tensor_tensor(out=emb[:, 1:3, :], in0=emb[:, 5:7, :], scalar=1.0, in1=emb[:, 3:5, :], op0=ALU.add, op1=ALU.mult).then_inc(emb_ready, 1)
                dve.wait_ge(mlp_mm, 1)
                for c in range(4):
                    dve.tensor_scalar(hid[:, c, :], G[0][:, 0, c * BATCHES:(c + 1) * BATCHES], cols[:, C_B1 + c:C_B1 + c + 1], 0.5, ALU.add, ALU.mult)
                dve.drain().then_inc(silu_half, 1)
                dve.wait_ge(silu_tanh, 2)
                dve.scalar_tensor_tensor(out=hid[:, 8:12, :], in0=hid[:, 4:8, :], scalar=1.0, in1=hid[:, 0:4, :], op0=ALU.add, op1=ALU.mult).then_inc(mlp_act, 1)
                dve.wait_ge(mlp_mm, 2)
                for c in range(4):
                    dve.tensor_scalar(hid[:, 12 + c, :], G[1][:, 0, c * BATCHES:(c + 1) * BATCHES], cols[:, C_B2 + c:C_B2 + c + 1], None, ALU.add)
                dve.drain().then_inc(mlp_act, 1)
                dve.wait_ge(mlp_mm, 3)
                for c in range(4):
                    dve.tensor_scalar(cond_all[:, :, c], F[:, 0, c * BATCHES:(c + 1) * BATCHES], cols[:, C_BSC + c:C_BSC + c + 1], 0.5, ALU.add, ALU.mult)
                for c in range(4):
                    dve.tensor_scalar(cond_all[:, :, 4 + c], F[:, 1, c * BATCHES:(c + 1) * BATCHES], cols[:, C_ADA + c:C_ADA + c + 1],
                                      1.0 if c < 2 else 0.0, ALU.add, ALU.add)
                dve.wait_ge(w_q_loaded, 16)
                dve.tensor_scalar(w_q[:, :, :], w_q[:, :, :], -1.0 / math.sqrt(HD), None, ALU.mult)
                dve.tensor_scalar(q_cols[:, :], cols[:, C_BQ:C_BQ + CH], -1.0 / math.sqrt(HD), None, ALU.mult)
                A0, A1, B0, B1, B2 = (grids[:, a, :, :] for a in range(5))
                dve.tensor_scalar(coef[:, K_MIXED, :, :], B2, 0.5, None, ALU.mult)
                dve.tensor_copy(coef[:, K_ROW, :, :], A0)
                dve.tensor_copy(coef[:, K_MIDDLE, :, :], B1)
                dve.tensor_scalar(coef[:, K_SECOND, :, :], B0, 0.5, None, ALU.mult)
                dve.tensor_scalar(prod[:, 0, :, :], A1, 0.5, None, ALU.mult)
                dve.tensor_scalar(prod[:, 1, :, :], B1, 0.5, None, ALU.mult)
                dve.drain()
                dve.tensor_tensor(out=coef[:, K_RIGHT, :, :], in0=prod[:, 1, :, :], in1=prod[:, 0, :, :], op=ALU.subtract)
                dve.tensor_tensor(out=coef[:, K_LEFT, :, :], in0=prod[:, 1, :, :], in1=prod[:, 0, :, :], op=ALU.add)
                N = DIM
                ec = edge_coef
                dve.wait_ge(edges_cleared, 1)
                for side, j, k in ((0, 0, -1.5), (0, 1, 2.0), (0, 2, -0.5), (1, 1, 0.5), (1, 2, -2.0), (1, 3, 1.5)):
                    col = j + (N - 4) * side
                    dve.tensor_scalar(ec[:, 0, :, side, j], B2[:, :, col], k, None, ALU.mult)
                for side, j, kb, ka in ((0, 0, 2.0, 1.5), (0, 1, -2.5, -2.0), (0, 2, 2.0, 0.5), (0, 3, -0.5, 0.0),
                                        (1, 0, -0.5, 0.0), (1, 1, 2.0, -0.5), (1, 2, -2.5, 2.0), (1, 3, 2.0, -1.5)):
                    col = j + (N - 4) * side
                    dve.tensor_scalar(edge[:, 0, :, side, j], A1[:, :, col], ka, None, ALU.mult)
                    dve.tensor_scalar(edge[:, 1, :, side, j], B1[:, :, col], kb, None, ALU.mult)
                dve.drain()
                dve.tensor_tensor(out=ec[:, 1, :, :, :], in0=edge[:, 0, :, :, :], in1=edge[:, 1, :, :, :], op=ALU.add)

            @block.scalar
            def _(act):
                act.wait_ge(angles_ready, 1)
                act.activation(emb[:, 0:3, :], ang[:, 12:15, :], ACT.Sin).then_inc(sines_ready, 1)
                act.wait_ge(select_loaded, 16)
                act.activation(select[:, :, :, :].rearrange("p a i n -> p (a i n)"), s_select, ACT.Copy)
                act.wait_ge(silu_half, 1)
                act.activation(emb[:, 5:7, :], emb[:, 3:5, :], ACT.Tanh).then_inc(silu_tanh, 1)
                act.wait_ge(silu_half, 2)
                act.activation(hid[:, 4:8, :], hid[:, 0:4, :], ACT.Tanh).then_inc(silu_tanh, 1)

            @block.tensor
            def _(pe):
                pe.wait_ge(cond_loaded, 16 * 14)
                pe.wait_ge(emb_ready, 1)
                for c in range(4):
                    last = pe.matmul(G[0][:, 0, c * BATCHES:(c + 1) * BATCHES], s_w1[:, c * P:(c + 1) * P], emb[:, 0, :], start=True, stop=True)
                last.then_inc(mlp_mm, 1)
                for c in range(4):
                    for k in range(2):
                        pe.matmul(F[:, 1, c * BATCHES:(c + 1) * BATCHES], s_ada[:, k, c * P:(c + 1) * P], emb[:, 1 + k, :], start=k == 0, stop=k == 1)
                pe.wait_ge(mlp_act, 1)
                for c in range(4):
                    for k in range(4):
                        last = pe.matmul(G[1][:, 0, c * BATCHES:(c + 1) * BATCHES], s_w2[:, k, c * P:(c + 1) * P], hid[:, 8 + k, :], start=k == 0, stop=k == 3)
                last.then_inc(mlp_mm, 1)
                pe.wait_ge(mlp_act, 2)
                for w, base in ((s_wsc, 0), (s_wsh, 2)):
                    for c in range(2):
                        for k in range(4):
                            last = pe.matmul(F[:, 0, (base + c) * BATCHES:(base + c + 1) * BATCHES], w[:, k, c * P:(c + 1) * P], hid[:, 12 + k, :], start=k == 0, stop=k == 3)
                last.then_inc(mlp_mm, 1)


        xT_loaded, x_loaded, mask_loaded = sem("xT_loaded"), sem("x_loaded"), sem("mask_loaded")
        bias_loaded = [sem(f"bias_loaded{g}") for g in range(GROUPS)]
        ex1_loaded, ex2_loaded, ex_rows_loaded, ex_cols_loaded = (sem(n) for n in ("ex1_loaded", "ex2_loaded", "ex_rows_loaded", "ex_cols_loaded"))
        xT_free, x_free, mask_free = sem("xT_free"), sem("x_free"), sem("mask_free")
        bias_free = [sem(f"bias_free{g}") for g in range(GROUPS)]
        stored = sem("stored")
        momentsA1_ready, momentsA2_ready, act1_ready, act2_ready, xn_ready, xn2_ready, x3_ready = (sem(n) for n in (
            "momentsA1_ready", "momentsA2_ready", "act1_ready", "act2_ready", "xn_ready", "xn2_ready", "x3_ready"))
        q_parts_ready, k_parts_ready, v_read, k_stacked, attnT_ready, expert_read = (sem(n) for n in (
            "q_parts_ready", "k_parts_ready", "v_read", "k_stacked", "attnT_ready", "expert_read"))
        probs_ready, field_read, stats_read = sem("probs_ready"), sem("field_read"), sem("stats_read")

        hT_ready, ff1_ready, x1T_ready, x3T_ready, q_stacked, ex_hidden_ready, probsT_ready, v_ready = (sem(n) for n in (
            "hT_ready", "ff1_ready", "x1T_ready", "x3T_ready", "q_stacked", "ex_hidden_ready", "probsT_ready", "v_ready"))
        stats1_done, stats2_done, proj_done, mm2_done, ff2_done, v_done = (sem(n) for n in (
            "stats1_done", "stats2_done", "proj_done", "mm2_done", "ff2_done", "v_done"))
        scores_done, k_select_done, attnT_done, ex2_done, stencil_done = (sem(n) for n in (
            "scores_done", "k_select_done", "attnT_done", "ex2_done", "stencil_done"))
        probsT_done, mm1_done, hT_done, ff1_done, x1T_done, x3T_done, qk_done, q_select_done, ex1_done = (sem(n) for n in (
            "probsT_done", "mm1_done", "hT_done", "ff1_done", "x1T_done", "x3T_done", "qk_done", "q_select_done", "ex1_done"))
        half_ready, tanh_ready, h1_ready, logits_ready, res_ready = (sem(n) for n in (
            "half_ready", "tanh_ready", "h1_ready", "logits_ready", "res_ready"))
        qk_high_ready, v_free, v_moved, exp_done = (sem(n) for n in (
            "qk_high_ready", "v_free", "v_moved", "exp_done"))
        varA_ready, rstdA_ready, varB_ready, rstdB_ready, varY_ready, rstdY_ready, x_bias_ready, x2_bias_ready = (sem(n) for n in (
            "varA_ready", "rstdA_ready", "varB_ready", "rstdB_ready", "varY_ready", "rstdY_ready", "x_bias_ready", "x2_bias_ready"))
        bias_masked, x3_for_bias, x3_bias_ready, y_ready, f_ready, edges_ready, terms_ready = (sem(n) for n in (
            "bias_masked", "x3_for_bias", "x3_bias_ready", "y_ready", "f_ready", "edges_ready", "terms_ready"))
        inner_ready, x1T_kept = sem("inner_ready"), sem("x1T_kept")

        AHEAD = 2
        LATER = HEADS - AHEAD

        def settle(eng, counts):
            for s, n in counts:
                eng.sem_inc(s, -n)

        def store(sp, b):
            sp.dma_start(out[bass.ds(b, 1), :, :].rearrange("a (c p) n -> p (a c) n", p=P), res[:, :, :]).then_inc(stored, 16)

        def sync_body(sp, front, attention, tail):
            used = []

            def reuse(s):
                sp.wait_ge(s, 1)
                used.append(s)

            def chunked(src, b):
                return d[src][bass.ds(b, 1), :, :].rearrange("a (c p) n -> p (a c) n", p=P)

            def load_bias(b, g, free):
                if free is not None:
                    reuse(bias_free[free])
                src = d["fside"][bass.ds(b, 1), g, :, :].rearrange("a p (h c n) -> p (a h) c n", h=HEADS_PER_GROUP, c=CH)
                sp.dma_start(bias[:, g % BIAS_BUFFERS, :, :, :], src).then_inc(bias_loaded[g], 16)

            later = not (isinstance(front, int) and front == 0)
            if front is not None:
                if later:
                    reuse(xT_free)
                sp.dma_start(xT[:, :, :], chunked("xT", front)).then_inc(xT_loaded, 16)
                if later:
                    reuse(x_free)
                sp.dma_start(x[:, :, :], chunked("x", front)).then_inc(x_loaded, 16)
            if tail is not None:
                sp.wait_ge(expert_loaded, 16)
                e = sp.value_load(expert[0:1, bass.ds(tail, 1)], min_val=0, max_val=EXPERTS - 1)
                one = bass.ds(e, 1)
                reuse(ex1_free)
                sp.dma_start(w_ex1[:, :, :], d["L2_cond_Wi"][one, :, :].rearrange("a (c p) n -> p (a c) n", p=P)).then_inc(ex1_loaded, 16)
                reuse(ex_small_free)
                sp.dma_start(ex_cols[:, :], d["ex_bi"][one, :, :].rearrange("a p n -> p (a n)")).then_inc(ex_cols_loaded, 16)
                sp.dma_start(ex_rows[:, :, :].rearrange("p a n -> p (a n)"),
                             d["ex_rows"][one, :].to_broadcast([P, 3 * DIM])).then_inc(ex_rows_loaded, 16)
            if tail is not None and not (isinstance(tail, int) and tail == 0):
                reuse(res_ready)
                store(sp, tail - 1)
            if attention is not None:
                load_bias(attention, 2, 0)
            if tail is not None:
                reuse(ex2_free)
                sp.dma_start(w_ex2[:, :, :], d["L2_cond_Wo"][one, :, :].rearrange("a (c p) n -> p (a c) n", p=P)).then_inc(ex2_loaded, 16)
            if front is not None:
                if later:
                    reuse(mask_free)
                sp.dma_start(mask_u8[:, :, :], chunked("mask", front)).then_inc(mask_loaded, 16)
            if attention is not None:
                load_bias(attention, 3, 1)
            if front is not None:
                for g in range(BIAS_BUFFERS):
                    load_bias(front, g, g + 2 if attention is not None else None)
            if used:
                settle(sp, [(s, 1) for s in used])

        def transposes(pe, dst, src):
            for c in range(CH):
                for r in range(CH):
                    last = pe.transpose(dst[:, c, r * P:(r + 1) * P], src[:, r, c * P:(c + 1) * P], ident[:, :])
            return last

        def feature_major(pe, dst, w, srcT):
            for c in range(CH):
                for k in range(CH):
                    last = pe.matmul(dst[:, c, :], w[:, k, c * P:(c + 1) * P], srcT[:, k, :], start=k == 0, stop=k == CH - 1)
            return last

        def row_major(pe, dst, srcT, w, r, chunks):
            for k in range(chunks):
                last = pe.matmul(dst[:, r, :], srcT[:, k, r * P:(r + 1) * P], w[:, k, :], start=k == 0, stop=k == chunks - 1)
            return last

        def tensor_body(pe, front, attention, tail):
            def hidden_layer(w, srcT, done, read, groups):
                for j in groups:
                    if j == len(HIDDEN_BANKS):
                        pe.wait_ge(read, 1)
                    for u in range(CH):
                        c = CH * j + u
                        for k in range(CH):
                            last = pe.matmul(HIDDEN_BANKS[j % 3][:, u, :], w[:, k, c * P:(c + 1) * P], srcT[:, k, :], start=k == 0, stop=k == CH - 1)
                    last.then_inc(done, 1)

            def scores(h):
                part = P // 2 * (h % 2)
                for r in range(CH):
                    last = pe.matmul(S[h % 2][:, r, :], q_stack[part:part + P // 2, h // 2, r * P:(r + 1) * P],
                                     k_stack[part:part + P // 2, h // 2, :], start=True, stop=True)
                last.then_inc(scores_done, 1)

            def values(g):
                pe.wait_ge(probsT_ready, HEADS_PER_GROUP * (g + 1))
                if g > 0:
                    pe.wait_ge(attnT_ready, g)
                for k in range(CH):
                    for j in range(HEADS_PER_GROUP):
                        h = HEADS_PER_GROUP * g + j
                        last = pe.matmul(C[32 * j:32 * (j + 1), g % 2, :], v[:, k, h * HD:h * HD + 32], probsT[:, h % PROBS_T, k, :],
                                         start=k == 0, stop=k == CH - 1)
                last.then_inc(attnT_done, 1)

            def stack(dst, parts, patterns, i):
                for c in range(CH):
                    for a in range(PARTS):
                        last = pe.matmul(dst[:, c, :], select[:, patterns[a], i, :], parts[:, a, c, :], start=a == 0, stop=a == 1)
                return last

            for h in range(HEADS):
                if h == HEADS - 2 and front:
                    settle(pe, [(s, 1) for s in (momentsA1_ready, act1_ready, momentsA2_ready, act2_ready, xn_ready, x1T_ready, q_parts_ready)] + [(stats_read, 2)])
                if h == HEADS - 2 and tail:
                    settle(pe, [(field_read, 1)] + [(s, 1) for s in (xn2_ready, hT_ready, x3_ready, x3T_ready)] + ([(expert_read, 1)] if front else [])
                           + [(ff1_ready, 4), (ex1_loaded, 16), (ex2_loaded, 16), (ex_hidden_ready, 4)])
                if attention:
                    pe.wait_ge(probs_ready, h + 1)
                    if h >= 2:
                        pe.wait_ge(probsT_ready, h - 1)
                    transposes(pe, T[h % 2], probs[:, h % RING, :, :]).then_inc(probsT_done, 1)
                    if h + AHEAD < HEADS:
                        scores(h + AHEAD)
                    if h % HEADS_PER_GROUP == 1 and h > HEADS_PER_GROUP:
                        values(h // HEADS_PER_GROUP - 1)
                if h == 0 and tail:
                    pe.wait_ge(xn2_ready, 1)
                    transposes(pe, G[1], xn2).then_inc(hT_done, 1)
                if h == 1 and tail:
                    pe.wait_ge(field_read, 1)
                    pe.wait_ge(hT_ready, 1)
                    hidden_layer(w_ff1, hT, ff1_done, ff1_ready, (0, 1))
                if h == 1 and front:
                    pe.wait_ge(momentsA1_ready, 1)
                    pe.matmul(F[:, 0, 0:2], mean_w[:, :], stat4[:, 0:2], start=True, stop=True).then_inc(stats1_done, 1)
                if h == 2 and tail:
                    if front:
                        pe.wait_ge(stats_read, 1)
                    hidden_layer(w_ff1, hT, ff1_done, ff1_ready, (2, 3))
                if h == 3 and tail:
                    pe.wait_ge(ff1_ready, 4)
                    row_major(pe, G[1], hidden, w_ff2, 0, FC)
                if h == 4 and front:
                    if tail:
                        pe.wait_ge(ff1_ready, 4)
                    pe.wait_ge(act1_ready, 1)
                    feature_major(pe, F, w_in, gate).then_inc(mm1_done, 1)
                if h == 5 and tail:
                    row_major(pe, G[1], hidden, w_ff2, 1, FC).then_inc(ff2_done, 1)
                if h == 5 and front:
                    pe.wait_ge(momentsA2_ready, 1)
                    pe.matmul(F[:, 0, 0:2], mean_w[:, :], stat4[:, 2:4], start=True, stop=True).then_inc(stats2_done, 1)
                if h == 6 and tail:
                    pe.wait_ge(x3_ready, 1)
                    transposes(pe, G[0], x3).then_inc(x3T_done, 1)
                if h == 7 and tail:
                    pe.wait_ge(x3T_ready, 1)
                    pe.wait_ge(ex1_loaded, 16)
                    hidden_layer(w_ex1, x3T, ex1_done, ex_hidden_ready, (0, 1))
                if h == 8 and tail:
                    if front:
                        pe.wait_ge(stats_read, 2)
                    hidden_layer(w_ex1, x3T, ex1_done, ex_hidden_ready, (2, 3))
                if h == 9 and tail:
                    pe.wait_ge(ex2_loaded, 16)
                    pe.wait_ge(ex_hidden_ready, 4)
                    row_major(pe, G[1], hidden, w_ex2, 0, FC)
                if h == 9 and front:
                    pe.wait_ge(act2_ready, 1)
                    for r in range(CH):
                        last = row_major(pe, F, gate, w_out, r, CH)
                    last.then_inc(mm2_done, 1)
                if h == 10 and tail:
                    row_major(pe, G[1], hidden, w_ex2, 1, FC).then_inc(ex2_done, 1)
                if h == 10 and front:
                    pe.wait_ge(xn_ready, 1)
                    transposes(pe, F, x0).then_inc(x1T_done, 1)
                if h == 11 and front:
                    pe.wait_ge(x1T_ready, 1)
                    feature_major(pe, F, w_q, x1T).then_inc(qk_done, 1)
                if h == 12 and front:
                    if tail:
                        pe.wait_ge(expert_read, 1)
                    feature_major(pe, G[1], w_k, x1T).then_inc(qk_done, 1)
                if h == 13 and front:
                    pe.wait_ge(q_parts_ready, 1)
                    for r in range(CH):
                        last = row_major(pe, F, x1T, w_v, r, CH)
                    last.then_inc(v_done, 1)
                if h >= HEADS - 2 and front:
                    stack(S[h % 2], q_parts, (0, 1), h % 2).then_inc(q_select_done, 1)
            if front:
                pe.wait_ge(k_parts_ready, 1)
                for i in range(4):
                    if i == 1:
                        pe.wait_ge(v_read, 1)
                    if i >= 2:
                        pe.wait_ge(k_stacked, i - 1)
                    stack((G[1], F)[i % 2], k_parts, (2, 3), i).then_inc(k_select_done, 1)
                    if i < 2:
                        pe.wait_ge(q_stacked, i + 1)
                        stack(S[i], q_parts, (0, 1), i + 2).then_inc(q_select_done, 1)
            if attention:
                values(GROUPS - 1)
            if front:
                pe.wait_ge(q_stacked, 4)
                pe.wait_ge(k_stacked, 4)
                for h in range(AHEAD):
                    scores(h)
            if attention:
                pe.wait_ge(attnT_ready, GROUPS)
                for r in range(CH):
                    for g in range(GROUPS):
                        last = pe.matmul(G[1][:, r, :], attnT[:, g, r * P:(r + 1) * P], w_o[:, g, :], start=g == 0, stop=g == GROUPS - 1)
                        if g == 0:
                            for c in range(CH):
                                pe.matmul(G[1][:, r, c * P:(c + 1) * P], x1T_copy[:, c, r * P:(r + 1) * P], ident[:, :], start=False, stop=False)
                last.then_inc(proj_done, 1)
            if tail:
                pe.wait_ge(inner_ready, 1)
                for r in range(CH):
                    for k in range(CH):
                        pe.matmul(G[0][:, r, :], firstT[:, k, r * P:(r + 1) * P], diff[:, 0, k, :], start=k == 0, stop=False)
                        last = pe.matmul(G[0][:, r, :], secondT[:, k, r * P:(r + 1) * P], prod[:, 2, k, :], start=False, stop=k == CH - 1)
                last.then_inc(stencil_done, 1)
            if front:
                pe.wait_ge(v_ready, 1)
            counts = []
            if front:
                counts += [(k_parts_ready, 1), (v_read, 1), (v_ready, 1), (q_stacked, 4), (k_stacked, 4)]
            if attention:
                counts += [(probs_ready, HEADS), (probsT_ready, HEADS), (attnT_ready, GROUPS)]
            if tail:
                counts += [(inner_ready, 1)]
            settle(pe, counts)

        def scalar_body(act, front, attention, tail):
            def affine(dst, src, scale, shift):
                for c in range(CH):
                    last = act.activation(dst[:, c, :], src[:, c, :], ACT.Identity,
                                          bias=shift[:, c:c + 1], scale=scale[:, c:c + 1] if scale is not None else 1.0)
                return last

            def softmax(h, k):
                for r in range(CH):
                    act.wait_ge(logits_ready, CH * k + r + 1)
                    p = probs[:, h % RING, r, :]
                    last = act.activation(p, p, ACT.Exp, scale=-1.0, bias=neg_max[:, h % 2, r, h:h + 1], accum_out=denom[:, r, h:h + 1])
                last.then_inc(exp_done, 1)
                if h % HEADS_PER_GROUP == HEADS_PER_GROUP - 1:
                    act.drain().then_inc(bias_free[h // HEADS_PER_GROUP], 1)

            def query_stack(i):
                act.wait_ge(q_select_done, i + 1)
                act.activation(q_stack[:, i::4, :], S[i % 2][:, :, :], ACT.Copy).then_inc(q_stacked, 1)

            def qk_high(parts, src, bias_cols, k):
                act.wait_ge(qk_done, k)
                affine(parts[:, 0, :, :], src, None, bias_cols).then_inc(qk_high_ready, 1)

            for h in range(HEADS):
                if h == HEADS - 2 and front:
                    settle(act, [(half_ready, 2), (mm1_done, 1), (x1T_done, 1), (qk_done, 2)] + ([(x1T_kept, 1)] if attention else []))
                if h == HEADS - 2 and tail is not None:
                    settle(act, [(hT_done, 1), (ff1_done, 4), (x3T_done, 1), (ex_cols_loaded, 16), (ex1_done, 4)])
                if attention:
                    act.wait_ge(probsT_done, h + 1)
                    act.activation(probsT[:, h % PROBS_T, :, :], T[h % 2][:, :, :], ACT.Copy).then_inc(probsT_ready, 1)
                if h == 0 and tail is not None:
                    act.wait_ge(hT_done, 1)
                    affine(hT, G[1], cols[:, C_G2:C_G2 + CH], cols[:, C_BETA2:C_BETA2 + CH]).then_inc(hT_ready, 1)
                if h == 6 and tail is not None:
                    act.wait_ge(x3T_done, 1)
                    act.activation(x3T[:, :, :], G[0][:, :, :], ACT.Copy).then_inc(x3T_ready, 1)
                if attention and h + AHEAD < HEADS:
                    softmax(h + AHEAD, h)
                if h == 1 and tail is not None:
                    for j in range(4):
                        act.wait_ge(ff1_done, j + 1)
                        for u in range(CH):
                            c = CH * j + u
                            last = act.activation(hidden[:, c, :], HIDDEN_BANKS[j % 3][:, u, :], ACT.Gelu_apprx_sigmoid, bias=cols[:, C_FF1 + c:C_FF1 + c + 1])
                        last.then_inc(ff1_ready, 1)
                if h == 2 and front:
                    act.wait_ge(half_ready, 1)
                    act.activation(gate[:, :, :], half_w[:, :, :], ACT.Tanh).then_inc(tanh_ready, 1)
                if h == 4 and front:
                    act.wait_ge(mm1_done, 1)
                    affine(h1, F, None, cols[:, C_BIN:C_BIN + CH]).then_inc(h1_ready, 1)
                if h == 6 and front:
                    act.wait_ge(half_ready, 2)
                    act.activation(gate[:, :, :], half_w[:, :, :], ACT.Tanh).then_inc(tanh_ready, 1)
                if h == 7 and tail is not None:
                    act.wait_ge(ex_cols_loaded, 16)
                    for j in range(4):
                        act.wait_ge(ex1_done, j + 1)
                        for u in range(CH):
                            c = CH * j + u
                            last = act.activation(hidden[:, c, :], HIDDEN_BANKS[j % 3][:, u, :], ACT.Gelu, bias=ex_cols[:, c:c + 1])
                            if j == 3 and u == 0:
                                last.then_inc(ex1_free, 1)
                        last.then_inc(ex_hidden_ready, 1)
                if h == 10 and front:
                    act.wait_ge(x1T_done, 1)
                    if attention:
                        act.wait_ge(x1T_kept, 1)
                    affine(x1T, F, cond[:, 4:4 + CH], cond[:, 6:6 + CH]).then_inc(x1T_ready, 1)
                    act.drain().then_inc(x_free, 1)
                if h == 11 and front:
                    qk_high(q_parts, F, q_cols, 1)
                if h == 12 and front:
                    qk_high(k_parts, G[1], cols[:, C_BK:C_BK + CH], 2)
                if h >= HEADS - 2 and front:
                    query_stack(h % 2)
            if front:
                query_stack(2)
                query_stack(3)
                for h in range(AHEAD):
                    softmax(h, (LATER if attention else 0) + h)
                act.wait_ge(v_free, 1)
                act.activation(v[:, :, 0:DIM], v_next[:, :, :], ACT.Copy).then_inc(v_ready, 1)
                act.drain().then_inc(v_moved, 1)
            heads = (LATER if attention else 0) + (AHEAD if front else 0)
            counts = [(logits_ready, CH * heads)] if front or attention else []
            if front:
                counts += [(q_select_done, 4), (v_free, 1)]
            elif attention:
                act.wait_ge(x1T_kept, 1)
                counts += [(x1T_kept, 1)]
            if attention:
                counts += [(probsT_done, HEADS)]
            settle(act, counts)

        def vector_body(dve, front, attention, tail, first_store):
            def layer_moments(src, s6, s2, var, eps):
                for r in range(CH):
                    dve.bn_stats(out=s6[:, r, :], in_=src[:, r, :])
                dve.drain()
                for r in range(CH):
                    dve.bn_aggr(out=s2[:, r, :], in_=s6[:, r, :])
                dve.drain()
                return dve.tensor_scalar(var[:, :], s2[:, :, 1], eps, None, ALU.add)

            def normalise(dst, src, s2, rstd):
                for r in range(CH):
                    last = dve.tensor_scalar(dst[:, r, :], src[:, r, :], s2[:, r, 0:1], rstd[:, r:r + 1], ALU.subtract, ALU.mult)
                return last

            def partition_moments(src, k):
                dve.bn_stats(out=stat6[:, 0, :], in_=src[:, :, :].rearrange("p c n -> p (c n)"))
                dve.drain()
                dve.bn_aggr(out=stat2[:, 0, :], in_=stat6[:, 0, :])
                dve.drain()
                dve.tensor_copy(stat4[:, 2 * k:2 * k + 1], stat2[:, 0, 0:1])
                dve.scalar_tensor_tensor(out=stat4[:, 2 * k + 1:2 * k + 2], in0=stat2[:, 0, 0:1], scalar=stat2[:, 0, 0:1], in1=stat2[:, 0, 1:2],
                                         op0=ALU.mult, op1=ALU.add)
                return dve.drain()

            def global_variance():
                dve.tensor_copy(stat2[:, 1, :], F[:, 0, 0:2]).then_inc(stats_read, 1)
                dve.drain()
                dve.scalar_tensor_tensor(out=varA[:, 1:2], in0=stat2[:, 1, 0:1], scalar=stat2[:, 1, 0:1], in1=stat2[:, 1, 1:2],
                                         op0=ALU.mult, op1=ALU.subtract)
                dve.drain()
                return dve.tensor_scalar(varA[:, 0:1], varA[:, 1:2], -1.0, 1e-5, ALU.mult, ALU.add)

            def silu_argument(src, free):
                ins = dve.scalar_tensor_tensor(out=h1[:, :, :], in0=src[:, :, :], scalar=stat2[:, 1, 0:1], in1=gammaT[:, :, :],
                                               op0=ALU.subtract, op1=ALU.mult)
                if free is not None:
                    ins.then_inc(free, 1)
                dve.drain()
                dve.scalar_tensor_tensor(out=h1[:, :, :], in0=h1[:, :, :], scalar=rstdA[:, 0:1], in1=betaT[:, :, :], op0=ALU.mult, op1=ALU.add)
                dve.drain()
                for c in range(CH):
                    last = dve.tensor_scalar(half_w[:, c, :], h1[:, c, :], cond[:, c:c + 1], cond[:, 2 + c:3 + c], ALU.mult, ALU.add)
                return last

            def silu_product():
                return dve.scalar_tensor_tensor(out=gate[:, :, :], in0=gate[:, :, :], scalar=1.0, in1=half_w[:, :, :], op0=ALU.add, op1=ALU.mult)

            def logits(h, k):
                dve.wait_ge(scores_done, k + 1)
                dve.wait_ge(bias_masked, k + 1)
                for r in range(CH):
                    dve.tensor_tensor_reduce(out=probs[:, h % RING, r, :], in0=S[h % 2][:, r, :],
                                             in1=bias[:, h // HEADS_PER_GROUP % BIAS_BUFFERS, h % HEADS_PER_GROUP, r, :], scale=1.0, scalar=3.0e38,
                                             op0=ALU.add, op1=ALU.min, accum_out=neg_max[:, h % 2, r, h:h + 1]).then_inc(logits_ready, 1)

            def softmax_division(h, k):
                dve.wait_ge(exp_done, k + 1)
                dve.reciprocal(inv[:, :, h:h + 1], denom[:, :, h:h + 1])
                dve.drain()
                for r in range(CH):
                    p = probs[:, h % RING, r, :]
                    last = dve.tensor_scalar(p, p, inv[:, r, h:h + 1], None, ALU.mult)
                last.then_inc(probs_ready, 1)

            def group_output(g):
                dve.wait_ge(attnT_done, g + 1)
                dve.tensor_copy(attnT[:, g, :], C[:, g % 2, :]).then_inc(attnT_ready, 1)

            def qk_low(parts, src, bias_cols, k):
                dve.wait_ge(qk_high_ready, k)
                for c in range(CH):
                    last = dve.scalar_tensor_tensor(out=parts[:, 1, c, :], in0=src[:, c, :], scalar=bias_cols[:, c:c + 1], in1=parts[:, 0, c, :],
                                                    op0=ALU.add, op1=ALU.subtract)
                return last

            for h in range(HEADS):
                if h == HEADS - 2 and front is not None:
                    settle(dve, [(xT_loaded, 16), (stats1_done, 1), (rstdA_ready, 3), (tanh_ready, 2), (h1_ready, 1), (stats2_done, 1), (mm2_done, 1),
                                 (x_bias_ready, 1), (qk_high_ready, 2), (v_done, 1)])
                if h == HEADS - 2 and tail is not None:
                    settle(dve, [(rstdY_ready, 1), (ff2_done, 1), (x2_bias_ready, 1), (ex2_done, 1), (x3_bias_ready, 1)])
                if attention:
                    if h + AHEAD < HEADS:
                        logits(h + AHEAD, h)
                    if h % HEADS_PER_GROUP == 1 and h > HEADS_PER_GROUP:
                        group_output(h // HEADS_PER_GROUP - 1)
                if h == 0 and front is not None:
                    dve.tensor_copy(cond[:, :], cond_all[:, bass.ds(front, 1), :].rearrange("p a n -> p (a n)"))
                    dve.wait_ge(xT_loaded, 16)
                    dve.bn_stats(out=stat6[:, 0, :], in_=xT[:, :, :].rearrange("p c n -> p (c n)"))
                    dve.drain()
                    dve.bn_aggr(out=stat2[:, 0, :], in_=stat6[:, 0, :])
                    dve.drain()
                    dve.tensor_copy(stat4[:, 0:1], stat2[:, 0, 0:1])
                    dve.scalar_tensor_tensor(out=stat4[:, 1:2], in0=stat2[:, 0, 0:1], scalar=stat2[:, 0, 0:1], in1=stat2[:, 0, 1:2],
                                             op0=ALU.mult, op1=ALU.add)
                    dve.drain().then_inc(momentsA1_ready, 1)
                if h == 1 and front is not None:
                    dve.wait_ge(stats1_done, 1)
                    global_variance().then_inc(varA_ready, 1)
                if h == 6 and front is not None:
                    dve.wait_ge(rstdA_ready, 2)
                    silu_argument(h1, None).then_inc(half_ready, 1)
                if attention and h + AHEAD < HEADS:
                    softmax_division(h + AHEAD, h)
                if h == 1 and front is not None:
                    dve.wait_ge(rstdA_ready, 1)
                    silu_argument(xT, xT_free).then_inc(half_ready, 1)
                if h == 2 and front is not None:
                    dve.wait_ge(tanh_ready, 1)
                    silu_product().then_inc(act1_ready, 1)
                if h == 4 and front is not None:
                    dve.wait_ge(h1_ready, 1)
                    partition_moments(h1, 1).then_inc(momentsA2_ready, 1)
                if h == 5 and tail is not None:
                    dve.wait_ge(ff2_done, 1)
                    dve.wait_ge(x2_bias_ready, 1)
                    dve.tensor_tensor(out=x3[:, :, :], in0=G[1][:, :, :], in1=x2_bias[:, :, :], op=ALU.add).then_inc(x3_ready, 1)
                    dve.drain().then_inc(x3_for_bias, 1)
                if h == 5 and front is not None:
                    dve.wait_ge(stats2_done, 1)
                    global_variance().then_inc(varA_ready, 1)
                if h == 7 and front is not None:
                    dve.wait_ge(tanh_ready, 2)
                    silu_product().then_inc(act2_ready, 1)
                if h == 9 and front is not None:
                    dve.wait_ge(mm2_done, 1)
                    dve.wait_ge(x_bias_ready, 1)
                    dve.tensor_tensor(out=x0[:, :, :], in0=F[:, :, :], in1=x_bias[:, :, :], op=ALU.add)
                    dve.drain()
                    layer_moments(x0, stat6, stat2, varA, 1e-5).then_inc(varA_ready, 1)
                if h == 10 and front is not None:
                    dve.wait_ge(rstdA_ready, 3)
                    normalise(x0, x0, stat2, rstdA).then_inc(xn_ready, 1)
                if h == 10 and tail is not None:
                    dve.wait_ge(ex2_done, 1)
                    dve.wait_ge(x3_bias_ready, 1)
                    dve.tensor_tensor(out=y[:, :, :], in0=G[1][:, :, :], in1=x3_bias[:, :, :], op=ALU.add).then_inc(ex2_free, 1)
                    y_written = dve.drain()
                    if front is not None:
                        y_written.then_inc(expert_read, 1)
                    layer_moments(y, statB6, statB2, varB, 1e-12).then_inc(varY_ready, 1)
                if h == 11 and front is not None:
                    qk_low(q_parts, F, q_cols, 1).then_inc(q_parts_ready, 1)
                if h == 11 and tail is not None:
                    dve.wait_ge(rstdY_ready, 1)
                    normalise(y, y, statB2, rstdB).then_inc(y_ready, 1)
                if h == 12 and front is not None:
                    qk_low(k_parts, G[1], cols[:, C_BK:C_BK + CH], 2).then_inc(k_parts_ready, 1)
                if h == 13 and front is not None:
                    dve.wait_ge(v_done, 1)
                    dve.tensor_tensor(out=v_next[:, :, :], in0=F[:, :, :], in1=rows[:, B_V:B_V + 1, :].to_broadcast([P, CH, DIM]), op=ALU.add)\
                        .then_inc(v_read, 1)
                if h == 14 and tail is not None:
                    dve.wait_ge(f_ready, 1)
                    for a in range(2):
                        for side in range(2):
                            lo = (DIM - 4) * side
                            dve.tensor_tensor(out=edge[:, a, :, side, :], in0=f[:, :, lo:lo + 4], in1=edge_coef[:, a, :, side, :], op=ALU.mult)
                    dve.drain()
                    dst = diff[:, :, :, :].rearrange("p a c n -> p (a c) n")[:, :, 0:DIM:DIM - 1]
                    dve.tensor_reduce(out=dst, in_=edge[:, :, :, :, :].rearrange("p a c s j -> p (a c) s j"), axis=AX.X, op=ALU.add).then_inc(edges_ready, 1)
            if front is not None:
                for i in range(4):
                    dve.wait_ge(k_select_done, i + 1)
                    dve.tensor_copy(k_stack[:, i::4, :], (G[1], F)[i % 2][:, :, :]).then_inc(k_stacked, 1)
            if attention:
                group_output(GROUPS - 1)
                settle(dve, [(attnT_done, GROUPS)])
            if front is not None:
                dve.drain().then_inc(v_free, 1)
                for h in range(AHEAD):
                    logits(h, (LATER if attention else 0) + h)
                for h in range(AHEAD):
                    softmax_division(h, (LATER if attention else 0) + h)
                dve.wait_ge(v_moved, 1)
            if attention or front is not None:
                heads = (LATER if attention else 0) + (AHEAD if front is not None else 0)
                settle(dve, [(s, heads) for s in (scores_done, bias_masked, exp_done)] + ([(k_select_done, 4), (v_moved, 1)] if front is not None else []))
            if attention:
                dve.wait_ge(proj_done, 1)
                dve.tensor_tensor(out=x2[:, :, :], in0=G[1][:, :, :], in1=rows[:, B_O:B_O + 1, :].to_broadcast([P, CH, DIM]), op=ALU.add)
                dve.drain()
                layer_moments(x2, statB6, statB2, varB, 1e-5).then_inc(varB_ready, 1)
                dve.wait_ge(rstdB_ready, 1)
                normalise(xn2, x2, statB2, rstdB).then_inc(xn2_ready, 1)
                settle(dve, [(proj_done, 1), (rstdB_ready, 1)])
                if tail is None:
                    dve.drain().then_inc(field_read, 1)
            if tail is not None:
                dve.tensor_copy(dt[:, :], dt_all[:, bass.ds(tail, 1)])
                dve.drain()
                dve.wait_ge(terms_ready, 1)
                dve.scalar_tensor_tensor(out=field[:, :, :], in0=diff[:, 1, :, :], scalar=dt[:, 0:1], in1=f[:, :, :], op0=ALU.mult, op1=ALU.add)
                dve.drain()
                dve.wait_ge(stencil_done, 1)
                if not first_store:
                    dve.wait_ge(stored, 16)
                dve.scalar_tensor_tensor(out=res[:, :, :], in0=G[0][:, :, :], scalar=dt[:, 0:1], in1=field[:, :, :], op0=ALU.mult, op1=ALU.add)
                dve.drain().then_inc(field_read, 1)
                dve.tensor_scalar(res[:, :, :], res[:, :, :], 0.0, None, ALU.max).then_inc(res_ready, 1)
            if tail is not None:
                settle(dve, [(f_ready, 1), (terms_ready, 1), (stencil_done, 1)] + ([] if first_store else [(stored, 16)]))

        def pool_body(pool, front, attention, tail):
            def rsqrt(var, rstd, n):
                return pool.tensor_tensor(out=rstd[:, 0:n], in0=var[:, 0:n], in1=consts[:, NEG_HALF:NEG_HALF + n], op=ALU.pow)

            def mask_bias(heads):
                for h in heads:
                    if h % HEADS_PER_GROUP == 0:
                        pool.wait_ge(bias_loaded[h // HEADS_PER_GROUP], 16)
                    t = bias[:, h // HEADS_PER_GROUP % BIAS_BUFFERS, h % HEADS_PER_GROUP, :, :]
                    pool.tensor_tensor(out=t, in0=mask_far[:, :, :], in1=t, op=ALU.subtract).then_inc(bias_masked, 1)

            def product(slot, k):
                return pool.tensor_tensor(out=prod[:, slot, :, :], in0=coef[:, k, :, :], in1=f[:, :, :], op=ALU.mult)

            def add_row(dst, src, row):
                return pool.tensor_tensor(out=dst[:, :, :], in0=src[:, :, :], in1=row.to_broadcast([P, CH, DIM]), op=ALU.add)

            for h in range(HEADS):
                if attention:
                    if h + HEADS_PER_GROUP < HEADS:
                        mask_bias(range(h + HEADS_PER_GROUP, h + HEADS_PER_GROUP + 1))
                if h == 1 and front:
                    pool.wait_ge(varA_ready, 1)
                    rsqrt(varA, rstdA, 1).then_inc(rstdA_ready, 1)
                if h == 4 and front:
                    pool.wait_ge(x_loaded, 16)
                    add_row(x_bias, x, rows[:, B_OUT:B_OUT + 1, :]).then_inc(x_bias_ready, 1)
                if h == 5 and tail:
                    pool.wait_ge(x3_for_bias, 1)
                    pool.wait_ge(ex_rows_loaded, 16)
                    add_row(x3_bias, x3, ex_rows[:, 0:1, :]).then_inc(x3_bias_ready, 1)
                if h == 5 and front:
                    pool.wait_ge(varA_ready, 2)
                    rsqrt(varA, rstdA, 1).then_inc(rstdA_ready, 1)
                if h == 9 and front:
                    pool.wait_ge(varA_ready, 3)
                    rsqrt(varA, rstdA, CH).then_inc(rstdA_ready, 1)
                if h == 9 and attention:
                    pool.tensor_copy(x1T_copy[:, :, :], x1T[:, :, :]).then_inc(x1T_kept, 1)
                if h == 10 and tail:
                    pool.wait_ge(varY_ready, 1)
                    rsqrt(varB, rstdB, CH).then_inc(rstdY_ready, 1)
                if h == 11 and front:
                    pool.wait_ge(mask_loaded, 16)
                    pool.drain()
                    pool.tensor_scalar(mask_far[:, :, :], mask_u8[:, :, :], 1.0e38, 1.0, ALU.mult, ALU.mult).then_inc(mask_free, 1)
                    pool.drain()
                if h == 11 and tail:
                    pool.wait_ge(y_ready, 1)
                    pool.tensor_tensor(out=f[:, :, :], in0=y[:, :, :], in1=ex_rows[:, 1:2, :].to_broadcast([P, CH, DIM]), op=ALU.mult)
                    pool.drain()
                    add_row(f, f, ex_rows[:, 2:3, :]).then_inc(f_ready, 1)
                    pool.drain().then_inc(ex_small_free, 1)
                if h == 12 and tail:
                    product(0, K_MIXED)
                    product(1, K_ROW)
                    product(2, K_SECOND)
                    pool.drain()
                    pool.tensor_tensor(out=diff[:, 0, :, 1:DIM - 1], in0=prod[:, 0, :, 2:DIM], in1=prod[:, 0, :, 0:DIM - 2], op=ALU.subtract)
                    pool.drain()
                if h == 13 and front:
                    mask_bias(range(2))
                if h == 14 and tail:
                    pool.wait_ge(edges_ready, 1)
                    pool.tensor_tensor(out=diff[:, 0, :, :], in0=diff[:, 0, :, :], in1=prod[:, 1, :, :], op=ALU.subtract).then_inc(inner_ready, 1)
                    pool.drain()
                    product(0, K_RIGHT)
                    product(1, K_LEFT)
                    pool.drain()
                    pool.tensor_tensor(out=diff[:, 1, :, 1:DIM - 1], in0=prod[:, 0, :, 2:DIM], in1=prod[:, 1, :, 0:DIM - 2], op=ALU.add)
                    pool.drain()
                    product(0, K_MIDDLE)
                    pool.drain()
                    pool.tensor_tensor(out=diff[:, 1, :, :], in0=diff[:, 1, :, :], in1=prod[:, 0, :, :], op=ALU.subtract).then_inc(terms_ready, 1)
            if attention:
                pool.wait_ge(varB_ready, 1)
                rsqrt(varB, rstdB, CH).then_inc(rstdB_ready, 1)
            if front:
                mask_bias(range(2, HEADS_PER_GROUP))
            if attention:
                add_row(x2_bias, x2, rows[:, B_FF2:B_FF2 + 1, :]).then_inc(x2_bias_ready, 1)
            counts = []
            if front:
                counts += [(mask_loaded, 16), (x_loaded, 16), (varA_ready, 3), (bias_loaded[0], 16)]
            if attention:
                counts += [(s, 16) for s in bias_loaded[1:]] + [(varB_ready, 1)]
            if tail:
                counts += [(varY_ready, 1), (x3_for_bias, 1), (ex_rows_loaded, 16), (y_ready, 1), (edges_ready, 1)]
            settle(pool, counts)

        def program(eng, body, **first):
            body(eng, 0, None, None)
            body(eng, 1, 0, None)
            body(eng, 2, 1, 0, **first)
            with eng.Fori(2, BATCHES - 1) as i:
                body(eng, i + 1, i, i - 1)
            body(eng, None, BATCHES - 1, BATCHES - 2)
            body(eng, None, None, BATCHES - 1)

        def flags(body):
            return lambda eng, front, attention, tail: body(eng, front is not None, attention is not None, tail is not None)

        with nc.Block() as block:
            @block.sync
            def _(sp):
                program(sp, sync_body)
                sp.wait_ge(res_ready, 1)
                store(sp, BATCHES - 1)

            @block.tensor
            def _(pe):
                program(pe, flags(tensor_body))

            @block.scalar
            def _(act):
                program(act, lambda eng, f_, a_, t_: scalar_body(eng, f_ is not None, a_ is not None, t_))

            @block.vector
            def _(dve):
                program(dve, lambda eng, f_, a_, t_, first_store=False: vector_body(eng, f_, a_ is not None, t_, first_store),
                        first_store=True)
                dve.wait_ge(stored, 16)

            @block.gpsimd
            def _(pool):
                program(pool, flags(pool_body))


def columns(v):
    return np.asarray(v).reshape(-1, P).T


def kernel(**inputs):
    import concourse.bacc as _bacc
    from concourse import mybir as _mybir
    from concourse.bass_utils import run_bass_kernel_spmd as _run

    g = {k: np.asarray(a) for k, a in inputs.items()}
    f0 = np.exp(np.arange(NOISE // 2, dtype=np.float32) * np.float32(-math.log(10000.0) / (NOISE // 2 - 1)))
    f1 = np.exp(np.arange(DIM // 2, dtype=np.float32) * np.float32(-math.log(10000.0) / (DIM // 2 - 1)))
    p = np.arange(P)
    phase0 = np.where(p < NOISE // 2, 0.0, 0.25).astype(np.float32)
    zero, quarter = np.zeros(P, np.float32), np.full(P, 0.25, np.float32)
    turn = np.float32(TWO_PI)
    select = np.zeros((P, 4, 4, P), np.float32)
    for pattern, pairings in enumerate(((0, 1), (2, 3), (0, 2), (1, 3))):
        for i in range(4):
            for t in pairings:
                for b in range(2):
                    for e in range(HD):
                        select[32 * i + HD * b + e, pattern, i, P // 2 * b + HD * t + e] = 1.0
    w_o = g["L1_cond_Wo"].reshape(HEADS, 1, HD, DIM)
    tables = np.stack([np.concatenate([f0, f0]), f1, phase0, zero, quarter, phase0 * turn, zero, quarter * turn], axis=1)
    cols = np.concatenate([columns(g[n]) for n in (
        "L0_cond_b_in", "L1_cond_bk", "L1_cond_g2", "L1_cond_beta2", "L1_cond_bq", "L1_cond_b1", "L0_cond_b1", "L0_cond_b2",
        "L0_cond_bsc", "L0_cond_bsh", "L1_cond_b_ada")] + [tables], axis=1)
    first, second = stencil_matrices()
    arrays = {
        "x": g["x"], "xT": g["x"].transpose(0, 2, 1),
        "mask": g["mask_Bx1xSxS_bk0"].reshape(BATCHES, SEQ, SEQ),
        "fside": g["fside_Bx16xSxS_0"].reshape(BATCHES, GROUPS, HEADS_PER_GROUP, CH, P, SEQ).transpose(0, 1, 4, 2, 3, 5)
        .reshape(BATCHES, GROUPS, P, HEADS_PER_GROUP * CH * SEQ),
        "cols": cols, "gammaT": g["L0_cond_gamma"].T, "betaT": g["L0_cond_beta"].T, "firstT": first.T, "secondT": second.T,
        "select": select.reshape(P, 16 * P), "Wo_spaced": np.concatenate([w_o, np.zeros_like(w_o)], axis=1).reshape(HEADS * 2 * HD, DIM),
        "ex_bi": g["L2_cond_bi"].reshape(EXPERTS, FC, P).transpose(0, 2, 1),
        "ex_rows": np.concatenate([g["L2_cond_bo"], g["L2_cond_gamma"], g["L2_cond_beta"]], axis=1),
    }
    for n in ("condB_t", "condB_dt", "itok_B_34_63", "itok_B_0_7", "L0_cond_W1", "L0_cond_W2", "L0_cond_Wsc", "L0_cond_Wsh", "L0_cond_W_in",
              "L0_cond_W_out", "L0_cond_b_out", "L1_cond_W_ada", "L1_cond_Wq", "L1_cond_Wk", "L1_cond_Wv", "L1_cond_bv",
              "L1_cond_bo", "L1_cond_W1", "L1_cond_W2", "L1_cond_b2", "L2_cond_Wi", "L2_cond_Wo", "L3_cond_A_grid", "L3_cond_B_grid"):
        arrays[n] = g[n]
    nc = _bacc.Bacc("TRN2", target_bir_lowering=False, num_devices=1)
    sent, d = {}, {}
    for n, a in arrays.items():
        a = np.ascontiguousarray(a)
        sent[f"in_{n}"] = a
        d[n] = nc.dram_tensor(f"in_{n}", a.shape, _mybir.dt.from_np(a.dtype), kind="ExternalInput").ap()
    out = nc.dram_tensor("out", (BATCHES, SEQ, DIM), _mybir.dt.float32, kind="ExternalOutput").ap()
    build_program(nc, d, out)
    r = _run(nc, [sent], core_ids=[0])
    return r.results[0]["out"]
```
